# Optimizing a Trainium2 kernel written in Bass

```python
import numpy as np
import jax
import jax.numpy as jnp

def _softmax(x, axis=-1):
    return jax.nn.softmax(x, axis=axis)

def _gelu(x):
    return jax.nn.gelu(x, approximate=True)

def _silu(x):
    return jax.nn.silu(x)

def _sigmoid(x):
    return jax.nn.sigmoid(x)

def _layernorm(x, axis=-1, eps=1e-05):
    m = jnp.mean(x, axis=axis, keepdims=True)
    v = jnp.var(x, axis=axis, keepdims=True)
    return (x - m) / jnp.sqrt(v + eps)

def _scatter_add(tgt, idx, src, axis=0):
    return tgt.at[idx].add(src)

def _segment_sum(src, seg, n):
    return jax.ops.segment_sum(src, seg, n)
kernel_name = 'mk_flamingo_gated_d4_seqx_r8_a62a6b'

def setup_inputs(seed: int=0):
    np.random.seed(seed)
    _w = jnp.asarray

    def _rec_inputs():
        import jax
        import jax.numpy as jnp
        _rk = jax.random.key(seed)
        x = -0.0002928 + 1 * jax.random.normal(jax.random.fold_in(_rk, 1), (32, 64, 128), jnp.float32)
        _lenS = 64 - jax.random.randint(jax.random.fold_in(_rk, 7), (32,), 0, max(1, 64 // 4) + 1, jnp.int32)
        _lenS2 = 64 - jax.random.randint(jax.random.fold_in(_rk, 8), (32,), 0, max(1, 64 // 4) + 1, jnp.int32)
        _ctx_1024P = jax.random.normal(jax.random.fold_in(_rk, 11), (32, 16, 128), jnp.float32)
        _ctx_1024c = jax.random.dirichlet(jax.random.fold_in(_rk, 511), 0.3 * jnp.ones((16,), jnp.float32), (32, 64))
        _ctx_1024t = jnp.einsum('bsk,bkd->bsd', _ctx_1024c, _ctx_1024P)
        _ctx_1024t = _ctx_1024t * jax.lax.rsqrt(jnp.mean(jnp.square(_ctx_1024t)) + 1e-12) * 0.953939
        ctx_1024 = -1.39393e-06 + 0.999914 * (_ctx_1024t + 0.3 * jax.random.normal(jax.random.fold_in(_rk, 611), (32, 64, 128), jnp.float32))
        fside_BxS_0 = jax.random.uniform(jax.random.fold_in(_rk, 13), (32, 64), jnp.float32, 0.0, 0.999943)
        _validS = jnp.arange(64)[None, :] < _lenS[:, None]
        _validS2 = jnp.arange(64)[None, :] < _lenS2[:, None]
        _causal = jnp.tril(jnp.ones((64, 64), dtype=bool))
        mask_BxS2_bk0 = jnp.logical_not(jnp.broadcast_to(_validS2[:, :], (32, 64)))
        _g = jax.random.normal(jax.random.fold_in(_rk, 9001), (2, 4), jnp.float32)
        _g = jnp.sign(_g) * jnp.maximum(jnp.abs(_g), 1.0) + (_g == 0) * 1.0
        g_xattn = _g[0]
        g_ffn = _g[1]
        return (x, ctx_1024, fside_BxS_0, mask_BxS2_bk0, g_xattn, g_ffn)
    x, ctx_1024, fside_BxS_0, mask_BxS2_bk0, g_xattn, g_ffn = _rec_inputs()

    def _L0_xattn_setup():
        import jax, jax.numpy as jnp
        import numpy as np
        NUM_HEADS = 16
        HIDDEN = 128
        HEAD_DIM = HIDDEN // NUM_HEADS
        B, S, D = (2, 256, 128)
        key = jax.random.key(seed)
        ks = jax.random.split(key, 7)
        scale = 1.0 / np.sqrt(D)
        return {'query': jax.random.normal(ks[0], (B, S, D), dtype=jnp.float32), 'key': jax.random.normal(ks[1], (B, S, D), dtype=jnp.float32), 'value': jax.random.normal(ks[2], (B, S, D), dtype=jnp.float32), 'Wk_w': jax.random.normal(ks[3], (HIDDEN, D), dtype=jnp.float32) * scale, 'Wk_b': jax.random.normal(ks[4], (HIDDEN,), dtype=jnp.float32) * scale, 'Wv_w': jax.random.normal(ks[5], (HIDDEN, D), dtype=jnp.float32) * scale, 'Wv_b': jax.random.normal(ks[6], (HIDDEN,), dtype=jnp.float32) * scale}
    _L0_xattn_all = _L0_xattn_setup()
    _L0_xattn_in = {k: v for k, v in _L0_xattn_all.items() if k in ('Wk_w', 'Wk_b', 'Wv_w', 'Wv_b')}
    del _L0_xattn_all

    def _L0_ffn_setup():
        import jax, jax.numpy as jnp
        import numpy as np
        N_EXPERTS = 8
        TOP_K = 2
        key = jax.random.key(seed)
        k1, k2, k3, k4 = jax.random.split(key, 4)
        B, T, C, H, E = (2, 256, 128, 512, N_EXPERTS)
        x = jax.random.normal(k1, (B, T, C), dtype=jnp.float32)
        router_w = jax.random.normal(k2, (E, C), dtype=jnp.float32) * 0.02
        w1 = jax.random.normal(k3, (E, C, H), dtype=jnp.float32) * (1.0 / np.sqrt(C))
        w2 = jax.random.normal(k4, (E, H, C), dtype=jnp.float32) * (1.0 / np.sqrt(H))
        return {'x': x, 'router_w': router_w, 'w1': w1, 'w2': w2}
    _L0_ffn_all = _L0_ffn_setup()
    _L0_ffn_in = {k: v for k, v in _L0_ffn_all.items() if k in ('router_w', 'w1', 'w2')}
    del _L0_ffn_all

    def _L1_xattn_setup():
        import jax, jax.numpy as jnp
        import numpy as np
        DIM = 128
        NUM_HEADS = 16
        HEAD_DIM = DIM // NUM_HEADS
        SCALE = HEAD_DIM ** (-0.5)
        EPS = 1e-05

        def _layernorm(x, w, b):
            mu = jnp.mean(x, axis=-1, keepdims=True)
            var = jnp.mean(jnp.square(x - mu), axis=-1, keepdims=True)
            return (x - mu) * jax.lax.rsqrt(var + EPS) * w + b

        def _split_heads(x):
            B, L, _ = x.shape
            return x.reshape(B, L, NUM_HEADS, HEAD_DIM).transpose(0, 2, 1, 3)
        key = jax.random.key(seed)
        ks = jax.random.split(key, 12)
        B, Lq, Lk = (4, 64, 256)
        inp = {'query': jax.random.normal(ks[0], (B, Lq, DIM), jnp.float32), 'context': jax.random.normal(ks[1], (B, Lk, DIM), jnp.float32), 'context_mask': jax.random.randint(ks[2], (B, Lk), 0, 2).astype(bool), 'qn_w': jnp.ones((DIM,), jnp.float32), 'qn_b': jnp.zeros((DIM,), jnp.float32), 'cn_w': jnp.ones((DIM,), jnp.float32), 'cn_b': jnp.zeros((DIM,), jnp.float32)}
        std = DIM ** (-0.5)
        for i, name in enumerate(['q', 'k', 'v', 'o']):
            inp[f'W{name}'] = jax.random.normal(ks[3 + i], (DIM, DIM), jnp.float32) * std
            inp[f'b{name}'] = jnp.zeros((DIM,), jnp.float32)
        return inp
    _L1_xattn_all = _L1_xattn_setup()
    _L1_xattn_in = {k: v for k, v in _L1_xattn_all.items() if k in ('qn_w', 'qn_b', 'cn_w', 'cn_b', 'Wq', 'bq', 'Wk', 'bk', 'Wv', 'bv', 'Wo', 'bo')}
    del _L1_xattn_all

    def _L1_ffn_setup():
        import jax, jax.numpy as jnp
        import numpy as np
        CAPACITY_FACTOR = 1.0

        def _top1_gate(x2d, wg):
            S, _ = x2d.shape
            E = wg.shape[1]
            C = int(CAPACITY_FACTOR * S / E)
            logits = x2d @ wg
            gates = jax.nn.softmax(logits, axis=-1)
            idx = jnp.argmax(gates, axis=-1)
            mask = jax.nn.one_hot(idx, E, dtype=jnp.int32)
            loc = jnp.cumsum(mask, axis=0) - 1
            me = jnp.mean(gates, axis=0)
            ce = jnp.mean(mask.astype(gates.dtype), axis=0)
            l_aux = E * jnp.sum(me * ce)
            mask = mask * (loc < C).astype(jnp.int32)
            gate_s = jnp.sum(gates * mask, axis=-1)
            loc_s = jnp.sum(loc * mask, axis=-1)
            loc_oh = jax.nn.one_hot(loc_s, C, dtype=gates.dtype)
            combine = (gate_s[:, None] * mask.astype(gates.dtype))[:, :, None] * loc_oh[:, None, :]
            dispatch = (combine > 0).astype(gates.dtype)
            return (l_aux, combine, dispatch)
        key = jax.random.key(seed)
        k1, k2, k3, k4 = jax.random.split(key, 4)
        s, b, m, E, ffn = (256, 4, 128, 8, 512)
        x = jax.random.normal(k1, (s, b, m), dtype=jnp.float32)
        wg = jax.random.normal(k2, (m, E), dtype=jnp.float32) * 0.02
        w1 = jax.random.normal(k3, (E, m, ffn), dtype=jnp.float32) * 0.02
        w2 = jax.random.normal(k4, (E, ffn, m), dtype=jnp.float32) * 0.02
        return {'x': x, 'wg': wg, 'w1': w1, 'w2': w2}
    _L1_ffn_all = _L1_ffn_setup()
    _L1_ffn_in = {k: v for k, v in _L1_ffn_all.items() if k in ('wg', 'w1', 'w2')}
    del _L1_ffn_all

    def _L2_xattn_setup():
        import jax, jax.numpy as jnp
        import numpy as np
        EPS = 1e-05

        def layernorm(x, g, b):
            mu = jnp.mean(x, axis=-1, keepdims=True)
            var = jnp.var(x, axis=-1, keepdims=True)
            return (x - mu) * jax.lax.rsqrt(var + EPS) * g + b
        DIM = 128
        CTX = 128
        HEADS = 12
        DHEAD = 64
        INNER = HEADS * DHEAD
        B = 4
        F = 256
        J = 128
        key = jax.random.key(seed)
        ks = jax.random.split(key, 8)
        s = lambda d: 1.0 / np.sqrt(d)
        return {'x': jax.random.normal(ks[0], (B, F, DIM), jnp.float32), 'tab_x': jax.random.normal(ks[1], (B, J, CTX), jnp.float32), 'tab_g': jnp.ones((CTX,), jnp.float32), 'tab_b': jnp.zeros((CTX,), jnp.float32), 'vid_g': jnp.ones((DIM,), jnp.float32), 'vid_b': jnp.zeros((DIM,), jnp.float32), 'Wq': jax.random.normal(ks[2], (DIM, INNER), jnp.float32) * s(DIM), 'Wk': jax.random.normal(ks[3], (CTX, INNER), jnp.float32) * s(CTX), 'Wv': jax.random.normal(ks[4], (CTX, INNER), jnp.float32) * s(CTX), 'q_g': jnp.ones((INNER,), jnp.float32), 'q_b': jnp.zeros((INNER,), jnp.float32), 'k_g': jnp.ones((INNER,), jnp.float32), 'k_b': jnp.zeros((INNER,), jnp.float32), 'Wo': jax.random.normal(ks[5], (INNER, DIM), jnp.float32) * s(INNER), 'bo': jnp.zeros((DIM,), jnp.float32)}
    _L2_xattn_all = _L2_xattn_setup()
    _L2_xattn_in = {k: v for k, v in _L2_xattn_all.items() if k in ('tab_g', 'tab_b', 'vid_g', 'vid_b', 'Wq', 'Wk', 'Wv', 'q_g', 'q_b', 'k_g', 'k_b', 'Wo', 'bo')}
    del _L2_xattn_all

    def _L2_ffn_setup():
        import jax, jax.numpy as jnp
        import numpy as np
        EPS = 1e-08
        key = jax.random.key(seed)
        kx, kw = jax.random.split(key)
        x = jax.random.normal(kx, (8, 512, 128), dtype=jnp.float32)
        weight = jax.random.normal(kw, (128, 128), dtype=jnp.float32) * (1.0 / np.sqrt(128))
        return {'x': x, 'weight': weight}
    _L2_ffn_all = _L2_ffn_setup()
    _L2_ffn_in = {k: v for k, v in _L2_ffn_all.items() if k in ('weight',)}
    del _L2_ffn_all

    def _L3_xattn_setup():
        import jax, jax.numpy as jnp
        import numpy as np
        key = jax.random.key(seed)
        ks = jax.random.split(key, 6)
        B, L1, L2, D = (8, 256, 256, 128)
        scale_g = 1.0 / np.sqrt(D)
        scale_l = 1.0 / np.sqrt(2 * D)
        return {'h': jax.random.normal(ks[0], (B, L1, D), jnp.float32), 'ht': jax.random.normal(ks[1], (B, L2, D), jnp.float32), 'position_weights': jax.random.uniform(ks[2], (B, L1), jnp.float32), 'W_gate': jax.random.normal(ks[3], (D, D), jnp.float32) * scale_g, 'b_gate': jnp.zeros((D,), jnp.float32), 'W_lin': jax.random.normal(ks[4], (2 * D, D), jnp.float32) * scale_l, 'b_lin': jnp.zeros((D,), jnp.float32)}
    _L3_xattn_all = _L3_xattn_setup()
    _L3_xattn_in = {k: v for k, v in _L3_xattn_all.items() if k in ('W_gate', 'b_gate', 'W_lin', 'b_lin')}
    del _L3_xattn_all

    def _L3_ffn_setup():
        import jax, jax.numpy as jnp
        import numpy as np
        EMB = 128
        HID = 256
        HEADS = 16
        HEAD_DIM = EMB // HEADS
        EXPERTS = 8
        TOPK = 2
        EPS = 1e-05

        def layernorm(x, scale, shift):
            mean = jnp.mean(x, axis=-1, keepdims=True)
            var = jnp.mean((x - mean) ** 2, axis=-1, keepdims=True)
            return scale * (x - mean) / jnp.sqrt(var + EPS) + shift

        def attention(x, wq, wk, wv, wo, bo):
            b, t, _ = x.shape
            q = (x @ wq).reshape(b, t, HEADS, HEAD_DIM)
            k = (x @ wk).reshape(b, t, HEADS, HEAD_DIM)
            v = (x @ wv).reshape(b, t, HEADS, HEAD_DIM)
            scores = jnp.einsum('bqhd,bkhd->bhqk', q, k)
            mask = jnp.arange(t)[:, None] < jnp.arange(t)[None, :]
            scores = jnp.where(mask, -jnp.inf, scores)
            attn = jax.nn.softmax(scores / np.sqrt(HEAD_DIM), axis=-1)
            ctx = jnp.einsum('bhqk,bkhd->bqhd', attn, v).reshape(b, t, EMB)
            return ctx @ wo + bo

        def moe_ff(x, gate_w, w1, w2, w3):
            b, t, d = x.shape
            xf = x.reshape(b * t, d)
            scores = xf @ gate_w
            topk_scores, topk_idx = jax.lax.top_k(scores, TOPK)
            topk_probs = jax.nn.softmax(topk_scores, axis=-1)
            weight = jnp.sum(jax.nn.one_hot(topk_idx, EXPERTS, dtype=xf.dtype) * topk_probs[..., None], axis=1)
            h = jax.nn.silu(jnp.einsum('td,edh->eth', xf, w1)) * jnp.einsum('td,edh->eth', xf, w2)
            out_e = jnp.einsum('eth,ehd->etd', h, w3)
            out = jnp.einsum('etd,te->td', out_e, weight)
            return out.reshape(b, t, d)
        key = jax.random.key(seed)
        ks = jax.random.split(key, 12)
        s = lambda k, shape, fan: jax.random.normal(k, shape, jnp.float32) / np.sqrt(fan)
        return {'x': jax.random.normal(ks[0], (2, 256, EMB), jnp.float32), 'ln1_scale': jnp.ones((EMB,), jnp.float32), 'ln1_shift': jnp.zeros((EMB,), jnp.float32), 'wq': s(ks[1], (EMB, EMB), EMB), 'wk': s(ks[2], (EMB, EMB), EMB), 'wv': s(ks[3], (EMB, EMB), EMB), 'wo': s(ks[4], (EMB, EMB), EMB), 'bo': jnp.zeros((EMB,), jnp.float32), 'ln2_scale': jnp.ones((EMB,), jnp.float32), 'ln2_shift': jnp.zeros((EMB,), jnp.float32), 'gate_w': s(ks[5], (EMB, EXPERTS), EMB), 'w1': s(ks[6], (EXPERTS, EMB, HID), EMB), 'w2': s(ks[7], (EXPERTS, EMB, HID), EMB), 'w3': s(ks[8], (EXPERTS, HID, EMB), HID)}
    _L3_ffn_all = _L3_ffn_setup()
    _L3_ffn_in = {k: v for k, v in _L3_ffn_all.items() if k in ('ln1_scale', 'ln1_shift', 'wq', 'wk', 'wv', 'wo', 'bo', 'ln2_scale', 'ln2_shift', 'gate_w', 'w1', 'w2', 'w3')}
    del _L3_ffn_all
    return {'x': x, 'ctx_1024': ctx_1024, 'fside_BxS_0': fside_BxS_0, 'mask_BxS2_bk0': mask_BxS2_bk0, 'g_xattn': g_xattn, 'g_ffn': g_ffn, 'L0_xattn_Wk_w': _L0_xattn_in['Wk_w'], 'L0_xattn_Wk_b': _L0_xattn_in['Wk_b'], 'L0_xattn_Wv_w': _L0_xattn_in['Wv_w'], 'L0_xattn_Wv_b': _L0_xattn_in['Wv_b'], 'L0_ffn_router_w': _L0_ffn_in['router_w'], 'L0_ffn_w1': _L0_ffn_in['w1'], 'L0_ffn_w2': _L0_ffn_in['w2'], 'L1_xattn_qn_w': _L1_xattn_in['qn_w'], 'L1_xattn_qn_b': _L1_xattn_in['qn_b'], 'L1_xattn_cn_w': _L1_xattn_in['cn_w'], 'L1_xattn_cn_b': _L1_xattn_in['cn_b'], 'L1_xattn_Wq': _L1_xattn_in['Wq'], 'L1_xattn_bq': _L1_xattn_in['bq'], 'L1_xattn_Wk': _L1_xattn_in['Wk'], 'L1_xattn_bk': _L1_xattn_in['bk'], 'L1_xattn_Wv': _L1_xattn_in['Wv'], 'L1_xattn_bv': _L1_xattn_in['bv'], 'L1_xattn_Wo': _L1_xattn_in['Wo'], 'L1_xattn_bo': _L1_xattn_in['bo'], 'L1_ffn_wg': _L1_ffn_in['wg'], 'L1_ffn_w1': _L1_ffn_in['w1'], 'L1_ffn_w2': _L1_ffn_in['w2'], 'L2_xattn_tab_g': _L2_xattn_in['tab_g'], 'L2_xattn_tab_b': _L2_xattn_in['tab_b'], 'L2_xattn_vid_g': _L2_xattn_in['vid_g'], 'L2_xattn_vid_b': _L2_xattn_in['vid_b'], 'L2_xattn_Wq': _L2_xattn_in['Wq'], 'L2_xattn_Wk': _L2_xattn_in['Wk'], 'L2_xattn_Wv': _L2_xattn_in['Wv'], 'L2_xattn_q_g': _L2_xattn_in['q_g'], 'L2_xattn_q_b': _L2_xattn_in['q_b'], 'L2_xattn_k_g': _L2_xattn_in['k_g'], 'L2_xattn_k_b': _L2_xattn_in['k_b'], 'L2_xattn_Wo': _L2_xattn_in['Wo'], 'L2_xattn_bo': _L2_xattn_in['bo'], 'L2_ffn_weight': _L2_ffn_in['weight'], 'L3_xattn_W_gate': _L3_xattn_in['W_gate'], 'L3_xattn_b_gate': _L3_xattn_in['b_gate'], 'L3_xattn_W_lin': _L3_xattn_in['W_lin'], 'L3_xattn_b_lin': _L3_xattn_in['b_lin'], 'L3_ffn_ln1_scale': _L3_ffn_in['ln1_scale'], 'L3_ffn_ln1_shift': _L3_ffn_in['ln1_shift'], 'L3_ffn_wq': _L3_ffn_in['wq'], 'L3_ffn_wk': _L3_ffn_in['wk'], 'L3_ffn_wv': _L3_ffn_in['wv'], 'L3_ffn_wo': _L3_ffn_in['wo'], 'L3_ffn_bo': _L3_ffn_in['bo'], 'L3_ffn_ln2_scale': _L3_ffn_in['ln2_scale'], 'L3_ffn_ln2_shift': _L3_ffn_in['ln2_shift'], 'L3_ffn_gate_w': _L3_ffn_in['gate_w'], 'L3_ffn_w1': _L3_ffn_in['w1'], 'L3_ffn_w2': _L3_ffn_in['w2'], 'L3_ffn_w3': _L3_ffn_in['w3']}

def reference(x, ctx_1024, fside_BxS_0, mask_BxS2_bk0, g_xattn, g_ffn, L0_xattn_Wk_w, L0_xattn_Wk_b, L0_xattn_Wv_w, L0_xattn_Wv_b, L0_ffn_router_w, L0_ffn_w1, L0_ffn_w2, L1_xattn_qn_w, L1_xattn_qn_b, L1_xattn_cn_w, L1_xattn_cn_b, L1_xattn_Wq, L1_xattn_bq, L1_xattn_Wk, L1_xattn_bk, L1_xattn_Wv, L1_xattn_bv, L1_xattn_Wo, L1_xattn_bo, L1_ffn_wg, L1_ffn_w1, L1_ffn_w2, L2_xattn_tab_g, L2_xattn_tab_b, L2_xattn_vid_g, L2_xattn_vid_b, L2_xattn_Wq, L2_xattn_Wk, L2_xattn_Wv, L2_xattn_q_g, L2_xattn_q_b, L2_xattn_k_g, L2_xattn_k_b, L2_xattn_Wo, L2_xattn_bo, L2_ffn_weight, L3_xattn_W_gate, L3_xattn_b_gate, L3_xattn_W_lin, L3_xattn_b_lin, L3_ffn_ln1_scale, L3_ffn_ln1_shift, L3_ffn_wq, L3_ffn_wk, L3_ffn_wv, L3_ffn_wo, L3_ffn_bo, L3_ffn_ln2_scale, L3_ffn_ln2_shift, L3_ffn_gate_w, L3_ffn_w1, L3_ffn_w2, L3_ffn_w3):
    import jax
    import jax.numpy as jnp

    def _L0_xattn_ref(query, key, value, Wk_w, Wk_b, Wv_w, Wv_b):
        import jax, jax.numpy as jnp
        import numpy as np
        NUM_HEADS = 16
        HIDDEN = 128
        HEAD_DIM = HIDDEN // NUM_HEADS
        B, S, D = (2, 256, 128)
        b, s, _ = query.shape

        def split_heads(x):
            return x.reshape(b, s, NUM_HEADS, HEAD_DIM).transpose(0, 2, 1, 3)
        q = split_heads(query @ Wk_w.T + Wk_b)
        k = split_heads(key @ Wv_w.T + Wv_b)
        v = split_heads(value @ Wv_w.T + Wv_b)
        scores = jnp.einsum('bhqd,bhkd->bhqk', q, k) / jnp.sqrt(jnp.asarray(HEAD_DIM, dtype=q.dtype))
        probs = jax.nn.softmax(scores, axis=-1)
        out = jnp.einsum('bhqk,bhkd->bhqd', probs, v)
        return out.transpose(0, 2, 1, 3).reshape(b, s, NUM_HEADS * HEAD_DIM)

    def _L0_ffn_ref(x, router_w, w1, w2):
        import jax, jax.numpy as jnp
        import numpy as np
        N_EXPERTS = 8
        TOP_K = 2
        B, T, C = x.shape
        E = N_EXPERTS
        xf = x.reshape(-1, C)
        logits = jnp.einsum('nc,ec->ne', xf, router_w)
        probs = jax.nn.softmax(logits, axis=-1)
        top_w, top_i = jax.lax.top_k(probs, TOP_K)
        top_w = top_w / jnp.sum(top_w, axis=-1, keepdims=True)
        comb = jnp.einsum('nk,nke->ne', top_w, jax.nn.one_hot(top_i, E, dtype=xf.dtype))
        h = jax.nn.gelu(jnp.einsum('nc,ech->enh', xf, w1), approximate=False)
        y = jnp.einsum('enh,ehc->enc', h, w2)
        out = jnp.einsum('ne,enc->nc', comb, y)
        return out.reshape(B, T, C)

    def _L1_xattn_ref(query, context, context_mask, qn_w, qn_b, cn_w, cn_b, Wq, bq, Wk, bk, Wv, bv, Wo, bo):
        import jax, jax.numpy as jnp
        import numpy as np
        DIM = 128
        NUM_HEADS = 16
        HEAD_DIM = DIM // NUM_HEADS
        SCALE = HEAD_DIM ** (-0.5)
        EPS = 1e-05

        def _layernorm(x, w, b):
            mu = jnp.mean(x, axis=-1, keepdims=True)
            var = jnp.mean(jnp.square(x - mu), axis=-1, keepdims=True)
            return (x - mu) * jax.lax.rsqrt(var + EPS) * w + b

        def _split_heads(x):
            B, L, _ = x.shape
            return x.reshape(B, L, NUM_HEADS, HEAD_DIM).transpose(0, 2, 1, 3)
        B, Lq, _ = query.shape
        fully_masked = jnp.all(context_mask, axis=1)
        mask = context_mask.at[:, 0].set(jnp.where(fully_masked, False, context_mask[:, 0]))
        qn = _layernorm(query, qn_w, qn_b)
        cn = _layernorm(context, cn_w, cn_b)
        q = _split_heads(qn @ Wq.T + bq)
        k = _split_heads(cn @ Wk.T + bk)
        v = _split_heads(cn @ Wv.T + bv)
        logits = jnp.einsum('bhqd,bhkd->bhqk', q * SCALE, k)
        logits = jnp.where(mask[:, None, None, :], -jnp.inf, logits)
        attn = jax.nn.softmax(logits, axis=-1)
        out = jnp.einsum('bhqk,bhkd->bhqd', attn, v)
        out = out.transpose(0, 2, 1, 3).reshape(B, Lq, DIM)
        return out @ Wo.T + bo

    def _L1_ffn_ref(x, wg, w1, w2):
        import jax, jax.numpy as jnp
        import numpy as np
        CAPACITY_FACTOR = 1.0

        def _top1_gate(x2d, wg):
            S, _ = x2d.shape
            E = wg.shape[1]
            C = int(CAPACITY_FACTOR * S / E)
            logits = x2d @ wg
            gates = jax.nn.softmax(logits, axis=-1)
            idx = jnp.argmax(gates, axis=-1)
            mask = jax.nn.one_hot(idx, E, dtype=jnp.int32)
            loc = jnp.cumsum(mask, axis=0) - 1
            me = jnp.mean(gates, axis=0)
            ce = jnp.mean(mask.astype(gates.dtype), axis=0)
            l_aux = E * jnp.sum(me * ce)
            mask = mask * (loc < C).astype(jnp.int32)
            gate_s = jnp.sum(gates * mask, axis=-1)
            loc_s = jnp.sum(loc * mask, axis=-1)
            loc_oh = jax.nn.one_hot(loc_s, C, dtype=gates.dtype)
            combine = (gate_s[:, None] * mask.astype(gates.dtype))[:, :, None] * loc_oh[:, None, :]
            dispatch = (combine > 0).astype(gates.dtype)
            return (l_aux, combine, dispatch)
        s, b, m = x.shape
        x2d = x.reshape(-1, m)
        l_aux, combine, dispatch = _top1_gate(x2d, wg)
        combine = combine[:, None]
        dispatch = dispatch[:, None]
        xr = x2d[:, None, :]
        dispatched = jnp.einsum('szfc,szm->zfcm', dispatch, xr)
        E = w1.shape[0]
        di = dispatched.reshape(E, -1, m)
        h = jax.nn.relu(jnp.einsum('ecm,emh->ech', di, w1))
        eo = jnp.einsum('ech,ehm->ecm', h, w2)
        eo = eo[None]
        out = jnp.einsum('szfc,zfcm->sm', combine, eo)
        return out.reshape(s, b, m)

    def _L2_xattn_ref(x, tab_x, tab_g, tab_b, vid_g, vid_b, Wq, Wk, Wv, q_g, q_b, k_g, k_b, Wo, bo):
        import jax, jax.numpy as jnp
        import numpy as np
        EPS = 1e-05

        def layernorm(x, g, b):
            mu = jnp.mean(x, axis=-1, keepdims=True)
            var = jnp.var(x, axis=-1, keepdims=True)
            return (x - mu) * jax.lax.rsqrt(var + EPS) * g + b
        DIM = 128
        CTX = 128
        HEADS = 12
        DHEAD = 64
        INNER = HEADS * DHEAD
        B = 4
        F = 256
        J = 128
        scale = DHEAD ** (-0.5)
        kv_in = layernorm(tab_x, tab_g, tab_b)
        q = layernorm(layernorm(x, vid_g, vid_b) @ Wq, q_g, q_b)
        k = layernorm(kv_in @ Wk, k_g, k_b)
        v = kv_in @ Wv
        split = lambda t: t.reshape(t.shape[0], t.shape[1], HEADS, DHEAD).transpose(0, 2, 1, 3)
        q, k, v = (split(q) * scale, split(k), split(v))
        sim = jnp.einsum('bhid,bhjd->bhij', q, k)
        attn = jax.nn.softmax(sim, axis=-1)
        out = jnp.einsum('bhij,bhjd->bhid', attn, v)
        out = out.transpose(0, 2, 1, 3).reshape(x.shape[0], x.shape[1], INNER)
        return out @ Wo + bo

    def _L2_ffn_ref(x, weight):
        import jax, jax.numpy as jnp
        import numpy as np
        EPS = 1e-08
        w_scale = jnp.mean(jnp.abs(weight)) + EPS
        u = weight / w_scale
        w_quant = u + jax.lax.stop_gradient(jnp.clip(jnp.round(u), -1.0, 1.0) - u)
        a_scale = jnp.max(jnp.abs(x), axis=-1, keepdims=True) + EPS
        z = jnp.clip(x / a_scale * 127.0, -128.0, 127.0)
        a_quant = z + jax.lax.stop_gradient(jnp.round(z) - z)
        y = jnp.einsum('bsi,oi->bso', a_quant, w_quant)
        y = y * (w_scale * a_scale / 127.0)
        return y

    def _L3_xattn_ref(h, ht, position_weights, W_gate, b_gate, W_lin, b_lin):
        import jax, jax.numpy as jnp
        import numpy as np
        t = jax.nn.sigmoid(jnp.einsum('bld,de->ble', h, W_gate) + b_gate)
        scores = jnp.einsum('bld,bmd->blm', h, ht)
        alpha = jax.nn.softmax(scores, axis=-1)
        r = jnp.einsum('blm,bmd->bld', alpha, ht)
        D = h.shape[-1]
        h_new = jnp.tanh(jnp.einsum('bld,de->ble', r, W_lin[:D]) + jnp.einsum('bld,de->ble', h, W_lin[D:]) + b_lin)
        h_new = h_new * position_weights[:, :, None]
        return t * h_new + (1.0 - t) * h

    def _L3_ffn_ref(x, ln1_scale, ln1_shift, wq, wk, wv, wo, bo, ln2_scale, ln2_shift, gate_w, w1, w2, w3):
        import jax, jax.numpy as jnp
        import numpy as np
        EMB = 128
        HID = 256
        HEADS = 16
        HEAD_DIM = EMB // HEADS
        EXPERTS = 8
        TOPK = 2
        EPS = 1e-05

        def layernorm(x, scale, shift):
            mean = jnp.mean(x, axis=-1, keepdims=True)
            var = jnp.mean((x - mean) ** 2, axis=-1, keepdims=True)
            return scale * (x - mean) / jnp.sqrt(var + EPS) + shift

        def attention(x, wq, wk, wv, wo, bo):
            b, t, _ = x.shape
            q = (x @ wq).reshape(b, t, HEADS, HEAD_DIM)
            k = (x @ wk).reshape(b, t, HEADS, HEAD_DIM)
            v = (x @ wv).reshape(b, t, HEADS, HEAD_DIM)
            scores = jnp.einsum('bqhd,bkhd->bhqk', q, k)
            mask = jnp.arange(t)[:, None] < jnp.arange(t)[None, :]
            scores = jnp.where(mask, -jnp.inf, scores)
            attn = jax.nn.softmax(scores / np.sqrt(HEAD_DIM), axis=-1)
            ctx = jnp.einsum('bhqk,bkhd->bqhd', attn, v).reshape(b, t, EMB)
            return ctx @ wo + bo

        def moe_ff(x, gate_w, w1, w2, w3):
            b, t, d = x.shape
            xf = x.reshape(b * t, d)
            scores = xf @ gate_w
            topk_scores, topk_idx = jax.lax.top_k(scores, TOPK)
            topk_probs = jax.nn.softmax(topk_scores, axis=-1)
            weight = jnp.sum(jax.nn.one_hot(topk_idx, EXPERTS, dtype=xf.dtype) * topk_probs[..., None], axis=1)
            h = jax.nn.silu(jnp.einsum('td,edh->eth', xf, w1)) * jnp.einsum('td,edh->eth', xf, w2)
            out_e = jnp.einsum('eth,ehd->etd', h, w3)
            out = jnp.einsum('etd,te->td', out_e, weight)
            return out.reshape(b, t, d)
        h = layernorm(x, ln1_scale, ln1_shift)
        x = x + attention(h, wq, wk, wv, wo, bo)
        h = layernorm(x, ln2_scale, ln2_shift)
        x = x + moe_ff(h, gate_w, w1, w2, w3)
        return x
    x = x + jnp.tanh(g_xattn[0]) * _L0_xattn_ref(_layernorm(x, axis=-1), ctx_1024, ctx_1024, L0_xattn_Wk_w, L0_xattn_Wk_b, L0_xattn_Wv_w, L0_xattn_Wv_b)
    x = x + jnp.tanh(g_ffn[0]) * _L0_ffn_ref(_layernorm(x, axis=-1), L0_ffn_router_w, L0_ffn_w1, L0_ffn_w2)
    x = x + jnp.tanh(g_xattn[1]) * _L1_xattn_ref(_layernorm(x, axis=-1), ctx_1024, mask_BxS2_bk0, L1_xattn_qn_w, L1_xattn_qn_b, L1_xattn_cn_w, L1_xattn_cn_b, L1_xattn_Wq, L1_xattn_bq, L1_xattn_Wk, L1_xattn_bk, L1_xattn_Wv, L1_xattn_bv, L1_xattn_Wo, L1_xattn_bo)
    x = x + jnp.tanh(g_ffn[1]) * _L1_ffn_ref(_layernorm(x, axis=-1), L1_ffn_wg, L1_ffn_w1, L1_ffn_w2)
    x = x + jnp.tanh(g_xattn[2]) * _L2_xattn_ref(_layernorm(x, axis=-1), ctx_1024, L2_xattn_tab_g, L2_xattn_tab_b, L2_xattn_vid_g, L2_xattn_vid_b, L2_xattn_Wq, L2_xattn_Wk, L2_xattn_Wv, L2_xattn_q_g, L2_xattn_q_b, L2_xattn_k_g, L2_xattn_k_b, L2_xattn_Wo, L2_xattn_bo)
    x = x + jnp.tanh(g_ffn[2]) * _L2_ffn_ref(_layernorm(x, axis=-1), L2_ffn_weight)
    x = x + jnp.tanh(g_xattn[3]) * _L3_xattn_ref(_layernorm(x, axis=-1), ctx_1024, fside_BxS_0, L3_xattn_W_gate, L3_xattn_b_gate, L3_xattn_W_lin, L3_xattn_b_lin)
    x = x + jnp.tanh(g_ffn[3]) * _L3_ffn_ref(_layernorm(x, axis=-1), L3_ffn_ln1_scale, L3_ffn_ln1_shift, L3_ffn_wq, L3_ffn_wk, L3_ffn_wv, L3_ffn_wo, L3_ffn_bo, L3_ffn_ln2_scale, L3_ffn_ln2_shift, L3_ffn_gate_w, L3_ffn_w1, L3_ffn_w2, L3_ffn_w3)
    return x

_drawn_inputs = setup_inputs


def setup_inputs(seed=0):
    import zlib

    import numpy as np

    out = dict(_drawn_inputs(seed))
    spreads = {'L1_xattn_qn_w': (1.0, 0.2),
     'L1_xattn_qn_b': (0.0, 0.284),
     'L1_xattn_cn_w': (1.0, 0.2),
     'L1_xattn_cn_b': (0.0, 0.1),
     'L1_xattn_bq': (0.0, 0.332),
     'L1_xattn_bk': (0.0, 0.8),
     'L1_xattn_bv': (0.0, 0.1),
     'L1_xattn_bo': (0.0, 0.1),
     'L2_xattn_tab_g': (1.0, 0.2),
     'L2_xattn_tab_b': (0.0, 0.1),
     'L2_xattn_vid_g': (1.0, 0.2),
     'L2_xattn_vid_b': (0.0, 0.324),
     'L2_xattn_q_g': (1.0, 0.2),
     'L2_xattn_q_b': (0.0, 0.352),
     'L2_xattn_k_g': (1.0, 0.2),
     'L2_xattn_k_b': (0.0, 0.8),
     'L2_xattn_bo': (0.0, 0.1),
     'L3_xattn_b_gate': (0.0, 0.31),
     'L3_xattn_b_lin': (0.0, 0.335),
     'L3_ffn_ln1_scale': (1.0, 0.2),
     'L3_ffn_ln1_shift': (0.0, 0.1),
     'L3_ffn_bo': (0.0, 0.1),
     'L3_ffn_ln2_scale': (1.0, 0.2),
     'L3_ffn_ln2_shift': (0.0, 0.1)}
    factors = {'L1_ffn_wg': 4.13, 'L1_ffn_w1': 5.062, 'L1_ffn_w2': 4.409}
    for name, (base, spread) in spreads.items():
        noise = np.random.default_rng([zlib.crc32(name.encode()), seed]).standard_normal(out[name].shape)
        drawn = base * np.exp(spread * noise) if base else spread * noise
        out[name] = jnp.asarray(drawn.astype(out[name].dtype))
    for name, factor in factors.items():
        out[name] = (out[name] * factor).astype(out[name].dtype)
    return out
```

```python
from contextlib import ExitStack

import numpy as np

import concourse.bass as bass
from concourse import mybir

F32 = mybir.dt.float32
BF16 = mybir.dt.bfloat16
I32 = mybir.dt.int32
U32 = mybir.dt.uint32
U8 = mybir.dt.uint8
ALU = mybir.AluOpType
ACT = mybir.ActivationFunctionType
AX = mybir.AxisListType

P = 128
C = 128
B, SEQ = 32, 64
TOK = B * SEQ
NT = TOK // P
PAIR = P // SEQ
HEADS, HD = 16, 8
GROUPS, HPG = 4, 4
H2, DH2 = 12, 64
INNER = H2 * DH2
CH2 = INNER // P
NE, HID = 8, 512
HJ = HID // P
HID3 = 256
CAP = TOK // NE
TOP2_BLOCKS = 2 * TOK // P + NE
TOP1_BLOCKS = TOK // P
ROWS = TOP2_BLOCKS * P
LN_EPS = 1e-5
BIT_EPS = 1e-8
NEG = -1e30
ROUND = 1.5 * 2.0 ** 23

COLS = ["bq0", "bk0", "qn_w1", "qn_b1", "cn_w1", "cn_b1", "bq1", "bk1", "tab_g", "tab_b", "vid_g", "vid_b",
        "ln1_w", "ln1_b", "ln2_w", "ln2_b"] + [f"qg{i}" for i in range(CH2)] + [f"qb{i}" for i in range(CH2)] + [
            f"kg{i}" for i in range(CH2)] + [f"kb{i}" for i in range(CH2)]
COL = {n: i for i, n in enumerate(COLS)}
ROWV = ["bv0", "bv1", "bo1", "bo2", "b_gate", "b_lin", "bo3"]
ROW = {n: i for i, n in enumerate(ROWV)}
SQ = ["wq0", "wv0", "wq1", "wk1", "wv1", "wo1", "w_gate", "w_lin_r", "w_lin_h", "wq3", "wk3", "wv3", "wo3", "w_bitT"]
SQI = {n: i for i, n in enumerate(SQ)}

N_PHASES = 8


class Ring:

    def __init__(self, n, lag):
        self.n, self.lag = n, lag

    def run(self, eng, stages):
        first = self.lag + 2 + self.lag % 2
        last = self.n - self.n % 2

        def step(i, par):
            for stage, lag in stages:
                t = i - lag
                if isinstance(i, int) and not 0 <= t < self.n:
                    continue
                stage(t, (par - lag) % 2)

        for i in range(min(first, self.n + self.lag)):
            step(i, i % 2)
        if last > first:
            with eng.Fori(first // 2, last // 2) as pair:
                for par in range(2):
                    step(pair * 2 + par, par)
        for i in range(max(first, last), self.n + self.lag):
            step(i, i % 2)


def upto(v, most):
    return min(v, most) if isinstance(v, int) else v


def build(nc, io):
    with ExitStack() as ctx:
        def sb(name, shape, dt=F32):
            return ctx.enter_context(nc.sbuf_tensor(name, shape, dt))

        def two(name, shape, dt=F32):
            return [sb(f"{name}{u}", shape, dt) for u in range(2)]

        sems = {}

        def sem(name):
            if name not in sems:
                sems[name] = ctx.enter_context(nc.semaphore(name))
            return sems[name]

        x = sb("x", [P, NT, C])
        y3 = sb("y3", [P, NT, C])
        hn = sb("hn", [P, NT, C])
        ctxn = sb("ctxn", [P, NT, C])
        ctxT = sb("ctxT", [P, TOK])
        zT = sb("zT", [P, TOK])
        wsq = sb("wsq", [P, len(SQ), P])
        cols = sb("cols", [P, len(COLS)])
        rows = sb("rows", [1, len(ROWV), P])
        bvB = sb("bvB", [P, 2, P])
        wq2 = sb("wq2", [P, INNER])
        wk2 = sb("wk2", [P, INNER])
        wv2 = sb("wv2", [P, INNER])
        wo2 = sb("wo2", [P, CH2, P])
        rw = sb("rw", [P, 3, NE])
        w1 = [sb(f"w1_{n}", [P, NE * HID]) for n in range(2)]
        w2 = [sb(f"w2_{n}", [P, NE * HJ * C]) for n in range(2)]
        w1, w2 = w1 + w1[:1], w2 + w2[:1]
        pw = sb("pw", [P, NT])
        gates_raw = sb("gates_raw", [P, 8])
        gates = sb("gates", [P, 8])
        maskraw = sb("maskraw", [PAIR, NT, SEQ // 4], I32)
        maskf = sb("maskf", [PAIR, NT, SEQ])
        maskall = sb("maskall", [PAIR, NT])
        maskrow = sb("maskrow", [PAIR, NT, SEQ], BF16)

        ident = sb("ident", [P, P])
        identb = sb("identb", [P, P], BF16)
        pairsel = sb("pairsel", [PAIR, P], BF16)
        causal = sb("causal", [P, SEQ], BF16)
        headmask = sb("headmask", [P, HPG])
        ones = sb("ones", [P, P])
        before = sb("before", [P, P])
        powm = sb("powm", [P, NT])
        iota8 = sb("iota8", [P, NE])
        iotab = sb("iotab", [1, TOP2_BLOCKS])
        runmask = sb("runmask", [P, NE, NT])
        tokid = sb("tokid", [P, NT])
        zero_rows = hn[:, 0:NT // 2, :].rearrange("p t c -> p (t c)")

        st = sb("st", [P, NT, 6])
        st_a = sb("st_a", [P, NT])
        st_b = sb("st_b", [P, NT])
        st_c = sb("st_c", [P, NT])
        mean = sb("mean", [P, NT])
        var = sb("var", [P, NT])
        veps = sb("veps", [P, NT])
        rs = sb("rs", [P, NT])
        rs1 = sb("rs1", [P, NT])

        hs = two("hs", [P, C])
        hT = two("hT", [P, P])
        cT = two("cT", [P, P])
        QT = two("QT", [P, P])
        Kb = two("Kb", [P, HPG, P])
        Vb = two("Vb", [P, HEADS // 2, PAIR, 2, HD + 1])
        Pr = two("Pr", [P, HEADS * SEQ])
        PT = two("PT", [P, HEADS * SEQ])
        mx = two("mx", [P, HEADS])
        rinv = two("rinv", [P, HEADS])
        Oh = two("Oh", [P, HEADS, HD])
        OT = two("OT", [P, P])
        qn = [hn[:, :, :].rearrange("p t c -> p (t c)")[:, u * INNER:(u + 1) * INNER] for u in range(2)]
        kn = [y3[:, :, :].rearrange("p t c -> p (t c)")[:, u * INNER:(u + 1) * INNER] for u in range(2)]
        QT2 = two("QT2", [P, INNER])
        KT2 = two("KT2", [P, INNER])
        Vs = two("Vs", [P, PAIR, INNER // 2])
        OT2 = two("OT2", [P, CH2, P])
        qst = two("qst", [P, 2, 6])
        kst = two("kst", [P, 2, 6])
        qmv = two("qmv", [P, 2])
        kmv = two("kmv", [P, 2])
        qr = two("qr", [P, 1])
        kr = two("kr", [P, 1])
        P3 = two("P3", [P, P])
        sm3 = two("sm3", [P, 4])
        th3, hn3, tmp3 = [[hn[:, 2 * i + u, :] for u in range(2)] for i in range(3)]
        bitq = two("bitq", [P, P], BF16)
        bitT = two("bitT", [P, P], BF16)
        bits = two("bits", [P, 4])
        aggr_gap = sb("aggr_gap", [P, 1])
        wbit = sb("wbit", [P, P], BF16)
        wbtmp = sb("wbtmp", [P, P])
        wstat = sb("wstat", [P, 4])

        route_parts = [Kb[u][:, i, :] for u in range(2) for i in range(HPG)]
        lg, lg2, rt, ohs, *oh = [m.rearrange("p (t e) -> p t e", e=NE) for m in route_parts[:6]]
        rn, rscan = [m.rearrange("p (e t) -> p e t", e=NE) for m in route_parts[6:]]
        rm = [sb(f"rm{k}", [P, NT]) for k in range(2)]
        rk = sb("rk", [P, NT])
        blk = sb("blk", [P, 4, NE])
        blki = sb("blki", [P, NE], I32)
        slotf = sb("slotf", [P, NT])
        keep = sb("keep", [P, NT])
        slot = [sb(f"slot{k}", [P, NT], U32) for k in range(2)]
        wt = [sb(f"wt{k}", [P, NT]) for k in range(2)]
        cmpb = sb("cmpb", [1, TOP2_BLOCKS, NE])
        blkef = sb("blkef", [1, TOP2_BLOCKS])
        blke = sb("blke", [1, TOP2_BLOCKS], I32)
        xb = [QT2[u][:, 0:C] for u in range(2)]
        xbT = [QT2[u][:, C:2 * C] for u in range(2)]
        G = [Pr[u][:, 0:HID] for u in range(2)]
        G3 = [Pr[u][:, HID:HID + HID3] for u in range(2)]
        GT = [PT[u][:, 0:HID] for u in range(2)]
        yb = [QT2[u][:, 2 * C:3 * C] for u in range(2)]

        rows_in = nc.dram_tensor("rows_in", (ROWS, C), F32).ap()
        rows_out = nc.dram_tensor("rows_out", (ROWS, C), F32).ap()

        bank = ctx.enter_context(nc.psum_tensor("bank", [P, 8, 512], F32))
        flat = bank[:, :, :].rearrange("p b n -> p (b n)")
        block = ctx.enter_context(nc.Block())

        def sq(name):
            return wsq[:, SQI[name], :]

        def col(name):
            return cols[:, COL[name]:COL[name] + 1]

        def row(name):
            return rows[0:1, ROW[name], :]

        def tile(buf, t):
            return buf[:, bass.ds(t, 1), :].rearrange("p a c -> p (a c)")

        def at(buf, t):
            return buf[:, bass.ds(t, 1)]

        def toks(buf, t):
            return buf[:, bass.ds(t * P, P)]

        def after(eng, s, n):
            if not isinstance(n, int) or n > 0:
                eng.wait_ge(s, n)

        LNS = [("ctx", False), ("x0", False), ("f0", False), ("x1", True), ("f1", False), ("x2", True), ("f2", False),
               ("x3", False), ("a3", True), ("m3", False)]
        POW = {}
        n = 0
        for name, twice in LNS:
            POW[name] = n
            n += 2 if twice else 1
        LNI = {name: i for i, (name, _) in enumerate(LNS)}
        LOOPS = ["ctx", "x0", "f0", "x1", "f1", "x2", "x3", "a3", "m3"]
        TB = {name: NT * i for i, name in enumerate(LOOPS)}
        ATT = {"x0": 0, "x1": NT, "a3": 2 * NT}
        PROJ = {"x1": 0, "a3": NT}
        MOE = ["f0", "f1", "m3"]
        ROUTE = {"f0": 0, "f1": NT, "m3": 2 * NT}
        NBLK = {"f0": TOP2_BLOCKS, "f1": TOP1_BLOCKS, "m3": TOP2_BLOCKS}
        BB = {"f0": 0, "f1": TOP2_BLOCKS, "m3": TOP2_BLOCKS + TOP1_BLOCKS}
        KTOP = {"f0": 2, "f1": 1, "m3": 2}
        SC = {"f0": 0, "f1": 2, "m3": 3}

        HT_READER = {"x2": ("q2_done", 0), "x3": ("l3_done", 0)}
        HT_READER.update({n: ("v_done", c) for n, c in ATT.items()})
        HT_READER.update({n: ("lg_done", c) for n, c in ROUTE.items()})

        PH = ["ctx", "x0", "f0", "x1", "f1", "x2", "f2", "x3", "a3", "m3"]
        PHI = {n: i for i, n in enumerate(PH)}

        def phases():
            return PH[:N_PHASES + 2] if N_PHASES >= 8 else PH[:N_PHASES + 1]

        def phase_start(eng, name):
            if PHI[name]:
                eng.wait_ge(sem("phase_done"), PHI[name])

        def second_rows(name):
            return ctxn if name == "m3" else y3

        att = Ring(NT, 5)
        att2 = Ring(NT, 4)
        pre = Ring(NT, 3)
        xl3 = Ring(NT, 3)
        bit = Ring(NT, 3)

        S_att = bank[:, 0:GROUPS, 0:256]
        PT_ps = flat[:, 4 * 512:6 * 512]
        TO_ps = bank[:, 6, 0:128]
        Q_ps = bank[:, 6, 0:128]
        K_ps = bank[:, 6, 128:256]
        V_ps = bank[:, 6, 256:512]
        O_ps = bank[:, 7, 0:288]
        OY_ps = bank[:, 7, 288:416]
        L_ps = bank[:, 7, 0:NE]
        A2 = bank[:, 0:2, 0:384]
        B2 = bank[:, 2:4, 0:384]
        C2 = bank[:, 4:6, 0:384]
        D2 = bank[:, 6:8, 0:384]
        T2_ps = bank[:, 6, 384:512]
        Y2_ps = bank[:, 3, 384:512]

        @block.sync
        def _(sp):
            sp.dma_start(x[:, :, :], io["x"].rearrange("(t p) c -> p t c", p=P)).then_inc(sem("x_in"), 16)
            sp.dma_start(ctxn[:, :, :], io["ctx"].rearrange("(t p) c -> p t c", p=P)).then_inc(sem("ctx_in"), 16)
            sp.dma_start(cols[:, :], io["cols"]).then_inc(sem("vec_in"), 16)
            sp.dma_start(wsq[:, :, :], io["wsq"].rearrange("n p c -> p n c")).then_inc(sem("vec_in"), 16)
            sp.dma_start(rows[0:1, :, :], io["rows"].rearrange("(a n) c -> a n c", a=1)).then_inc(sem("vec_in"), 16)
            sp.dma_start(bvB[:, 0, :], io["rows"][0:1, :].to_broadcast([P, P])).then_inc(sem("vec_in"), 16)
            sp.dma_start(bvB[:, 1, :], io["rows"][1:2, :].to_broadcast([P, P])).then_inc(sem("vec_in"), 16)
            sp.dma_start(gates_raw[:, :], io["g"].to_broadcast([P, 8])).then_inc(sem("vec_in"), 16)
            sp.dma_start(pw[:, :], io["pw"]).then_inc(sem("vec_in"), 16)
            sp.dma_start(maskraw[:, :, :], io["mask"].rearrange("(t b) s -> b t s", b=PAIR)).then_inc(sem("vec_in"), 16)
            sp.dma_start(rw[:, :, :], io["rw"].rearrange("n p e -> p n e")).then_inc(sem("vec_in"), 16)
            sp.dma_start(ctxT[:, :], io["ctxT"]).then_inc(sem("ctxT_in"), 16)
            for name, buf in (("wq2", wq2), ("wk2", wk2), ("wv2", wv2)):
                sp.dma_start(buf[:, :], io[name]).then_inc(sem("w_in2"), 16)
            sp.dma_start(wo2[:, :, :], io["wo2"].rearrange("(i p) c -> p i c", p=P)).then_inc(sem("w_in2"), 16)

            def expert_weights(k):
                w1v = w1[k][:, :].rearrange("p (e h) -> p e h", e=NE)
                if k < 2:
                    sp.dma_start(w1v, io[f"w1_{k}"].rearrange("e c h -> c e h")).then_inc(sem("moe_w"), 16)
                else:
                    sp.dma_start(w1v[:, :, 0:HID3], io["w1_2"].rearrange("e c h -> c e h")).then_inc(sem("moe_w"), 16)
                    sp.dma_start(w1v[:, :, HID3:HID], io["w1_3"].rearrange("e c h -> c e h")).then_inc(sem("moe_w"), 16)
                n = io[f"w2_{k}"].shape[1] // P
                for e in range(NE):
                    sp.dma_start(w2[k][:, e * n * C:(e + 1) * n * C].rearrange("p (j c) -> p j c", c=C),
                                 io[f"w2_{k}"][e].rearrange("(j p) c -> p j c", p=P)).then_inc(sem("moe_w"), 16)

            expert_weights(0)
            expert_weights(1)
            sp.wait_ge(sem("zeros"), 1)
            zr = rows_in.rearrange("(p n) c -> p (n c)", p=P)
            for k in range(ROWS * C // P // 1024):
                sp.dma_start(zr[:, k * 1024:(k + 1) * 1024], zero_rows).then_inc(sem("rows_zeroed"), 16)

            for name in phases():
                if name not in MOE:
                    continue
                base, nb = BB[name], NBLK[name]
                sp.wait_ge(sem("scattered"), 16 * NT * (SC[name] + KTOP[name]))

                def load(b, u):
                    after(sp, sem("xbT1"), base + b - 1)
                    sp.dma_start(xb[u], rows_in[bass.ds(b * P, P), :]).then_inc(sem(f"xb_in{u}"), 16)

                def store(b, u):
                    sp.wait_ge(sem("yb_ready"), base + b + 1)
                    sp.dma_start(rows_out[bass.ds(b * P, P), :], yb[u]).then_inc(sem(f"yb_out{u}"), 16)

                Ring(nb, 4).run(sp, [(load, 0), (store, 4)])
                if name == "f0":
                    sp.wait_ge(sem("phase_done"), PHI[name] + 1)
                    expert_weights(2)

            sp.wait_ge(sem("phase_done"), len(phases()))
            sp.dma_start(io["out"].rearrange("(t p) c -> p t c", p=P), x[:, :, :]).then_inc(sem("out_done"), 16)
            sp.wait_ge(sem("out_done"), 16)

        @block.gpsimd
        def _(pool):
            g = nc.gpsimd
            chain = [0]

            def link(ins):
                chain[0] += 1
                ins.then_inc(sem("pool_chain"), 1)
                pool.wait_ge(sem("pool_chain"), chain[0])

            def select(out, fill, base, pattern, mult, op=ALU.not_equal):
                link(g.affine_select(out=out, in_=out, compare_op=op, fill=fill, base=base, pattern=pattern,
                                     channel_multiplier=mult))

            link(g.memset(ident[:, :], 0.0))
            select(ident[:, :], 1.0, 0, [[-1, P]], 1)
            link(g.tensor_copy(identb[:, :], ident[:, :]))
            link(g.memset(powm[:, :], -0.5))
            link(g.memset(ones[:, :], 1.0))
            link(g.memset(headmask[:, :], 0.0))
            for grp in range(GROUPS):
                link(g.memset(before[:, 0:HPG], 1.0))
                select(before[:, 0:HPG], 0.0, -32 * grp, [[-8, HPG]], 1, ALU.is_ge)
                select(before[:, 0:HPG], 0.0, 32 * grp + 7, [[8, HPG]], -1, ALU.is_ge)
                link(g.tensor_tensor(headmask[:, :], headmask[:, :], before[:, 0:HPG], ALU.add))
            link(g.memset(pairsel[:, :], 1.0))
            select(pairsel[:, :].rearrange("b (c q) -> b c q", c=PAIR), 0.0, 0, [[-1, PAIR], [0, SEQ]], 1, ALU.is_equal)
            link(g.memset(causal[:, :], 0.0))
            select(causal[0:SEQ, :], NEG, 0, [[-1, SEQ]], 1, ALU.is_ge)
            select(causal[SEQ:P, :], NEG, 0, [[-1, SEQ]], 1, ALU.is_ge)
            link(g.memset(before[:, :], 1.0))
            select(before[:, :], 0.0, 0, [[1, P]], -1, ALU.is_gt)
            link(g.iota(slot[0][:, 0:NE].bitcast(I32), pattern=[[1, NE]], base=0, channel_multiplier=0))
            link(g.tensor_copy(iota8[:, :], slot[0][:, 0:NE].bitcast(I32)))
            link(g.iota(blke[:, :], pattern=[[1, TOP2_BLOCKS]], base=0, channel_multiplier=0))
            link(g.tensor_copy(iotab[:, :], blke[:, :]))
            link(g.iota(slot[1][:, :].bitcast(I32), pattern=[[P, NT]], base=0, channel_multiplier=1))
            link(g.tensor_copy(tokid[:, :], slot[1][:, :].bitcast(I32)))
            link(g.memset(runmask[:, :, :], 1.0))
            link(g.memset(runmask[:, :, 0:1], 0.0))
            for u in range(2):
                link(g.memset(Vb[u][:, :, :, :, :], 0.0))
                for half in range(2):
                    link(g.memset(Vb[u][half * SEQ:(half + 1) * SEQ, :, :, half, HD:HD + 1], 1.0))
                link(g.memset(P3[u][:, :], 0.0))
            link(g.memset(zero_rows, 0.0))
            g.engine_nop().then_inc(sem("zeros"), 1)
            g.engine_nop().then_inc(sem("pool_ready"), 2)

            def powers(name, count):
                for k in range(count):
                    pool.wait_ge(sem("var_ready"), POW[name] + k + 1)
                    g.tensor_tensor(rs[:, :], veps[:, :], powm[:, :], ALU.pow).then_inc(sem("rstd_ready"), 1)

            for name in phases():
                phase_start(pool, name)
                powers(name, 2 if dict(LNS)[name] else 1)
                if name == "x0":
                    pool.wait_ge(sem("ctxT_in"), 16)

                    def stage(t, u):
                        after(pool, sem("v_done"), ATT[name] + t - 1)
                        g.tensor_copy(cT[u][:, :], toks(ctxT, t)).then_inc(sem("cT_ready"), 1)

                    att.run(pool, [(stage, 0)])
                if name == "x2":
                    def pow_q(t, u):
                        pool.wait_ge(sem("qvar"), t + 1)
                        g.tensor_tensor(qr[u][:, :], qmv[u][:, 1:2], powm[:, 0:1], ALU.pow).then_inc(sem("qr_ready"), 1)

                    def pow_k(t, u):
                        pool.wait_ge(sem("kvar"), t + 1)
                        g.tensor_tensor(kr[u][:, :], kmv[u][:, 1:2], powm[:, 0:1], ALU.pow).then_inc(sem("kr_ready"), 1)

                    def pnorm(t, u):
                        pool.wait_ge(sem("rinv2"), t + 1)
                        pv = Pr[u][:, 0:INNER].rearrange("p (h k) -> p h k", h=H2)
                        g.tensor_tensor(pv, pv, rinv[u][:, 0:H2].unsqueeze(2).to_broadcast([P, H2, SEQ]),
                                        ALU.mult).then_inc(sem("pn2"), 1)

                    att2.run(pool, [(pow_q, 1), (pnorm, 3), (pow_k, 1)])
                if name == "x3":
                    def keep_ctx(t, u):
                        after(pool, sem("r3_done"), t - 1)
                        g.tensor_copy(cT[u][:, :], tile(ctxn, t)).then_inc(sem("cs3_ready"), 1)

                    def keep_h(t, u):
                        pool.wait_ge(sem("hs_ready"), TB[name] + t + 1)
                        g.tensor_copy(tile(y3, t), hs[u][:, :]).then_inc(sem("hs_kept"), 1)

                    xl3.run(pool, [(keep_ctx, 0), (keep_h, 0)])
                if name in MOE:
                    def keep_h(t, u):
                        pool.wait_ge(sem("hs_ready"), TB[name] + t + 1)
                        g.tensor_copy(tile(hn, t), hs[u][:, :]).then_inc(sem("hn_kept"), 1)

                    if name == "f0":
                        pool.wait_ge(sem("rows_zeroed"), 16 * (ROWS * C // P // 1024))
                    pre.run(pool, [(keep_h, 0)])
                    pool.wait_ge(sem("hn_kept"), ROUTE[name] + NT)
                    pool.wait_ge(sem("slots_ready"), MOE.index(name) + 1)
                    for t in range(NT):
                        for k in range(KTOP[name]):
                            g.indirect_dma_start(rows_in[:, :], bass.IndirectOffsetOnAxis(ap=slot[k][:, t:t + 1], axis=0),
                                                 hn[:, t, :], None).then_inc(sem("scattered"), 16)
                    nb, before_b = NBLK[name], BB[name]
                    for u in range(2):
                        pool.wait_ge(sem(f"yb_out{u}"), 16 * (before_b + nb) // 2)
                    for t in range(NT):
                        for k in range(KTOP[name]):
                            g.indirect_dma_start((hn if k == 0 else second_rows(name))[:, t, :], None, rows_out[:, :],
                                                 bass.IndirectOffsetOnAxis(ap=slot[k][:, t:t + 1], axis=0)) \
                                .then_inc(sem(f"gathered{t // 4}"), 16)

        @block.scalar
        def _(act):
            a = nc.scalar
            act.wait_ge(sem("vec_in"), 16 * 9)
            a.activation(gates[:, :], gates_raw[:, :], ACT.Tanh).then_inc(sem("gates_ready"), 1)

            def evac_hT(name, region, w=None, b=None):
                def stage(t, u):
                    act.wait_ge(sem("t1_done"), TB[name] + t + 1)
                    after(act, sem(HT_READER[name][0]), HT_READER[name][1] + t - 1)
                    if w:
                        ins = a.activation(hT[u][:, :], region, ACT.Identity, bias=col(b), scale=col(w))
                    else:
                        ins = a.activation(hT[u][:, :], region, ACT.Copy)
                    ins.then_inc(sem("hT_ready"), 1)
                return stage

            def stage_ctx(scale, shift, used, used_before):
                def stage(t, u):
                    after(act, sem(used), used_before + t - 1)
                    a.activation(cT[u][:, :], toks(zT, t), ACT.Identity, bias=col(shift), scale=col(scale)) \
                        .then_inc(sem("cT_ready"), 1)
                return stage

            for name in phases():
                phase_start(act, name)
                if name == "ctx":
                    def evac_z(t, u):
                        act.wait_ge(sem("t1_done"), t + 1)
                        a.activation(toks(zT, t), TO_ps, ACT.Copy).then_inc(sem("hT_ready"), 1)

                    pre.run(act, [(evac_z, 0)])
                if name in ATT:
                    base = ATT[name]
                    affine = {"x0": (None, None), "x1": ("qn_w1", "qn_b1"), "a3": ("ln1_w", "ln1_b")}[name]
                    bias_q = {"x0": "bq0", "x1": "bq1", "a3": None}[name]

                    def evac_Q(t, u):
                        act.wait_ge(sem("v_done"), base + t + 1)
                        after(act, sem("s_done"), base + t - 1)
                        if bias_q:
                            ins = a.activation(QT[u][:, :], Q_ps, ACT.Identity, bias=col(bias_q))
                        else:
                            ins = a.activation(QT[u][:, :], Q_ps, ACT.Copy)
                        ins.then_inc(sem("QT_ready"), 1)

                    def expo(t, u):
                        act.wait_ge(sem("sub_done"), base + t + 1)
                        a.activation(Pr[u][:, :], Pr[u][:, :], ACT.Exp, scale=float(HD) ** -0.5) \
                            .then_inc(sem("exp_done"), 1)

                    def evac_PT(t, u):
                        act.wait_ge(sem("pt_done"), base + t + 1)
                        after(act, sem("pv_done"), base + t - 1)
                        a.activation(PT[u][:, :], PT_ps, ACT.Copy).then_inc(sem("PT_ready"), 1)

                    def evac_OT(t, u):
                        pbase = PROJ[name]
                        act.wait_ge(sem("ot_done"), pbase + t + 1)
                        after(act, sem("y_done"), pbase + t - 1)
                        a.activation(OT[u][:, :], OY_ps, ACT.Copy).then_inc(sem("OT_ready"), 1)

                    proj = [(evac_OT, 4)] if name in PROJ else []
                    own_ctx = [(stage_ctx("cn_w1", "cn_b1", "v_done", base), 0)] if name == "x1" else []
                    att.run(act, [(evac_PT, 3), (evac_hT(name, TO_ps, *affine), 0)] + proj
                            + [(evac_Q, 1), (expo, 2)] + own_ctx)
                if name == "x2":
                    def expo(t, u):
                        act.wait_ge(sem("sub2"), t + 1)
                        a.activation(Pr[u][:, 0:INNER], Pr[u][:, 0:INNER], ACT.Exp, scale=float(DH2) ** -0.5) \
                            .then_inc(sem("exp2"), 1)

                    def evac_QT2(t, u):
                        act.wait_ge(sem("qtr2"), t + 1)
                        after(act, sem("s2_done"), t - 1)
                        for i in range(CH2):
                            ins = a.activation(QT2[u][:, i * P:(i + 1) * P], C2[:, i // 3, (i % 3) * P:(i % 3 + 1) * P],
                                               ACT.Identity, bias=col(f"qb{i}"), scale=col(f"qg{i}"))
                        ins.then_inc(sem("QT2_ready"), 1)

                    def norm_rows(dst, src, rr, mv, ready, done, used):
                        def stage(t, u):
                            act.wait_ge(sem(ready), t + 1)
                            after(act, sem(used), t - 1)
                            ins = a.activation(dst[u].rearrange("p (k n) -> p k n", k=2), src, ACT.Identity,
                                               bias=mv[u][:, 0:1])
                            ins.then_inc(sem(done + "_c"), 1)
                            act.wait_ge(sem(done + "_c"), t + 1)
                            a.activation(dst[u], dst[u], ACT.Copy, scale=rr[u][:, 0:1]) \
                                .then_inc(sem(done), 1)
                        return stage

                    def evac_PT2(t, u):
                        act.wait_ge(sem("ptr2"), t + 1)
                        after(act, sem("ot2_done"), t - 1)
                        a.activation(PT[u][:, 0:INNER].rearrange("p (k n) -> p k n", k=2), C2, ACT.Copy) \
                            .then_inc(sem("PT2_ready"), 1)

                    def evac_V2(t, u):
                        act.wait_ge(sem("v2_done"), t + 1)
                        after(act, sem("ot2_done"), t - 1)
                        a.activation(Vs[u][:, :, :], A2, ACT.Copy).then_inc(sem("Vs_ready"), 1)

                    def evac_OT2(t, u):
                        act.wait_ge(sem("ot2_done"), t + 1)
                        after(act, sem("y2_done"), t - 1)
                        a.activation(OT2[u][:, :, :].rearrange("p (k i) n -> p k (i n)", k=2), B2, ACT.Copy).then_inc(sem("OT2_ready"), 1)

                    att2.run(act, [(stage_ctx("tab_g", "tab_b", "v2_done", 0), 0), (evac_QT2, 2), (expo, 3), (evac_hT(name, T2_ps, "vid_g", "vid_b"), 0),
                                   (norm_rows(qn, A2, qr, qmv, "qr_ready", "qn_ready", "qtr2"), 1),
                                   (norm_rows(kn, B2, kr, kmv, "kr_ready", "kn_ready", "ktr2"), 1),
                                   (evac_PT2, 3), (evac_V2, 1), (evac_OT2, 3)])
                if name == "f2":
                    def evac_bT(t, u):
                        act.wait_ge(sem("bt_done"), t + 1)
                        after(act, sem("yb_done"), t - 1)
                        a.activation(bitT[u][:, :], bank[:, 0, 0:64].bitcast(BF16), ACT.Copy).then_inc(sem("bT_ready"), 1)

                    bit.run(act, [(evac_bT, 1)])
                if name == "x3":
                    def expo(t, u):
                        act.wait_ge(sem("m3_ready"), 2 * (t + 1))
                        after(act, sem("pt3_done"), t - 1)
                        for b in range(PAIR):
                            half = slice(b * SEQ, (b + 1) * SEQ)
                            ins = a.activation(P3[u][half, half], bank[half, 1, half], ACT.Exp,
                                               bias=sm3[u][half, 0:1], accum_out=sm3[u][half, 1:2])
                            ins.then_inc(sem("exp3"), 1)

                    def sig(t, u):
                        act.wait_ge(sem("g3_done"), t + 1)
                        after(act, sem("x3_upd"), t - 1)
                        a.activation(th3[u], bank[:, 0, 0:P], ACT.Tanh, scale=0.5).then_inc(sem("th3"), 1)

                    def evac_PT3(t, u):
                        act.wait_ge(sem("pt3_done"), t + 1)
                        after(act, sem("r3_done"), t - 1)
                        a.activation(PT[u][:, 0:P], bank[:, 2, 0:P], ACT.Copy).then_inc(sem("PT3_ready"), 1)

                    def evac_rT(t, u):
                        act.wait_ge(sem("r3_done"), t + 1)
                        after(act, sem("l3_done"), t - 1)
                        a.activation(OT[u][:, :], bank[:, 3, 0:P], ACT.Copy).then_inc(sem("rT_ready"), 1)

                    def tanh_l(t, u):
                        act.wait_ge(sem("l3_done"), t + 1)
                        after(act, sem("x3_upd"), t - 1)
                        a.activation(hn3[u], bank[:, 4, 0:P], ACT.Tanh).then_inc(sem("hn3"), 1)

                    xl3.run(act, [(evac_hT(name, TO_ps), 0), (sig, 1), (expo, 1), (evac_PT3, 1), (evac_rT, 1), (tanh_l, 2)])
                if name in MOE:
                    affine = ("ln2_w", "ln2_b") if name == "m3" else (None, None)
                    pre.run(act, [(evac_hT(name, TO_ps, *affine), 0)])
                    n = MOE.index(name)
                    act.wait_ge(sem("gate_in"), n + 1)
                    if name == "f1":
                        a.activation(rt[:, :, :], rt[:, :, :], ACT.Exp).then_inc(sem("gate_exp"), 1)
                    else:
                        a.activation(wt[1][:, :], wt[1][:, :], ACT.Exp).then_inc(sem("gate_exp"), 1)
                    base, nb = BB[name], NBLK[name]

                    def evac_xbT(b, u):
                        act.wait_ge(sem("xbT1"), base + b + 1)
                        after(act, sem("h_done"), base + b - 1)
                        if name == "m3":
                            ins = a.activation(xbT[u], TO_ps, ACT.Identity, bias=col("ln2_b"), scale=col("ln2_w"))
                        else:
                            ins = a.activation(xbT[u], TO_ps, ACT.Copy)
                        ins.then_inc(sem("xbT_ready"), 1)

                    def hidden(b, u):
                        act.wait_ge(sem("h_done"), base + b + 1)
                        if name == "m3":
                            after(act, sem("g3_prod"), b - 1)
                            a.activation(G[u][:, 0:HID3], bank[:, u, 0:HID3], ACT.Silu).then_inc(sem("g_act"), 1)
                        else:
                            after(act, sem("gtr_done"), base + b - 1)
                            fn = ACT.Gelu if name == "f0" else ACT.Relu
                            a.activation(G[u][:, :], bank[:, u, :], fn).then_inc(sem("g_act"), 1)

                    def evac_y(b, u):
                        act.wait_ge(sem("yps_done"), base + b + 1)
                        after(act, sem(f"yb_out{u}"), 8 * (base + b - u))
                        a.activation(yb[u], bank[:, 4 + u, 0:C], ACT.Copy).then_inc(sem("yb_ready"), 1)

                    Ring(nb, 3).run(act, [(evac_xbT, 0), (hidden, 1), (evac_y, 3)])

        @block.tensor
        def _(pe):
            mm = nc.tensor.matmul
            pe.wait_ge(sem("pool_ready"), 1)
            pe.wait_ge(sem("vec_in"), 16 * 9)

            def t1(name, region):
                def stage(t, u):
                    pe.wait_ge(sem("hs_ready"), TB[name] + t + 1)
                    after(pe, sem("hT_ready"), TB[name] + t)
                    if name in ATT:
                        after(pe, sem("Vb_ready"), 2 * (ATT[name] + t - 1))
                    if name == "x2":
                        after(pe, sem("sub2"), t - 2)
                    nc.tensor.transpose(region, hs[u][:, :], ident[:, :]).then_inc(sem("t1_done"), 1)
                return stage

            for name in phases():
                phase_start(pe, name)
                if name == "ctx":
                    pre.run(pe, [(t1(name, TO_ps), 0)])
                if name in ATT:
                    base = ATT[name]
                    wq, wk, wv = {"x0": ("wq0", "wv0", "wv0"), "x1": ("wq1", "wk1", "wv1"), "a3": ("wq3", "wk3", "wv3")}[name]

                    def qkv(t, u):
                        src = hT if name == "a3" else cT
                        pe.wait_ge(sem("hT_ready"), TB[name] + upto(t + 2, NT))
                        after(pe, sem("Vb_ready"), 2 * (base + t))
                        mm(Q_ps, sq(wq), hT[u][:, :], start=True, stop=True)
                        if name != "a3":
                            pe.wait_ge(sem("cT_ready"), base + t + 1)
                        mm(K_ps, sq(wk), src[u][:, :], start=True, stop=True)
                        for b in range(PAIR):
                            for half in range(2):
                                ins = mm(V_ps[half * SEQ:(half + 1) * SEQ, b * P:(b + 1) * P],
                                         src[u][:, b * SEQ:(b + 1) * SEQ], sq(wv), start=True, stop=True)
                        ins.then_inc(sem("v_done"), 1)

                    def scores(t, u):
                        pe.wait_ge(sem("QT_ready"), base + t + 1)
                        pe.wait_ge(sem("Kb_ready"), base + t + 1)
                        after(pe, sem("sub_done"), base + t)
                        for g in range(GROUPS):
                            if name == "x1":
                                mm(S_att[:, g, :], pairsel[:, :],
                                   maskrow[:, bass.ds(t, 1), :].to_broadcast([PAIR, HPG, SEQ]), start=True, stop=True,
                                   skip_group_check=True)
                            if name == "a3":
                                mm(S_att[:, g, :], identb[:, :],
                                   causal[:, :].unsqueeze(1).to_broadcast([P, HPG, SEQ]), start=True, stop=True,
                                   skip_group_check=True)
                        for g in range(GROUPS):
                            rows32 = slice(32 * g, 32 * g + 32)
                            for b in range(PAIR):
                                half = slice(b * SEQ, (b + 1) * SEQ)
                                ins = mm(S_att[half, g, :], QT[u][rows32, half], Kb[u][rows32, :, half],
                                         start=name == "x0", stop=True, skip_group_check=name != "x0")
                        ins.then_inc(sem("s_done"), 1)

                    def transpose_P(t, u):
                        pe.wait_ge(sem("exp_done"), base + t + 1)
                        after(pe, sem("PT_ready"), base + t)
                        for j in range(HEADS // 2):
                            ins = nc.tensor.transpose(PT_ps[:, j * P:(j + 1) * P], Pr[u][:, j * P:(j + 1) * P], ident[:, :])
                        ins.then_inc(sem("pt_done"), 1)

                    def values(t, u):
                        pe.wait_ge(sem("PT_ready"), base + t + 1)
                        pe.wait_ge(sem("Vb_ready"), 2 * (base + t + 1))
                        after(pe, sem("O_ready"), 2 * (base + t))
                        out = O_ps.rearrange("p (b j n) -> p j b n", b=PAIR, j=HEADS // 2)
                        for j in range(HEADS // 2):
                            ins = mm(out[:, j, :, :], PT[u][:, j * P:(j + 1) * P],
                                     Vb[u][:, j, :, :, :].rearrange("p b h d -> p b (h d)"), start=True, stop=True)
                        ins.then_inc(sem("pv_done"), 1)

                    def transpose_O(t, u):
                        pe.wait_ge(sem("O_ready"), 2 * (base + t + 1))
                        nc.tensor.transpose(OY_ps, Oh[u][:, :, :].rearrange("p h d -> p (h d)"), ident[:, :]) \
                            .then_inc(sem("ot_done"), 1)

                    def project(t, u):
                        pe.wait_ge(sem("OT_ready"), PROJ[name] + t + 1)
                        i = {"x1": 1, "a3": 3}[name]
                        mm(OY_ps, OT[u][:, :], sq(f"wo{i}"), start=True, stop=False)
                        mm(OY_ps, ones[0:1, :], row(f"bo{i}"), start=False, stop=True).then_inc(sem("y_done"), 1)

                    proj = name in PROJ
                    att.run(pe, [(transpose_P, 3), (t1(name, TO_ps), 0)] + [(transpose_O, 4)] * proj + [(qkv, 1)]
                            + [(project, 4)] * proj + [(values, 3), (scores, 1)])
                if name == "x2":
                    pe.wait_ge(sem("w_in2"), 16 * 4)

                    def proj_Q(t, u):
                        pe.wait_ge(sem("hT_ready"), TB[name] + t + 1)
                        after(pe, sem("Vs_ready"), t)
                        for k in range(2):
                            ins = mm(A2[:, k, :], hT[u][:, :], wq2[:, k * 384:(k + 1) * 384], start=True, stop=True)
                        ins.then_inc(sem("q2_done"), 1)

                    def proj_K(t, u):
                        pe.wait_ge(sem("cT_ready"), 2 * NT + t + 1)
                        if not isinstance(t, int) or t >= 3:
                            pe.wait_ge(sem("x2_upd"), t - 2)
                        for k in range(2):
                            ins = mm(B2[:, k, :], cT[u][:, :], wk2[:, k * 384:(k + 1) * 384], start=True, stop=True)
                        ins.then_inc(sem("k2_done"), 1)

                    def proj_V(t, u):
                        pe.wait_ge(sem("qn_ready"), t + 1)
                        for b in range(PAIR):
                            for hf in range(2):
                                ins = mm(A2[hf * SEQ:(hf + 1) * SEQ, b, :], cT[u][:, b * SEQ:(b + 1) * SEQ],
                                         wv2[:, :].rearrange("c (m f n) -> c m f n", f=2, n=P)[:, :, hf, :],
                                         start=True, stop=True)
                        ins.then_inc(sem("v2_done"), 1)

                    def transpose_rows(src, ready, freed, done):
                        def stage(t, u):
                            pe.wait_ge(sem(ready), t + 1)
                            freed(t)
                            for i in range(CH2):
                                ins = nc.tensor.transpose(C2[:, i // 3, (i % 3) * P:(i % 3 + 1) * P],
                                                          src[u][:, i * P:(i + 1) * P], ident[:, :])
                            ins.then_inc(sem(done), 1)
                        return stage

                    def scores2(t, u):
                        pe.wait_ge(sem("pool_ready"), 1)
                        pe.wait_ge(sem("QT2_ready"), t + 1)
                        pe.wait_ge(sem("KT2_ready"), t + 1)
                        after(pe, sem("sub2"), t)
                        pe.wait_ge(sem("hT_ready"), TB[name] + upto(t + 3, NT))
                        for i in range(CH2):
                            for p in range(2):
                                for b in range(PAIR):
                                    half = slice(b * SEQ, (b + 1) * SEQ)
                                    hrow = slice(p * DH2, (p + 1) * DH2)
                                    tok = slice(i * P + b * SEQ, i * P + (b + 1) * SEQ)
                                    ins = mm(D2[half, p, i * SEQ:(i + 1) * SEQ], QT2[u][hrow, tok], KT2[u][hrow, tok],
                                             start=True, stop=True)
                        ins.then_inc(sem("s2_done"), 1)

                    def values2(t, u):
                        pe.wait_ge(sem("pool_ready"), 1)
                        pe.wait_ge(sem("PT2_ready"), t + 1)
                        pe.wait_ge(sem("Vs_ready"), t + 1)
                        pe.wait_ge(sem("kn_ready"), upto(t + 3, NT))
                        for i in range(CH2):
                            for p in range(2):
                                m, hf = i // 2, i % 2
                                for b in range(PAIR):
                                    krow = slice(hf * SEQ, (hf + 1) * SEQ)
                                    vcol = m * P + p * DH2
                                    pcol = (p * 3 + m) * P + b * SEQ
                                    ins = mm(B2[p * DH2:(p + 1) * DH2, i % 2, (i // 2) * P + b * SEQ:(i // 2) * P + (b + 1) * SEQ],
                                             Vs[u][krow, b, vcol:vcol + DH2], PT[u][krow, pcol:pcol + SEQ],
                                             start=True, stop=True)
                        ins.then_inc(sem("ot2_done"), 1)

                    def project2(t, u):
                        pe.wait_ge(sem("OT2_ready"), t + 1)
                        for i in range(CH2):
                            mm(Y2_ps, OT2[u][:, 3 * (i % 2) + i // 2, :], wo2[:, i, :], start=i == 0, stop=False)
                        mm(Y2_ps, ones[0:1, :], row("bo2"), start=False, stop=True).then_inc(sem("y2_done"), 1)

                    att2.run(pe, [
                        (project2, 4), (proj_Q, 1),
                        (transpose_rows(qn, "qn_ready", lambda t: after(pe, sem("PT2_ready"), t - 1), "qtr2"), 2),
                        (t1(name, T2_ps), 0), (proj_K, 1),
                        (transpose_rows(kn, "kn_ready", lambda t: pe.wait_ge(sem("QT2_ready"), t + 1), "ktr2"), 2),
                        (proj_V, 1), (scores2, 2),
                        (transpose_rows(Pr, "pn2", lambda t: pe.wait_ge(sem("KT2_ready"), upto(t + 2, NT)), "ptr2"), 3),
                        (values2, 3)])
                if name == "f2":
                    pe.wait_ge(sem("wabs"), 1)
                    mm(bank[:, 7, 0:1], ones[:, :], wstat[:, 0:1], start=True, stop=True).then_inc(sem("wsum"), 1)
                    pe.wait_ge(sem("wbit_ready"), 1)

                    def tb(t, u):
                        pe.wait_ge(sem("bitq_ready"), t + 1)
                        after(pe, sem("bT_ready"), t)
                        nc.tensor.transpose(bank[:, 0, 0:64].bitcast(BF16), bitq[u][:, :], identb[:, :]) \
                            .then_inc(sem("bt_done"), 1)

                    def yb_(t, u):
                        pe.wait_ge(sem("bT_ready"), t + 1)
                        after(pe, sem("xb_upd"), t)
                        mm(bank[:, 1, 0:C], bitT[u][:, :], wbit[:, :], start=True, stop=True).then_inc(sem("yb_done"), 1)

                    bit.run(pe, [(tb, 1), (yb_, 2)])
                if name == "x3":
                    def gate_scores(t, u):
                        pe.wait_ge(sem("hT_ready"), TB[name] + t + 1)
                        after(pe, sem("th3"), t)
                        mm(bank[:, 0, 0:P], hT[u][:, :], sq("w_gate"), start=True, stop=False)
                        mm(bank[:, 0, 0:P], ones[0:1, :], row("b_gate"), start=False, stop=True).then_inc(sem("g3_done"), 1)
                        after(pe, sem("exp3"), 2 * t)
                        mm(bank[:, 1, 0:P], hT[u][:, :], toks(ctxT, t), start=True, stop=True).then_inc(sem("s3_done"), 1)

                    def pt3(t, u):
                        pe.wait_ge(sem("pn3"), t + 1)
                        after(pe, sem("PT3_ready"), t)
                        nc.tensor.transpose(bank[:, 2, 0:P], P3[u][:, :], ident[:, :]).then_inc(sem("pt3_done"), 1)

                    def r3(t, u):
                        pe.wait_ge(sem("PT3_ready"), t + 1)
                        pe.wait_ge(sem("cs3_ready"), t + 1)
                        after(pe, sem("rT_ready"), t)
                        mm(bank[:, 3, 0:P], cT[u][:, :], PT[u][:, 0:P], start=True, stop=True).then_inc(sem("r3_done"), 1)

                    def l3(t, u):
                        pe.wait_ge(sem("rT_ready"), t + 1)
                        after(pe, sem("hn3"), t)
                        mm(bank[:, 4, 0:P], OT[u][:, :], sq("w_lin_r"), start=True, stop=False)
                        mm(bank[:, 4, 0:P], hT[u][:, :], sq("w_lin_h"), start=False, stop=False)
                        mm(bank[:, 4, 0:P], ones[0:1, :], row("b_lin"), start=False, stop=True).then_inc(sem("l3_done"), 1)

                    xl3.run(pe, [(l3, 2), (t1(name, TO_ps), 0), (gate_scores, 1), (pt3, 1), (r3, 1)])
                if name in MOE:
                    k = MOE.index(name)

                    def logits(t, u):
                        pe.wait_ge(sem("hT_ready"), TB[name] + t + 1)
                        after(pe, sem("lg_ready"), ROUTE[name] + t)
                        mm(L_ps, hT[u][:, :], rw[:, k, :], start=True, stop=True).then_inc(sem("lg_done"), 1)

                    pre.run(pe, [(t1(name, TO_ps), 0), (logits, 1)])
                    pe.wait_ge(sem("oh_ready"), k + 1)
                    ohf = ohs[:, :, :].rearrange("p t e -> p (t e)")
                    mm(bank[:, 0, 0:P], before[:, :], ohf, start=True, stop=True)
                    mm(bank[:, 1, 0:P], ones[:, :], ohf, start=True, stop=True).then_inc(sem("count_done"), 1)
                    pe.wait_ge(sem("slots_ready"), k + 1)
                    pe.wait_ge(sem("moe_w"), 16 * (18 if k < 2 else 28))
                    base, nb = BB[name], NBLK[name]
                    nj = (HJ if k < 2 else HID3 // P)

                    def expert(b, u):
                        if name == "f1":
                            return (b - u) * (nj * C // 2)
                        e = nc.tensor.value_load(blke[0:1, bass.ds(b, 1)], min_val=0, max_val=NE - 1)
                        return e * (nj * C)

                    def tblk(b, u):
                        pe.wait_ge(sem(f"xb_in{u}"), 8 * (base + b - u) + 16)
                        after(pe, sem("xbT_ready"), base + b)
                        nc.tensor.transpose(TO_ps, xb[u], ident[:, :]).then_inc(sem("xbT1"), 1)

                    def hid(b, u):
                        pe.wait_ge(sem("xbT_ready"), base + b + 1)
                        after(pe, sem("g_act"), base + b - 1)
                        if name == "m3":
                            after(pe, sem("g3_prod"), b - 1)
                        off = expert(b, u) * (HID // (nj * C))
                        mm(bank[:, u, :], xbT[u], w1[k][:, bass.ds(off, HID)], start=True, stop=True) \
                            .then_inc(sem("h_done"), 1)

                    def tg(b, u):
                        src = G3 if name == "m3" else G
                        pe.wait_ge(sem("g3_prod" if name == "m3" else "g_act"), (0 if name == "m3" else base) + b + 1)
                        after(pe, sem("GT_ready"), base + b - 1)
                        for j in range(nj):
                            ins = nc.tensor.transpose(bank[:, 2 + u, j * P:(j + 1) * P], src[u][:, j * P:(j + 1) * P],
                                                      ident[:, :])
                        ins.then_inc(sem("gtr_done"), 1)

                    def down(b, u):
                        pe.wait_ge(sem("GT_ready"), base + b + 1)
                        after(pe, sem("yb_ready"), base + b - 1)
                        off = expert(b, u)
                        for j in range(nj):
                            ins = mm(bank[:, 4 + u, 0:C], GT[u][:, j * P:(j + 1) * P], w2[k][:, bass.ds(off + j * C, C)],
                                     start=j == 0, stop=j == nj - 1)
                        ins.then_inc(sem("yps_done"), 1)

                    Ring(nb, 3).run(pe, [(tblk, 0), (tg, 2), (hid, 1), (down, 3)])

        @block.vector
        def _(dve):
            v = nc.vector
            chain = [0]

            def link(ins):
                chain[0] += 1
                ins.then_inc(sem("dve_chain"), 1)
                dve.wait_ge(sem("dve_chain"), chain[0])

            def stats(name, src):
                i, twice = LNI[name], dict(LNS)[name]
                with dve.Fori(0, NT) as t:
                    v.bn_stats(tile(st, t), tile(src, t)).then_inc(sem("bn_done"), 1)
                dve.wait_ge(sem("bn_done"), (i + 1) * NT)
                v.tensor_tensor(st_a[:, :], st[:, :, 1], st[:, :, 4], ALU.add).then_inc(sem("st_parts"), 1)
                v.tensor_tensor(st_b[:, :], st[:, :, 1], st[:, :, 4], ALU.subtract).then_inc(sem("st_parts"), 1)
                v.tensor_tensor(st_c[:, :], st[:, :, 2], st[:, :, 5], ALU.add).then_inc(sem("st_parts"), 1)
                dve.wait_ge(sem("st_parts"), 3 * (i + 1))
                link(v.tensor_scalar(mean[:, :], st_a[:, :], 0.5, None, ALU.mult))
                link(v.scalar_tensor_tensor(st_b[:, :], st_b[:, :], 0.25, st_b[:, :], ALU.mult, ALU.mult))
                link(v.scalar_tensor_tensor(var[:, :], st_c[:, :], 1.0 / C, st_b[:, :], ALU.mult, ALU.add))
                v.tensor_scalar(veps[:, :], var[:, :], LN_EPS, None, ALU.add).then_inc(sem("var_ready"), 1)
                dve.wait_ge(sem("rstd_ready"), POW[name] + 1)
                if twice:
                    link(v.tensor_copy(rs1[:, :], rs[:, :]))
                    link(v.tensor_tensor(st_a[:, :], var[:, :], rs1[:, :], ALU.mult))
                    link(v.tensor_tensor(st_b[:, :], st_a[:, :], rs1[:, :], ALU.mult))
                    v.tensor_scalar(veps[:, :], st_b[:, :], LN_EPS, None, ALU.add).then_inc(sem("var_ready"), 1)
                    dve.wait_ge(sem("rstd_ready"), POW[name] + 2)
                    link(v.tensor_tensor(rs[:, :], rs[:, :], rs1[:, :], ALU.mult))

            def norm(name, src, also=None):
                def stage(t, u):
                    after(dve, sem("t1_done"), TB[name] + t - 1)
                    if also:
                        after(dve, sem(also[0]), also[1] + t - 1)
                    v.tensor_scalar(hs[u][:, :], tile(src, t), at(mean, t), at(rs, t), ALU.subtract, ALU.mult) \
                        .then_inc(sem("hs_ready"), 1)
                return stage

            def gx(layer):
                return gates[:, layer:layer + 1]

            def gf(layer):
                return gates[:, 4 + layer:5 + layer]

            dve.wait_ge(sem("pool_ready"), 1)
            dve.wait_ge(sem("ctx_in"), 16)
            dve.wait_ge(sem("x_in"), 16)
            dve.wait_ge(sem("vec_in"), 16 * 9)
            link(v.tensor_copy(maskf[:, :, :].rearrange("b t s -> b (t s)"),
                               maskraw[:, :, :].rearrange("b t s -> b (t s)").bitcast(U8)))
            link(v.tensor_reduce(maskall[:, :], maskf[:, :, :], AX.X, ALU.min))
            link(v.tensor_tensor(maskf[:, :, 0], maskf[:, :, 0], maskall[:, :], ALU.subtract))
            link(v.tensor_scalar(maskrow[:, :, :], maskf[:, :, :], NEG, None, ALU.mult))
            dve.wait_ge(sem("gates_ready"), 1)

            for name in phases():
                phase_start(dve, name)
                src = {"ctx": ctxn, "m3": y3}.get(name, x)
                stats(name, src)
                if name == "ctx":
                    pre.run(dve, [(norm(name, src), 0)])
                    dve.wait_ge(sem("hT_ready"), NT)
                    v.engine_nop().then_inc(sem("phase_done"), 1)
                if name in ATT:
                    base = ATT[name]
                    bias_k = {"x0": "bk0", "x1": "bk1", "a3": None}[name]
                    bias_v = {"x0": 0, "x1": 1, "a3": None}[name]

                    def keys(t, u):
                        dve.wait_ge(sem("QT_ready"), base + t + 1)
                        after(dve, sem("s_done"), base + t - 1)
                        src_k = K_ps.unsqueeze(1).to_broadcast([P, HPG, P])
                        sel = headmask[:, :].unsqueeze(2).to_broadcast([P, HPG, P])
                        v.scalar_tensor_tensor(Kb[u][:, :, :], src_k, col(bias_k) if bias_k else 0.0, sel,
                                               ALU.add, ALU.mult).then_inc(sem("Kb_ready"), 1)

                    def vals(t, u):
                        dve.wait_ge(sem("QT_ready"), base + t + 1)
                        after(dve, sem("pv_done"), base + t - 1)
                        for half in range(2):
                            r = slice(half * SEQ, (half + 1) * SEQ)
                            src_v = V_ps[r, :].rearrange("p (b j h d) -> p j b h d", b=PAIR, h=2, d=HD)[:, :, :, half, :]
                            dst = Vb[u][r, :, :, half, 0:HD]
                            if bias_v is None:
                                ins = v.tensor_copy(dst, src_v)
                            else:
                                bb = bvB[r, bias_v, :].rearrange("p (j h d) -> p j h d", h=2, d=HD)[:, :, half, :]
                                ins = v.tensor_tensor(dst, src_v, bb.unsqueeze(2).to_broadcast([SEQ, HEADS // 2, PAIR, HD]),
                                                      ALU.add)
                            ins.then_inc(sem("Vb_ready"), 1)

                    def s4(u):
                        return S_att.rearrange("p g (h k) -> p g h k", h=HPG)

                    def row_max(t, u):
                        dve.wait_ge(sem("s_done"), base + t + 1)
                        v.tensor_reduce(mx[u][:, :].rearrange("p (g h) -> p g h", g=GROUPS), s4(u), AX.X, ALU.max) \
                            .then_inc(sem("mx_ready"), 1)

                    def subtract(t, u):
                        dve.wait_ge(sem("mx_ready"), base + t + 1)
                        after(dve, sem("pt_done"), base + t - 1)
                        mb = mx[u][:, :].rearrange("p (g h) -> p g h", g=GROUPS).unsqueeze(3) \
                            .to_broadcast([P, GROUPS, HPG, SEQ])
                        v.tensor_tensor(Pr[u][:, :].rearrange("p (g h k) -> p g h k", g=GROUPS, h=HPG), s4(u), mb,
                                        ALU.subtract).then_inc(sem("sub_done"), 1)

                    def normalise(t, u):
                        dve.wait_ge(sem("pv_done"), base + t + 1)
                        if name in PROJ:
                            after(dve, sem("ot_done"), PROJ[name] + t - 1)
                        o4 = O_ps.rearrange("p (b h n) -> p b h n", b=PAIR, n=HD + 1)
                        for b in range(PAIR):
                            r = slice(b * SEQ, (b + 1) * SEQ)
                            v.reciprocal(rinv[u][r, :], o4[r, b, :, HD]).then_inc(sem("rinv_ready"), 1)
                        dve.wait_ge(sem("rinv_ready"), 2 * (base + t + 1))
                        for b in range(PAIR):
                            r = slice(b * SEQ, (b + 1) * SEQ)
                            v.tensor_tensor(Oh[u][r, :, :], o4[r, b, :, 0:HD],
                                            rinv[u][r, :].unsqueeze(2).to_broadcast([SEQ, HEADS, HD]),
                                            ALU.mult).then_inc(sem("O_ready"), 1)

                    def update(t, u):
                        if name == "x0":
                            dve.wait_ge(sem("O_ready"), 2 * (base + t + 1))
                            v.scalar_tensor_tensor(tile(x, t), Oh[u][:, :, :].rearrange("p h d -> p (h d)"), gx(0),
                                                   tile(x, t), ALU.mult, ALU.add).then_inc(sem("x_upd"), 1)
                        else:
                            dve.wait_ge(sem("y_done"), PROJ[name] + t + 1)
                            dve.wait_ge(sem("pv_done"), base + upto(t + 2, NT))
                            if name == "x1":
                                v.scalar_tensor_tensor(tile(x, t), OY_ps, gx(1), tile(x, t), ALU.mult, ALU.add) \
                                    .then_inc(sem("x_upd"), 1)
                            else:
                                v.tensor_tensor(tile(y3, t), OY_ps, tile(y3, t), ALU.add).then_inc(sem("x_upd"), 1)

                    def keep_rows(t, u):
                        v.tensor_scalar(tile(y3, t), tile(x, t), at(mean, t), at(rs1, t), ALU.subtract, ALU.mult) \
                            .then_inc(sem("y3_kept"), 1)

                    def update3(t, u):
                        dve.wait_ge(sem("y3_kept"), t + 1)
                        update(t, u)

                    a3 = name == "a3"
                    att.run(dve, [(update3 if a3 else update, 5), (normalise, 4), (row_max, 2), (norm(name, src), 0)]
                            + [(keep_rows, 0)] * a3 + [(subtract, 2), (keys, 1), (vals, 1)])
                    dve.wait_ge(sem("x_upd"), base + NT)
                    v.engine_nop().then_inc(sem("phase_done"), 1)
                if name == "x2":
                    def bn_rows(ps, stt, mv, done, ready, var_sem):
                        def stage(t, u):
                            dve.wait_ge(sem(done), t + 1)
                            after(dve, sem(ready), t - 1)
                            for k in range(2):
                                v.bn_stats(stt[u][:, k, :], ps[:, k, :]).then_inc(sem(var_sem + "_c"), 1)
                            dve.wait_ge(sem(var_sem + "_c"), 4 * t + 2)
                            v.memset(aggr_gap[:, :], 0.0)
                            v.bn_aggr(mv[u][:, :], stt[u][:, :, :].rearrange("p k s -> p (k s)")) \
                                .then_inc(sem(var_sem + "_c"), 1)
                            dve.wait_ge(sem(var_sem + "_c"), 4 * t + 3)
                            v.tensor_scalar(mv[u][:, 0:1], mv[u][:, 0:1], -1.0, None, ALU.mult) \
                                .then_inc(sem(var_sem + "_c"), 1)
                            v.tensor_scalar(mv[u][:, 1:2], mv[u][:, 1:2], LN_EPS, None, ALU.add).then_inc(sem(var_sem), 1)
                            dve.wait_ge(sem(var_sem + "_c"), 4 * t + 4)
                        return stage

                    def keys2(t, u):
                        dve.wait_ge(sem("ktr2"), t + 1)
                        after(dve, sem("s2_done"), t - 1)
                        for i in range(CH2):
                            ins = v.tensor_scalar(KT2[u][:, i * P:(i + 1) * P], C2[:, i // 3, (i % 3) * P:(i % 3 + 1) * P],
                                                  col(f"kg{i}"), col(f"kb{i}"), ALU.mult, ALU.add)
                        ins.then_inc(sem("KT2_ready"), 1)

                    def s4b():
                        return D2.rearrange("p a (i k) -> p a i k", k=SEQ)

                    def row_max2(t, u):
                        dve.wait_ge(sem("s2_done"), t + 1)
                        v.tensor_reduce(mx[u][:, 0:H2].rearrange("p (a i) -> p a i", a=2), s4b(), AX.X, ALU.max) \
                            .then_inc(sem("mx2"), 1)
                        dve.wait_ge(sem("mx2"), t + 1)
                        after(dve, sem("ptr2"), t - 1)
                        mb = mx[u][:, 0:H2].rearrange("p (a i) -> p a i", a=2).unsqueeze(3).to_broadcast([P, 2, CH2, SEQ])
                        v.tensor_tensor(Pr[u][:, 0:INNER].rearrange("p (a i k) -> p a i k", a=2, i=CH2), s4b(), mb,
                                        ALU.subtract).then_inc(sem("sub2"), 1)

                    def sums2(t, u):
                        dve.wait_ge(sem("exp2"), t + 1)
                        v.tensor_reduce(mx[u][:, 0:H2], Pr[u][:, 0:INNER].rearrange("p (h k) -> p h k", h=H2), AX.X,
                                        ALU.add).then_inc(sem("sum2"), 1)
                        dve.wait_ge(sem("sum2"), t + 1)
                        after(dve, sem("pn2"), t - 1)
                        v.reciprocal(rinv[u][:, 0:H2], mx[u][:, 0:H2]).then_inc(sem("rinv2"), 1)

                    def update2(t, u):
                        dve.wait_ge(sem("y2_done"), t + 1)
                        v.scalar_tensor_tensor(tile(x, t), Y2_ps, gx(2), tile(x, t), ALU.mult, ALU.add) \
                            .then_inc(sem("x2_upd"), 1)

                    att2.run(dve, [(update2, 4), (row_max2, 3), (norm(name, src), 0),
                                  (bn_rows(A2, qst, qmv, "q2_done", "qn_ready", "qvar"), 1), (sums2, 3), (keys2, 2),
                                  (bn_rows(B2, kst, kmv, "k2_done", "kn_ready", "kvar"), 1)])
                    dve.wait_ge(sem("x2_upd"), NT)
                    v.engine_nop().then_inc(sem("phase_done"), 1)
                if name == "f2":
                    link(v.tensor_reduce(wstat[:, 0:1], sq("w_bitT"), AX.X, ALU.add, apply_absolute_value=True))
                    v.engine_nop().then_inc(sem("wabs"), 1)
                    dve.wait_ge(sem("wsum"), 1)
                    link(v.tensor_scalar(wstat[:, 1:2], bank[:, 7, 0:1], 1.0 / (C * C), BIT_EPS, ALU.mult, ALU.add))
                    link(v.reciprocal(wstat[:, 2:3], wstat[:, 1:2]))
                    link(v.tensor_scalar(wbtmp[:, :], sq("w_bitT"), wstat[:, 2:3], ROUND, ALU.mult, ALU.add))
                    link(v.tensor_scalar(wbtmp[:, :], wbtmp[:, :], ROUND, -1.0, ALU.subtract, ALU.max))
                    v.tensor_scalar(wbit[:, :], wbtmp[:, :], 1.0, None, ALU.min).then_inc(sem("wbit_ready"), 1)
                    link(v.scalar_tensor_tensor(wstat[:, 3:4], wstat[:, 1:2], 1.0 / 127.0, gf(2), ALU.mult, ALU.mult))

                    def normb(t, u):
                        v.tensor_scalar(hs[u][:, :], tile(x, t), at(mean, t), at(rs, t), ALU.subtract, ALU.mult) \
                            .then_inc(sem("bit_rows"), 1)

                    def quant(t, u):
                        c = sem("bit_chain")
                        dve.wait_ge(sem("bit_rows"), t + 1)
                        v.tensor_reduce(bits[u][:, 0:1], hs[u][:, :], AX.X, ALU.max, apply_absolute_value=True).then_inc(c, 1)
                        dve.wait_ge(c, 6 * t + 1)
                        v.tensor_scalar(bits[u][:, 1:2], bits[u][:, 0:1], BIT_EPS, None, ALU.add).then_inc(c, 1)
                        dve.wait_ge(c, 6 * t + 2)
                        v.reciprocal(bits[u][:, 2:3], bits[u][:, 1:2]).then_inc(c, 1)
                        v.tensor_tensor(bits[u][:, 3:4], bits[u][:, 1:2], wstat[:, 3:4], ALU.mult).then_inc(c, 1)
                        dve.wait_ge(c, 6 * t + 4)
                        v.tensor_scalar(hs[u][:, :], hs[u][:, :], bits[u][:, 2:3], 127.0, ALU.mult, ALU.mult).then_inc(c, 1)
                        dve.wait_ge(c, 6 * t + 5)
                        v.tensor_scalar(hs[u][:, :], hs[u][:, :], 127.0, ROUND, ALU.min, ALU.add).then_inc(c, 1)
                        dve.wait_ge(c, 6 * t + 6)
                        after(dve, sem("bt_done"), t - 1)
                        v.tensor_scalar(bitq[u][:, :], hs[u][:, :], ROUND, -128.0, ALU.subtract, ALU.max) \
                            .then_inc(sem("bitq_ready"), 1)
                        dve.wait_ge(sem("bitq_ready"), t + 1)

                    def updateb(t, u):
                        dve.wait_ge(sem("yb_done"), t + 1)
                        v.scalar_tensor_tensor(tile(x, t), bank[:, 1, 0:C], bits[u][:, 3:4], tile(x, t), ALU.mult,
                                               ALU.add).then_inc(sem("xb_upd"), 1)

                    bit.run(dve, [(normb, 0), (updateb, 3), (quant, 1)])
                    dve.wait_ge(sem("xb_upd"), NT)
                    v.engine_nop().then_inc(sem("phase_done"), 1)
                if name == "x3":
                    def max3(t, u):
                        dve.wait_ge(sem("s3_done"), t + 1)
                        after(dve, sem("exp3"), 2 * (t - 1))
                        for b in range(PAIR):
                            half = slice(b * SEQ, (b + 1) * SEQ)
                            v.tensor_reduce(sm3[u][half, 0:1], bank[half, 1, half], AX.X, ALU.max, negate=True) \
                                .then_inc(sem("m3_ready"), 1)

                    def norm3(t, u):
                        dve.wait_ge(sem("exp3"), 2 * (t + 1))
                        v.reciprocal(sm3[u][:, 2:3], sm3[u][:, 1:2]).then_inc(sem("r3inv"), 1)
                        dve.wait_ge(sem("r3inv"), t + 1)
                        v.tensor_scalar(P3[u][:, :], P3[u][:, :], sm3[u][:, 2:3], None, ALU.mult).then_inc(sem("pn3"), 1)

                    def update3x(t, u):
                        c = sem("x3_chain")
                        dve.wait_ge(sem("hn3"), t + 1)
                        dve.wait_ge(sem("hs_kept"), t + 1)
                        v.scalar_tensor_tensor(hn3[u], hn3[u], at(pw, t), tile(y3, t), ALU.mult, ALU.subtract) \
                            .then_inc(c, 1)
                        dve.wait_ge(sem("th3"), t + 1)
                        v.tensor_scalar(th3[u], th3[u], 0.5, 0.5, ALU.mult, ALU.add).then_inc(c, 1)
                        dve.wait_ge(c, 4 * t + 2)
                        v.tensor_tensor(tmp3[u], th3[u], hn3[u], ALU.mult).then_inc(c, 1)
                        dve.wait_ge(c, 4 * t + 3)
                        v.tensor_tensor(tmp3[u], tmp3[u], tile(y3, t), ALU.add).then_inc(c, 1)
                        dve.wait_ge(c, 4 * t + 4)
                        v.scalar_tensor_tensor(tile(x, t), tmp3[u], gx(3), tile(x, t), ALU.mult, ALU.add) \
                            .then_inc(sem("x3_upd"), 1)

                    xl3.run(dve, [(norm(name, src, ("hs_kept", 0)), 0), (update3x, 3), (max3, 1), (norm3, 1)])
                    dve.wait_ge(sem("x3_upd"), NT)
                    v.engine_nop().then_inc(sem("phase_done"), 1)
                if name in MOE:
                    k = MOE.index(name)

                    def take_logits(t, u):
                        dve.wait_ge(sem("lg_done"), ROUTE[name] + t + 1)
                        v.tensor_copy(tile(lg, t), L_ps).then_inc(sem("lg_ready"), 1)

                    pre.run(dve, [(norm(name, src, ("hn_kept", ROUTE[name])), 0), (take_logits, 2)])
                    dve.wait_ge(sem("lg_ready"), ROUTE[name] + NT)

                    def over_e(m):
                        return m.unsqueeze(2).to_broadcast([P, NT, NE])

                    def over_t(m):
                        return m.unsqueeze(1).to_broadcast([P, NT, NE])

                    def first_max(scores, best, onehot):
                        link(v.tensor_reduce(best[:, :], scores[:, :, :], AX.X, ALU.max))
                        link(v.tensor_tensor(rt[:, :, :], scores[:, :, :], over_e(best[:, :]), ALU.is_equal))
                        link(v.tensor_tensor(rt[:, :, :], rt[:, :, :], over_t(blk[:, 3, :]), ALU.mult))
                        link(v.tensor_reduce(rk[:, :], rt[:, :, :], AX.X, ALU.max))
                        link(v.tensor_tensor(onehot[:, :, :], over_t(blk[:, 3, :]), over_e(rk[:, :]), ALU.is_equal))

                    link(v.tensor_scalar(blk[:, 3, :], iota8[:, :], -1.0, float(NE), ALU.mult, ALU.add))
                    first_max(lg, rm[0], oh[0])
                    if KTOP[name] == 2:
                        link(v.scalar_tensor_tensor(lg2[:, :, :], oh[0][:, :, :], NEG, lg[:, :, :], ALU.mult, ALU.add))
                        first_max(lg2, rm[1], oh[1])
                        link(v.tensor_tensor(ohs[:, :, :], oh[0][:, :, :], oh[1][:, :, :], ALU.add))
                        v.engine_nop().then_inc(sem("oh_ready"), 1)
                        v.tensor_tensor(wt[1][:, :], rm[1][:, :], rm[0][:, :], ALU.subtract).then_inc(sem("gate_in"), 1)
                    else:
                        link(v.tensor_copy(ohs[:, :, :], oh[0][:, :, :]))
                        v.engine_nop().then_inc(sem("oh_ready"), 1)
                        v.tensor_tensor(rt[:, :, :], lg[:, :, :], over_e(rm[0][:, :]), ALU.subtract) \
                            .then_inc(sem("gate_in"), 1)
                    gate = gf({"f0": 0, "f1": 1, "m3": 3}[name])
                    dve.wait_ge(sem("gate_exp"), k + 1)
                    if KTOP[name] == 2:
                        link(v.tensor_scalar(rk[:, :], wt[1][:, :], 1.0, None, ALU.add))
                        link(v.reciprocal(rk[:, :], rk[:, :]))
                        link(v.tensor_scalar(wt[0][:, :], rk[:, :], gate, None, ALU.mult))
                        link(v.tensor_tensor(wt[1][:, :], wt[1][:, :], wt[0][:, :], ALU.mult))
                    else:
                        link(v.tensor_reduce(rk[:, :], rt[:, :, :], AX.X, ALU.add))
                        link(v.reciprocal(rk[:, :], rk[:, :]))
                        link(v.tensor_scalar(wt[0][:, :], rk[:, :], gate, None, ALU.mult))
                    dve.wait_ge(sem("count_done"), k + 1)
                    cnt = bank[:, 0, 0:P].rearrange("p (t e) -> p t e", e=NE)
                    link(v.tensor_copy(rn[:, :, :], bank[:, 1, 0:P].rearrange("p (t e) -> p e t", e=NE)))
                    link(v.tensor_tensor_scan(rscan[:, :, :].rearrange("p e t -> p (e t)"),
                                              runmask[:, :, :].rearrange("p e t -> p (e t)"),
                                              rn[:, :, :].rearrange("p e t -> p (e t)"), 0.0, ALU.mult, ALU.add))
                    link(v.tensor_tensor(rn[:, :, :], rscan[:, :, :], rn[:, :, :], ALU.subtract))
                    link(v.tensor_tensor(rt[:, :, :], cnt, rn[:, :, :].rearrange("p e t -> p t e"), ALU.add))
                    if KTOP[name] == 2:
                        link(v.tensor_scalar(blki[:, :], rscan[:, :, NT - 1], float(P - 1), None, ALU.add))
                        link(v.tensor_scalar(blki[:, :], blki[:, :], 7, None, ALU.arith_shift_right))
                        link(v.tensor_copy(blk[:, 0, :], blki[:, :]))
                        link(v.tensor_tensor_scan(blk[:, 1, :], ones[:, 0:NE], blk[:, 0, :], 0.0, ALU.mult, ALU.add))
                        link(v.tensor_tensor(blk[:, 2, :], blk[:, 1, :], blk[:, 0, :], ALU.subtract))
                        link(v.tensor_scalar(blk[:, 2, :], blk[:, 2, :], float(P), None, ALU.mult))
                        link(v.tensor_tensor(rt[:, :, :], rt[:, :, :], over_t(blk[:, 2, :]), ALU.add))
                        link(v.tensor_tensor(cmpb[:, :, :],
                                             iotab[:, :].unsqueeze(2).to_broadcast([1, TOP2_BLOCKS, NE]),
                                             blk[0:1, 1, :].unsqueeze(1).to_broadcast([1, TOP2_BLOCKS, NE]), ALU.is_ge))
                        link(v.tensor_reduce(blkef[:, :], cmpb[:, :, :], AX.X, ALU.add))
                        link(v.tensor_scalar(blke[:, :], blkef[:, :], float(NE - 1), None, ALU.min))
                    for j in range(KTOP[name]):
                        link(v.tensor_tensor(lg2[:, :, :], rt[:, :, :], oh[j][:, :, :], ALU.mult))
                        link(v.tensor_reduce(slotf[:, :], lg2[:, :, :], AX.X, ALU.add))
                        if KTOP[name] == 1:
                            link(v.tensor_scalar(keep[:, :], slotf[:, :], float(CAP), None, ALU.is_lt))
                            link(v.tensor_tensor(wt[0][:, :], wt[0][:, :], keep[:, :], ALU.mult))
                            link(v.tensor_tensor(lg2[:, :, :], over_t(iota8[:, :]), oh[0][:, :, :], ALU.mult))
                            link(v.tensor_reduce(rk[:, :], lg2[:, :, :], AX.X, ALU.add))
                            link(v.scalar_tensor_tensor(slotf[:, :], rk[:, :], float(CAP), slotf[:, :], ALU.mult, ALU.add))
                            link(v.tensor_scalar(rk[:, :], tokid[:, :], float(NE * CAP), None, ALU.add))
                            link(v.tensor_tensor(slotf[:, :], slotf[:, :], rk[:, :], ALU.subtract))
                            link(v.tensor_tensor(slotf[:, :], slotf[:, :], keep[:, :], ALU.mult))
                            link(v.tensor_tensor(slotf[:, :], slotf[:, :], rk[:, :], ALU.add))
                        link(v.tensor_copy(slot[j][:, :], slotf[:, :]))
                    v.engine_nop().then_inc(sem("slots_ready"), 1)
                    base, nb = BB[name], NBLK[name]

                    def product3(b, u):
                        dve.wait_ge(sem("g_act"), base + b + 1)
                        after(dve, sem("gtr_done"), base + b - 1)
                        v.tensor_tensor(G3[u][:, :], G[u][:, 0:HID3], bank[:, u, HID3:HID], ALU.mult) \
                            .then_inc(sem("g3_prod"), 1)

                    def evac_GT(b, u):
                        dve.wait_ge(sem("gtr_done"), base + b + 1)
                        after(dve, sem("yps_done"), base + b - 1)
                        w = HID if k < 2 else HID3
                        v.tensor_copy(GT[u][:, 0:w], bank[:, 2 + u, 0:w]).then_inc(sem("GT_ready"), 1)

                    Ring(nb, 3).run(dve, ([(product3, 1)] if name == "m3" else []) + [(evac_GT, 2)])
                    if name == "m3":
                        dve.wait_ge(sem("t1_done"), TB[name] + NT)
                        link(v.scalar_tensor_tensor(x[:, :, :], y3[:, :, :], gate, x[:, :, :], ALU.mult, ALU.add))
                    second = second_rows(name)
                    tiles = 4
                    for q in range(NT // tiles):
                        dve.wait_ge(sem(f"gathered{q}"), 16 * tiles * (SC[name] + KTOP[name]))
                        for j in range(KTOP[name]):
                            rowsj = hn if j == 0 else second
                            with dve.Fori(q * tiles, (q + 1) * tiles) as t:
                                v.scalar_tensor_tensor(tile(x, t), tile(rowsj, t), at(wt[j], t), tile(x, t), ALU.mult,
                                                       ALU.add).then_inc(sem("comb_done"), 1)
                            dve.wait_ge(sem("comb_done"), NT * SC[name] + tiles * (KTOP[name] * q + j + 1))
                    v.engine_nop().then_inc(sem("phase_done"), 1)


def kernel(**inputs):
    import concourse.bacc as bacc
    from concourse.bass_utils import run_bass_kernel_spmd

    a = {k: np.asarray(v) for k, v in inputs.items()}
    xi, ci = a["x"].reshape(TOK, C), a["ctx_1024"].reshape(TOK, C)
    vec = {"bq0": "L0_xattn_Wk_b", "bk0": "L0_xattn_Wv_b", "qn_w1": "L1_xattn_qn_w", "qn_b1": "L1_xattn_qn_b",
           "cn_w1": "L1_xattn_cn_w", "cn_b1": "L1_xattn_cn_b", "bq1": "L1_xattn_bq", "bk1": "L1_xattn_bk",
           "tab_g": "L2_xattn_tab_g", "tab_b": "L2_xattn_tab_b", "vid_g": "L2_xattn_vid_g", "vid_b": "L2_xattn_vid_b",
           "ln1_w": "L3_ffn_ln1_scale", "ln1_b": "L3_ffn_ln1_shift", "ln2_w": "L3_ffn_ln2_scale",
           "ln2_b": "L3_ffn_ln2_shift"}
    columns = [a[vec[n]] for n in COLS[:16]]
    for name in ("q_g", "q_b", "k_g", "k_b"):
        columns += list(a[f"L2_xattn_{name}"].reshape(CH2, P))
    rowv = [a[n] for n in ("L0_xattn_Wv_b", "L1_xattn_bv", "L1_xattn_bo", "L2_xattn_bo", "L3_xattn_b_gate",
                           "L3_xattn_b_lin", "L3_ffn_bo")]
    square = [a["L0_xattn_Wk_w"].T, a["L0_xattn_Wv_w"].T] + [a[f"L1_xattn_{n}"].T for n in ("Wq", "Wk", "Wv", "Wo")] + [
        a["L3_xattn_W_gate"], a["L3_xattn_W_lin"][:C], a["L3_xattn_W_lin"][C:]] + [
            a[f"L3_ffn_{n}"] for n in ("wq", "wk", "wv", "wo")] + [a["L2_ffn_weight"].T]
    arrays = {
        "x": xi, "ctx": ci, "ctxT": ci.T, "cols": np.stack(columns, 1), "rows": np.stack(rowv), "wsq": np.stack(square),
        "g": np.concatenate([a["g_xattn"], a["g_ffn"]]).reshape(1, 8), "pw": a["fside_BxS_0"].reshape(NT, P).T,
        "mask": a["mask_BxS2_bk0"].view(np.int32),
        "rw": np.stack([a["L0_ffn_router_w"].T, a["L1_ffn_wg"], a["L3_ffn_gate_w"]]),
        "wq2": a["L2_xattn_Wq"], "wk2": a["L2_xattn_Wk"], "wv2": a["L2_xattn_Wv"], "wo2": a["L2_xattn_Wo"],
        "w1_0": a["L0_ffn_w1"], "w1_1": a["L1_ffn_w1"], "w1_2": a["L3_ffn_w1"], "w1_3": a["L3_ffn_w2"],
        "w2_0": a["L0_ffn_w2"], "w2_1": a["L1_ffn_w2"], "w2_2": a["L3_ffn_w3"],
    }
    nc = bacc.Bacc("TRN2", target_bir_lowering=False, num_devices=1)
    feed, io = {}, {}
    for name, arr in arrays.items():
        arr = np.ascontiguousarray(arr)
        feed[f"in_{name}"] = arr
        io[name] = nc.dram_tensor(f"in_{name}", arr.shape, mybir.dt.from_np(arr.dtype), kind="ExternalInput").ap()
    io["out"] = nc.dram_tensor("out_dram", (TOK, C), F32, kind="ExternalOutput").ap()
    build(nc, io)
    r = run_bass_kernel_spmd(nc, [feed], core_ids=[0])
    return r.results[0]["out_dram"].reshape(B, SEQ, C)
```

```python
from contextlib import ExitStack

import numpy as np

import concourse.bass as bass
from concourse import mybir

F32 = mybir.dt.float32
BF16 = mybir.dt.bfloat16
I32 = mybir.dt.int32
U32 = mybir.dt.uint32
U8 = mybir.dt.uint8
ALU = mybir.AluOpType
ACT = mybir.ActivationFunctionType
AX = mybir.AxisListType

P = 128
C = 128
B, SEQ = 32, 64
TOK = B * SEQ
NT = TOK // P
PAIR = P // SEQ
HEADS, HD = 16, 8
GROUPS, HPG = 4, 4
H2, DH2 = 12, 64
INNER = H2 * DH2
CH2 = INNER // P
NE, HID = 8, 512
HJ = HID // P
HID3 = 256
CAP = TOK // NE
TOP2_BLOCKS = 2 * TOK // P + NE
TOP1_BLOCKS = TOK // P
ROWS = TOP2_BLOCKS * P
LN_EPS = 1e-5
BIT_EPS = 1e-8
NEG = -1e30
ROUND = 1.5 * 2.0 ** 23

COLS = ["bq0", "bk0", "qn_w1", "qn_b1", "cn_w1", "cn_b1", "bq1", "bk1", "tab_g", "tab_b", "vid_g", "vid_b",
        "ln1_w", "ln1_b", "ln2_w", "ln2_b"] + [f"qg{i}" for i in range(CH2)] + [f"qb{i}" for i in range(CH2)] + [
            f"kg{i}" for i in range(CH2)] + [f"kb{i}" for i in range(CH2)]
COL = {n: i for i, n in enumerate(COLS)}
ROWV = ["bv0", "bv1", "bo1", "bo2", "b_gate", "b_lin", "bo3"]
ROW = {n: i for i, n in enumerate(ROWV)}
SQ = ["wq0", "wv0", "wq1", "wk1", "wv1", "wo1", "w_gate", "w_lin_r", "w_lin_h", "wq3", "wk3", "wv3", "wo3", "w_bitT"]
SQI = {n: i for i, n in enumerate(SQ)}

VEC_LOADS = 11

N_PHASES = 8


class Ring:

    def __init__(self, n, lag):
        self.n, self.lag = n, lag

    def run(self, eng, stages):
        first = self.lag + 2 + self.lag % 2
        last = self.n - self.n % 2

        def step(i, par):
            for stage, lag in stages:
                t = i - lag
                if isinstance(i, int) and not 0 <= t < self.n:
                    continue
                stage(t, (par - lag) % 2)

        for i in range(min(first, self.n + self.lag)):
            step(i, i % 2)
        if last > first:
            with eng.Fori(first // 2, last // 2) as pair:
                for par in range(2):
                    step(pair * 2 + par, par)
        for i in range(max(first, last), self.n + self.lag):
            step(i, i % 2)


def upto(v, most):
    return min(v, most) if isinstance(v, int) else v


def build(nc, io):
    with ExitStack() as ctx:
        def sb(name, shape, dt=F32):
            return ctx.enter_context(nc.sbuf_tensor(name, shape, dt))

        def two(name, shape, dt=F32):
            return [sb(f"{name}{u}", shape, dt) for u in range(2)]

        sems = {}

        def sem(name):
            if name not in sems:
                sems[name] = ctx.enter_context(nc.semaphore(name))
            return sems[name]

        x = sb("x", [P, NT, C])
        y3 = sb("y3", [P, NT, C])
        hn = sb("hn", [P, NT, C])
        ctxn = sb("ctxn", [P, NT, C])
        ctxT = sb("ctxT", [P, TOK])
        zT = sb("zT", [P, TOK])
        wsq = sb("wsq", [P, len(SQ), P])
        cols = sb("cols", [P, len(COLS)])
        rows = sb("rows", [1, len(ROWV), P])
        bvB = sb("bvB", [P, 2, GROUPS, PAIR, HPG * HD])
        wq2 = sb("wq2", [P, INNER])
        wk2 = sb("wk2", [P, INNER])
        wv2 = sb("wv2", [P, INNER])
        wo2 = sb("wo2", [P, CH2, P])
        rw = sb("rw", [P, 3, NE])
        w1 = [sb(f"w1_{n}", [P, NE * HID]) for n in range(2)]
        w2 = [sb(f"w2_{n}", [P, NE * HJ * C]) for n in range(2)]
        w1, w2 = w1 + w1[:1], w2 + w2[:1]
        pw = sb("pw", [P, NT])
        gates_raw = sb("gates_raw", [P, 8])
        gates = sb("gates", [P, 8])
        maskraw = sb("maskraw", [PAIR, NT, SEQ // 4], I32)
        maskf = sb("maskf", [PAIR, NT, SEQ])
        maskall = sb("maskall", [PAIR, NT])
        maskrow = sb("maskrow", [PAIR, NT, SEQ], BF16)

        ident = sb("ident", [P, P])
        identb = sb("identb", [P, P], BF16)
        pairsel = sb("pairsel", [PAIR, P], BF16)
        causal = sb("causal", [P, SEQ], BF16)
        headmask = sb("headmask", [P, HPG])
        ones = sb("ones", [P, P])
        before = sb("before", [P, P])
        powm = sb("powm", [P, NT])
        iota8 = sb("iota8", [P, NE])
        iotab = sb("iotab", [1, TOP2_BLOCKS])
        runmask = sb("runmask", [P, NE, NT])
        tokid = sb("tokid", [P, NT])
        zero_rows = hn[:, 0:NT // 2, :].rearrange("p t c -> p (t c)")

        st = sb("st", [P, NT, 6])
        st_a = sb("st_a", [P, NT])
        st_b = sb("st_b", [P, NT])
        st_c = sb("st_c", [P, NT])
        mean = sb("mean", [P, NT])
        var = sb("var", [P, NT])
        veps = sb("veps", [P, NT])
        rs = sb("rs", [P, NT])
        rs1 = sb("rs1", [P, NT])
        meanc = sb("meanc", [P, NT])
        rsc = sb("rsc", [P, NT])

        hs = two("hs", [P, C])
        hT = two("hT", [P, P])
        cT = two("cT", [P, P])
        QT = two("QT", [P, P])
        Kb = two("Kb", [P, HPG, P])
        Vb = two("Vb", [P, GROUPS * PAIR, 4, 2, HD])
        headsum = sb("headsum", [P, 2, 2, 2, HD])
        Pr = two("Pr", [P, HEADS * SEQ])
        PT = two("PT", [P, HEADS * SEQ])
        mx = two("mx", [P, HEADS])
        rinv = two("rinv", [P, HEADS])
        OT = two("OT", [P, P])
        qn = [hn[:, :, :].rearrange("p t c -> p (t c)")[:, u * INNER:(u + 1) * INNER] for u in range(2)]
        kn = [y3[:, :, :].rearrange("p t c -> p (t c)")[:, u * INNER:(u + 1) * INNER] for u in range(2)]
        QT2 = two("QT2", [P, INNER])
        rsum = [QT2[u][:, 0:P] for u in range(2)]
        KT2 = two("KT2", [P, INNER])
        Vs = two("Vs", [P, PAIR, INNER // 2])
        OT2 = two("OT2", [P, CH2, P])
        qst = two("qst", [P, 2, 6])
        kst = two("kst", [P, 2, 6])
        qmv = two("qmv", [P, 2])
        kmv = two("kmv", [P, 2])
        qr = two("qr", [P, 1])
        kr = two("kr", [P, 1])
        cV2 = [Kb[u][:, 0, :] for u in range(2)]
        P3 = two("P3", [P, P])
        sm3 = two("sm3", [P, 4])
        th3, hn3, tmp3 = [[hn[:, 2 * i + u, :] for u in range(2)] for i in range(3)]
        bitq = two("bitq", [P, P], BF16)
        bitT = two("bitT", [P, P], BF16)
        bits = two("bits", [P, 4])
        aggr_gap = sb("aggr_gap", [P, 1])
        wbit = sb("wbit", [P, P], BF16)
        wbtmp = sb("wbtmp", [P, P])
        wstat = sb("wstat", [P, 4])

        route_parts = [Kb[u][:, i, :] for u in range(2) for i in range(HPG)]
        lg, lg2, rt, ohs, *oh = [m.rearrange("p (t e) -> p t e", e=NE) for m in route_parts[:6]]
        rn, rscan = [m.rearrange("p (e t) -> p e t", e=NE) for m in route_parts[6:]]
        rm = [sb(f"rm{k}", [P, NT]) for k in range(2)]
        rk = sb("rk", [P, NT])
        blk = sb("blk", [P, 4, NE])
        blki = sb("blki", [P, NE], I32)
        slotf = sb("slotf", [P, NT])
        keep = sb("keep", [P, NT])
        slot = [sb(f"slot{k}", [P, NT], U32) for k in range(2)]
        wt = [sb(f"wt{k}", [P, NT]) for k in range(2)]
        cmpb = sb("cmpb", [1, TOP2_BLOCKS, NE])
        blkef = sb("blkef", [1, TOP2_BLOCKS])
        blke = sb("blke", [1, TOP2_BLOCKS], I32)
        xb = [QT2[u][:, 0:C] for u in range(2)]
        xbT = [QT2[u][:, C:2 * C] for u in range(2)]
        G = [Pr[u][:, 0:HID] for u in range(2)]
        G3 = [Pr[u][:, HID:HID + HID3] for u in range(2)]
        GT = [PT[u][:, 0:HID] for u in range(2)]
        yb = [QT2[u][:, 2 * C:3 * C] for u in range(2)]

        rows_in = nc.dram_tensor("rows_in", (ROWS, C), F32).ap()
        rows_out = nc.dram_tensor("rows_out", (ROWS, C), F32).ap()

        bank = ctx.enter_context(nc.psum_tensor("bank", [P, 8, 512], F32))
        flat = bank[:, :, :].rearrange("p b n -> p (b n)")
        block = ctx.enter_context(nc.Block())

        def sq(name):
            return wsq[:, SQI[name], :]

        def col(name):
            return cols[:, COL[name]:COL[name] + 1]

        def row(name):
            return rows[0:1, ROW[name], :]

        def tile(buf, t):
            return buf[:, bass.ds(t, 1), :].rearrange("p a c -> p (a c)")

        def at(buf, t):
            return buf[:, bass.ds(t, 1)]

        def toks(buf, t):
            return buf[:, bass.ds(t * P, P)]

        def after(eng, s, n):
            if not isinstance(n, int) or n > 0:
                eng.wait_ge(s, n)

        LNS = [("x0", False), ("ctx", False), ("f0", False), ("x1", True), ("f1", False), ("x2", True), ("f2", False),
               ("x3", False), ("a3", True), ("m3", False)]
        POW = {}
        n = 0
        for name, twice in LNS:
            POW[name] = n
            n += 2 if twice else 1
        LNI = {name: i for i, (name, _) in enumerate(LNS)}
        LOOPS = ["x0", "f0", "ctx", "x1", "f1", "x2", "x3", "a3", "m3"]
        TB = {name: NT * i for i, name in enumerate(LOOPS)}
        ATT = {"x0": 0, "x1": NT, "a3": 2 * NT}
        MOE = ["f0", "f1", "m3"]
        ROUTE = {"f0": 0, "f1": NT, "m3": 2 * NT}
        NBLK = {"f0": TOP2_BLOCKS, "f1": TOP1_BLOCKS, "m3": TOP2_BLOCKS}
        BB = {"f0": 0, "f1": TOP2_BLOCKS, "m3": TOP2_BLOCKS + TOP1_BLOCKS}
        KTOP = {"f0": 2, "f1": 1, "m3": 2}
        SC = {"f0": 0, "f1": 2, "m3": 3}

        HT_READER = {"x2": ("q2_done", 0), "x3": ("l3_done", 0)}
        HT_READER.update({n: ("v_done", c) for n, c in ATT.items()})
        HT_READER.update({n: ("lg_done", c) for n, c in ROUTE.items()})

        PH = ["x0", "f0", "x1", "f1", "x2", "f2", "x3", "a3", "m3"]
        PHI = {n: i for i, n in enumerate(PH)}

        def phases():
            return PH[:N_PHASES + 1] if N_PHASES >= 8 else PH[:N_PHASES]

        def phase_start(eng, name):
            if PHI[name]:
                eng.wait_ge(sem("phase_done"), PHI[name])

        def second_rows(name):
            return ctxn if name == "m3" else y3

        att = Ring(NT, 4)
        att2 = Ring(NT, 5)
        pre = Ring(NT, 3)
        xl3 = Ring(NT, 3)
        bit = Ring(NT, 3)

        S_att = bank[:, 0:GROUPS, 0:256]
        PT_ps = flat[:, 4 * 512:6 * 512]
        TO_ps = bank[:, 6, 0:128]
        Q_ps = bank[:, 6, 0:128]
        K_ps = bank[:, 6, 128:256]
        V_ps = bank[:, 6, 256:512]
        O_ps = bank[:, 7, 0:128]
        sum_ps = bank[:, 7, 128:256]
        OY_ps = bank[:, 7, 256:384]
        L_ps = bank[:, 7, 0:NE]
        A2 = bank[:, 0:2, 0:384]
        B2 = bank[:, 2:4, 0:384]
        C2 = bank[:, 4:6, 0:384]
        D2 = bank[:, 6:8, 0:384]
        T2_ps = bank[:, 6, 384:512]
        Y2_ps = bank[:, 7, 384:512]

        @block.sync
        def _(sp):
            sp.dma_start(x[:, :, :], io["x"].rearrange("(t p) c -> p t c", p=P)).then_inc(sem("x_in"), 16)
            sp.dma_start(ctxn[:, :, :], io["ctx"].rearrange("(t p) c -> p t c", p=P)).then_inc(sem("ctx_in"), 16)
            sp.dma_start(cols[:, :], io["cols"]).then_inc(sem("vec_in"), 16)
            sp.dma_start(wsq[:, :, :], io["wsq"].rearrange("n p c -> p n c")).then_inc(sem("vec_in"), 16)
            sp.dma_start(rows[0:1, :, :], io["rows"].rearrange("(a n) c -> a n c", a=1)).then_inc(sem("vec_in"), 16)
            for layer in range(2):
                for b in range(PAIR):
                    sp.dma_start(bvB[:, layer, :, b, :], io["rows"][layer:layer + 1, :].rearrange("a (m f) -> a m f", m=GROUPS)
                                 .to_broadcast([P, GROUPS, HPG * HD])).then_inc(sem("vec_in"), 16)
            sp.dma_start(gates_raw[:, :], io["g"].to_broadcast([P, 8])).then_inc(sem("vec_in"), 16)
            sp.dma_start(pw[:, :], io["pw"]).then_inc(sem("vec_in"), 16)
            sp.dma_start(maskraw[:, :, :], io["mask"].rearrange("(t b) s -> b t s", b=PAIR)).then_inc(sem("vec_in"), 16)
            sp.dma_start(rw[:, :, :], io["rw"].rearrange("n p e -> p n e")).then_inc(sem("vec_in"), 16)
            sp.dma_start(ctxT[:, :], io["ctxT"]).then_inc(sem("ctxT_in"), 16)
            for name, buf in (("wq2", wq2), ("wk2", wk2), ("wv2", wv2)):
                sp.dma_start(buf[:, :], io[name]).then_inc(sem("w_in2"), 16)
            sp.dma_start(wo2[:, :, :], io["wo2"].rearrange("(i p) c -> p i c", p=P)).then_inc(sem("w_in2"), 16)

            def expert_weights(k):
                w1v = w1[k][:, :].rearrange("p (e h) -> p e h", e=NE)
                if k < 2:
                    sp.dma_start(w1v, io[f"w1_{k}"].rearrange("e c h -> c e h")).then_inc(sem("moe_w"), 16)
                else:
                    sp.dma_start(w1v[:, :, 0:HID3], io["w1_2"].rearrange("e c h -> c e h")).then_inc(sem("moe_w"), 16)
                    sp.dma_start(w1v[:, :, HID3:HID], io["w1_3"].rearrange("e c h -> c e h")).then_inc(sem("moe_w"), 16)
                n = io[f"w2_{k}"].shape[1] // P
                for e in range(NE):
                    sp.dma_start(w2[k][:, e * n * C:(e + 1) * n * C].rearrange("p (j c) -> p j c", c=C),
                                 io[f"w2_{k}"][e].rearrange("(j p) c -> p j c", p=P)).then_inc(sem("moe_w"), 16)

            expert_weights(0)
            expert_weights(1)
            sp.wait_ge(sem("zeros"), 1)
            zr = rows_in.rearrange("(p n) c -> p (n c)", p=P)
            for k in range(ROWS * C // P // 1024):
                sp.dma_start(zr[:, k * 1024:(k + 1) * 1024], zero_rows).then_inc(sem("rows_zeroed"), 16)

            for name in phases():
                if name not in MOE:
                    continue
                base, nb = BB[name], NBLK[name]
                sp.wait_ge(sem("scattered"), 16 * NT * (SC[name] + KTOP[name]))

                def load(b, u):
                    after(sp, sem("xbT1"), base + b - 1)
                    sp.dma_start(xb[u], rows_in[bass.ds(b * P, P), :]).then_inc(sem(f"xb_in{u}"), 16)

                def store(b, u):
                    sp.wait_ge(sem("yb_ready"), base + b + 1)
                    sp.dma_start(rows_out[bass.ds(b * P, P), :], yb[u]).then_inc(sem(f"yb_out{u}"), 16)

                Ring(nb, 4).run(sp, [(load, 0), (store, 4)])
                if name == "f0":
                    sp.wait_ge(sem("phase_done"), PHI[name] + 1)
                    expert_weights(2)

            sp.wait_ge(sem("phase_done"), len(phases()))
            sp.dma_start(io["out"].rearrange("(t p) c -> p t c", p=P), x[:, :, :]).then_inc(sem("out_done"), 16)
            sp.wait_ge(sem("out_done"), 16)

        @block.gpsimd
        def _(pool):
            g = nc.gpsimd
            chain = [0]

            def link(ins):
                chain[0] += 1
                ins.then_inc(sem("pool_chain"), 1)
                pool.wait_ge(sem("pool_chain"), chain[0])

            def select(out, fill, base, pattern, mult, op=ALU.not_equal):
                link(g.affine_select(out=out, in_=out, compare_op=op, fill=fill, base=base, pattern=pattern,
                                     channel_multiplier=mult))

            link(g.memset(ident[:, :], 0.0))
            select(ident[:, :], 1.0, 0, [[-1, P]], 1)
            link(g.tensor_copy(identb[:, :], ident[:, :]))
            link(g.memset(powm[:, :], -0.5))
            link(g.memset(ones[:, :], 1.0))
            link(g.memset(headmask[:, :], 0.0))
            for grp in range(GROUPS):
                link(g.memset(before[:, 0:HPG], 1.0))
                select(before[:, 0:HPG], 0.0, -32 * grp, [[-8, HPG]], 1, ALU.is_ge)
                select(before[:, 0:HPG], 0.0, 32 * grp + 7, [[8, HPG]], -1, ALU.is_ge)
                link(g.tensor_tensor(headmask[:, :], headmask[:, :], before[:, 0:HPG], ALU.add))
            link(g.memset(pairsel[:, :], 1.0))
            select(pairsel[:, :].rearrange("b (c q) -> b c q", c=PAIR), 0.0, 0, [[-1, PAIR], [0, SEQ]], 1, ALU.is_equal)
            link(g.memset(causal[:, :], 0.0))
            select(causal[0:SEQ, :], NEG, 0, [[-1, SEQ]], 1, ALU.is_ge)
            select(causal[SEQ:P, :], NEG, 0, [[-1, SEQ]], 1, ALU.is_ge)
            link(g.memset(before[:, :], 1.0))
            select(before[:, :], 0.0, 0, [[1, P]], -1, ALU.is_gt)
            link(g.iota(slot[0][:, 0:NE].bitcast(I32), pattern=[[1, NE]], base=0, channel_multiplier=0))
            link(g.tensor_copy(iota8[:, :], slot[0][:, 0:NE].bitcast(I32)))
            link(g.iota(blke[:, :], pattern=[[1, TOP2_BLOCKS]], base=0, channel_multiplier=0))
            link(g.tensor_copy(iotab[:, :], blke[:, :]))
            link(g.iota(slot[1][:, :].bitcast(I32), pattern=[[P, NT]], base=0, channel_multiplier=1))
            link(g.tensor_copy(tokid[:, :], slot[1][:, :].bitcast(I32)))
            link(g.memset(runmask[:, :, :], 1.0))
            link(g.memset(runmask[:, :, 0:1], 0.0))
            for u in range(2):
                link(g.memset(Vb[u][:, :, :, :, :], 0.0))
                link(g.memset(P3[u][:, :], 0.0))
            link(g.memset(headsum[:, :, :, :, :], 0.0))
            for half in range(2):
                for r in range(2):
                    link(g.memset(headsum[half * SEQ:(half + 1) * SEQ, r, r, half, :], 1.0))
            link(g.memset(zero_rows, 0.0))
            g.engine_nop().then_inc(sem("zeros"), 1)
            g.engine_nop().then_inc(sem("pool_ready"), 2)

            def powers(name, count):
                for k in range(count):
                    pool.wait_ge(sem("var_ready"), POW[name] + k + 1)
                    g.tensor_tensor((rsc if name == "ctx" else rs)[:, :], veps[:, :], powm[:, :], ALU.pow) \
                        .then_inc(sem("rstd_ready"), 1)

            for name in phases():
                phase_start(pool, name)
                powers(name, 2 if dict(LNS)[name] else 1)
                if name == "x0":
                    powers("ctx", 1)
                if name == "x0":
                    pool.wait_ge(sem("ctxT_in"), 16)

                    def stage(t, u):
                        after(pool, sem("v_done"), ATT[name] + t - 1)
                        g.tensor_copy(cT[u][:, :], toks(ctxT, t)).then_inc(sem("cT_ready"), 1)

                    att.run(pool, [(stage, 0)])
                if name == "x2":
                    def pow_rows(mv, rr, var, ready):
                        def stage(t, u):
                            pool.wait_ge(sem(var), t + 1)
                            g.tensor_tensor(rr[u][:, :], mv[u][:, 1:2], powm[:, 0:1], ALU.pow).then_inc(sem(ready + "_c"), 1)
                            pool.wait_ge(sem(ready + "_c"), t + 1)
                            g.tensor_tensor(mv[u][:, 0:1], mv[u][:, 0:1], rr[u][:, :], ALU.mult).then_inc(sem(ready), 1)
                        return stage

                    def stage_keys(t, u):
                        after(pool, sem("k2_done"), t - 1)
                        g.tensor_copy(cT[u][:, :], toks(zT, t)).then_inc(sem("cT_ready"), 1)

                    def stage_values(t, u):
                        after(pool, sem("v2_done"), t - 1)
                        g.tensor_copy(cV2[u], toks(zT, t)).then_inc(sem("cV2_ready"), 1)

                    def pnorm(t, u):
                        pool.wait_ge(sem("rinv2"), t + 1)
                        pv = Pr[u][:, 0:INNER].rearrange("p (h k) -> p h k", h=H2)
                        g.tensor_tensor(pv, pv, rinv[u][:, 0:H2].unsqueeze(2).to_broadcast([P, H2, SEQ]),
                                        ALU.mult).then_inc(sem("pn2"), 1)

                    pool.wait_ge(sem("z_scaled"), 1)
                    att2.run(pool, [(pow_rows(qmv, qr, "qvar", "qr_ready"), 1), (pow_rows(kmv, kr, "kvar", "kr_ready"), 1),
                                    (stage_keys, 0), (stage_values, 2), (pnorm, 3)])
                if name == "x3":
                    def keep_ctx(t, u):
                        after(pool, sem("r3_done"), t - 1)
                        g.tensor_copy(cT[u][:, :], tile(ctxn, t)).then_inc(sem("cs3_ready"), 1)

                    def keep_h(t, u):
                        pool.wait_ge(sem("hs_ready"), TB[name] + t + 1)
                        g.tensor_copy(tile(y3, t), hs[u][:, :]).then_inc(sem("hs_kept"), 1)

                    xl3.run(pool, [(keep_ctx, 0), (keep_h, 0)])
                if name in MOE:
                    def keep_h(t, u):
                        pool.wait_ge(sem("hs_ready"), TB[name] + t + 1)
                        g.tensor_copy(tile(hn, t), hs[u][:, :]).then_inc(sem("hn_kept"), 1)

                    if name == "f0":
                        pool.wait_ge(sem("rows_zeroed"), 16 * (ROWS * C // P // 1024))
                    pre.run(pool, [(keep_h, 0)])
                    pool.wait_ge(sem("hn_kept"), ROUTE[name] + NT)
                    pool.wait_ge(sem("slots_ready"), MOE.index(name) + 1)
                    for t in range(NT):
                        for k in range(KTOP[name]):
                            g.indirect_dma_start(rows_in[:, :], bass.IndirectOffsetOnAxis(ap=slot[k][:, t:t + 1], axis=0),
                                                 hn[:, t, :], None).then_inc(sem("scattered"), 16)
                    nb, before_b = NBLK[name], BB[name]
                    for u in range(2):
                        pool.wait_ge(sem(f"yb_out{u}"), 16 * (before_b + nb) // 2)
                    for t in range(NT):
                        for k in range(KTOP[name]):
                            g.indirect_dma_start((hn if k == 0 else second_rows(name))[:, t, :], None, rows_out[:, :],
                                                 bass.IndirectOffsetOnAxis(ap=slot[k][:, t:t + 1], axis=0)) \
                                .then_inc(sem(f"gathered{t // 4}"), 16)

        @block.scalar
        def _(act):
            a = nc.scalar
            act.wait_ge(sem("vec_in"), 16 * VEC_LOADS)
            a.activation(gates[:, :], gates_raw[:, :], ACT.Tanh).then_inc(sem("gates_ready"), 1)

            def evac_hT(name, region, w=None, b=None):
                def stage(t, u):
                    act.wait_ge(sem("t1_done"), TB[name] + t + 1)
                    after(act, sem(HT_READER[name][0]), HT_READER[name][1] + t - 1)
                    if w:
                        ins = a.activation(hT[u][:, :], region, ACT.Identity, bias=col(b), scale=col(w))
                    else:
                        ins = a.activation(hT[u][:, :], region, ACT.Copy)
                    ins.then_inc(sem("hT_ready"), 1)
                return stage

            def stage_ctx(scale, shift, used, used_before):
                def stage(t, u):
                    after(act, sem(used), used_before + t - 1)
                    a.activation(cT[u][:, :], toks(zT, t), ACT.Identity, bias=col(shift), scale=col(scale)) \
                        .then_inc(sem("cT_ready"), 1)
                return stage

            for name in phases():
                phase_start(act, name)
                if name in ATT:
                    base = ATT[name]
                    affine = {"x0": (None, None), "x1": ("qn_w1", "qn_b1"), "a3": ("ln1_w", "ln1_b")}[name]
                    bias_q = {"x0": "bq0", "x1": "bq1", "a3": None}[name]

                    def evac_Q(t, u):
                        act.wait_ge(sem("v_done"), base + t + 1)
                        after(act, sem("s_done"), base + t - 1)
                        if bias_q:
                            ins = a.activation(QT[u][:, :], Q_ps, ACT.Identity, bias=col(bias_q))
                        else:
                            ins = a.activation(QT[u][:, :], Q_ps, ACT.Copy)
                        ins.then_inc(sem("QT_ready"), 1)

                    def expo(t, u):
                        act.wait_ge(sem("sub_done"), base + t + 1)
                        a.activation(Pr[u][:, :], Pr[u][:, :], ACT.Exp, scale=float(HD) ** -0.5) \
                            .then_inc(sem("exp_done"), 1)

                    def evac_PT(t, u):
                        act.wait_ge(sem("pt_done"), base + t + 1)
                        after(act, sem("pv_done"), base + t - 1)
                        a.activation(PT[u][:, :], PT_ps, ACT.Copy).then_inc(sem("PT_ready"), 1)

                    own_ctx = [(stage_ctx("cn_w1", "cn_b1", "v_done", base), 0)] if name == "x1" else []
                    att.run(act, [(evac_PT, 3), (evac_Q, 1), (expo, 2), (evac_hT(name, TO_ps, *affine), 0)] + own_ctx)
                if name == "x2":
                    a.activation(zT[:, :], zT[:, :], ACT.Identity, bias=col("tab_b"), scale=col("tab_g")) \
                        .then_inc(sem("z_scaled"), 1)

                    def expo(t, u):
                        act.wait_ge(sem("sub2"), t + 1)
                        a.activation(Pr[u][:, 0:INNER], Pr[u][:, 0:INNER], ACT.Exp, scale=float(DH2) ** -0.5) \
                            .then_inc(sem("exp2"), 1)

                    def scaled_rows(dst, done, gain, shift, ready):
                        def stage(t, u):
                            act.wait_ge(sem(done), t + 1)
                            after(act, sem("s2_done"), t - 1)
                            for i in range(CH2 // 2):
                                ins = a.activation(dst[u][:, i * P:(i + 1) * P], C2[:, 0, i * P:(i + 1) * P],
                                                   ACT.Identity, bias=col(f"{shift}{i}"), scale=col(f"{gain}{i}"))
                            ins.then_inc(sem(ready), 1)
                        return stage

                    def norm_rows(dst, src, rr, mv, ready, done, used):
                        def stage(t, u):
                            act.wait_ge(sem(ready), t + 1)
                            after(act, sem(used), t - 1)
                            a.activation(dst[u].rearrange("p (k n) -> p k n", k=2), src, ACT.Identity,
                                         bias=mv[u][:, 0:1], scale=rr[u][:, 0:1]).then_inc(sem(done), 1)
                        return stage

                    def evac_PT2(t, u):
                        act.wait_ge(sem("ptr2"), t + 1)
                        after(act, sem("ot2_done"), t - 1)
                        a.activation(PT[u][:, 0:INNER].rearrange("p (k n) -> p k n", k=2), C2, ACT.Copy) \
                            .then_inc(sem("PT2_ready"), 1)

                    def evac_V2(t, u):
                        act.wait_ge(sem("v2_done"), t + 1)
                        after(act, sem("ot2_done"), t - 1)
                        a.activation(Vs[u][:, :, :], A2, ACT.Copy).then_inc(sem("Vs_ready"), 1)

                    def evac_OT2(t, u):
                        act.wait_ge(sem("ot2_done"), t + 1)
                        after(act, sem("y2_done"), t - 1)
                        a.activation(OT2[u][:, :, :].rearrange("p (k i) n -> p k (i n)", k=2), B2, ACT.Copy).then_inc(sem("OT2_ready"), 1)

                    att2.run(act, [(scaled_rows(KT2, "ktr2", "kg", "kb", "KT2_first"), 2),
                                   (norm_rows(qn, A2, qr, qmv, "qr_ready", "qn_ready", "qtr2"), 1),
                                   (norm_rows(kn, B2, kr, kmv, "kr_ready", "kn_ready", "ktr2"), 1),
                                   (evac_PT2, 4), (expo, 3), (evac_V2, 3), (evac_hT(name, T2_ps, "vid_g", "vid_b"), 0),
                                   (evac_OT2, 4), (scaled_rows(QT2, "qtr2", "qg", "qb", "QT2_first"), 1)])
                if name == "f2":
                    def evac_bT(t, u):
                        act.wait_ge(sem("bt_done"), t + 1)
                        after(act, sem("yb_done"), t - 1)
                        a.activation(bitT[u][:, :], bank[:, 0, 0:64].bitcast(BF16), ACT.Copy).then_inc(sem("bT_ready"), 1)

                    bit.run(act, [(evac_bT, 1)])
                if name == "x3":
                    def expo(t, u):
                        act.wait_ge(sem("m3_ready"), 2 * (t + 1))
                        after(act, sem("pt3_done"), t - 1)
                        for b in range(PAIR):
                            half = slice(b * SEQ, (b + 1) * SEQ)
                            ins = a.activation(P3[u][half, half], bank[half, 1, half], ACT.Exp,
                                               bias=sm3[u][half, 0:1], accum_out=sm3[u][half, 1:2])
                            ins.then_inc(sem("exp3"), 1)

                    def sig(t, u):
                        act.wait_ge(sem("g3_done"), t + 1)
                        after(act, sem("x3_upd"), t - 1)
                        a.activation(th3[u], bank[:, 0, 0:P], ACT.Tanh, scale=0.5).then_inc(sem("th3"), 1)

                    def evac_PT3(t, u):
                        act.wait_ge(sem("pt3_done"), t + 1)
                        after(act, sem("r3_done"), t - 1)
                        a.activation(PT[u][:, 0:P], bank[:, 2, 0:P], ACT.Copy).then_inc(sem("PT3_ready"), 1)

                    def evac_rT(t, u):
                        act.wait_ge(sem("r3_done"), t + 1)
                        after(act, sem("l3_done"), t - 1)
                        a.activation(OT[u][:, :], bank[:, 3, 0:P], ACT.Copy).then_inc(sem("rT_ready"), 1)

                    def tanh_l(t, u):
                        act.wait_ge(sem("l3_done"), t + 1)
                        after(act, sem("x3_upd"), t - 1)
                        a.activation(hn3[u], bank[:, 4, 0:P], ACT.Tanh).then_inc(sem("hn3"), 1)

                    xl3.run(act, [(evac_hT(name, TO_ps), 0), (sig, 1), (expo, 1), (evac_PT3, 1), (evac_rT, 1), (tanh_l, 2)])
                if name in MOE:
                    affine = ("ln2_w", "ln2_b") if name == "m3" else (None, None)
                    pre.run(act, [(evac_hT(name, TO_ps, *affine), 0)])
                    n = MOE.index(name)

                    def evac_z(t, u):
                        act.wait_ge(sem("t1_done"), TB["ctx"] + t + 1)
                        a.activation(toks(zT, t), TO_ps, ACT.Copy).then_inc(sem("hT_ready"), 1)

                    act.wait_ge(sem("gate_in"), n + 1)
                    if name == "f1":
                        a.activation(rt[:, :, :], rt[:, :, :], ACT.Exp).then_inc(sem("gate_exp"), 1)
                    else:
                        a.activation(wt[1][:, :], wt[1][:, :], ACT.Exp).then_inc(sem("gate_exp"), 1)
                    if name == "f0":
                        pre.run(act, [(evac_z, 0)])
                    base, nb = BB[name], NBLK[name]

                    def evac_xbT(b, u):
                        act.wait_ge(sem("xbT1"), base + b + 1)
                        after(act, sem("h_done"), base + b - 1)
                        if name == "m3":
                            ins = a.activation(xbT[u], TO_ps, ACT.Identity, bias=col("ln2_b"), scale=col("ln2_w"))
                        else:
                            ins = a.activation(xbT[u], TO_ps, ACT.Copy)
                        ins.then_inc(sem("xbT_ready"), 1)

                    def hidden(b, u):
                        act.wait_ge(sem("h_done"), base + b + 1)
                        if name == "m3":
                            after(act, sem("g3_prod"), b - 1)
                            a.activation(G[u][:, 0:HID3], bank[:, u, 0:HID3], ACT.Silu).then_inc(sem("g_act"), 1)
                        else:
                            after(act, sem("gtr_done"), base + b - 1)
                            fn = ACT.Gelu if name == "f0" else ACT.Relu
                            a.activation(G[u][:, :], bank[:, u, :], fn).then_inc(sem("g_act"), 1)

                    def evac_y(b, u):
                        act.wait_ge(sem("yps_done"), base + b + 1)
                        after(act, sem(f"yb_out{u}"), 8 * (base + b - u))
                        a.activation(yb[u], bank[:, 4 + u, 0:C], ACT.Copy).then_inc(sem("yb_ready"), 1)

                    Ring(nb, 3).run(act, [(evac_xbT, 0), (hidden, 1), (evac_y, 3)])

        @block.tensor
        def _(pe):
            mm = nc.tensor.matmul
            pe.wait_ge(sem("pool_ready"), 1)
            pe.wait_ge(sem("vec_in"), 16 * VEC_LOADS)

            def t1(name, region):
                def stage(t, u):
                    pe.wait_ge(sem("hs_ready"), TB[name] + t + 1)
                    after(pe, sem("hT_ready"), TB[name] + t)
                    if name in ATT:
                        after(pe, sem("Vb_ready"), 2 * (ATT[name] + t))
                    if name == "x2":
                        after(pe, sem("sub2"), t - 2)
                    nc.tensor.transpose(region, hs[u][:, :], ident[:, :]).then_inc(sem("t1_done"), 1)
                return stage

            for name in phases():
                phase_start(pe, name)
                if name in ATT:
                    base = ATT[name]
                    wq, wk, wv = {"x0": ("wq0", "wv0", "wv0"), "x1": ("wq1", "wk1", "wv1"), "a3": ("wq3", "wk3", "wv3")}[name]

                    def qkv(t, u):
                        src = hT if name == "a3" else cT
                        pe.wait_ge(sem("hT_ready"), TB[name] + t + 1)
                        mm(Q_ps, sq(wq), hT[u][:, :], start=True, stop=True)
                        if name != "a3":
                            pe.wait_ge(sem("cT_ready"), base + t + 1)
                        mm(K_ps, sq(wk), src[u][:, :], start=True, stop=True)
                        for b in range(PAIR):
                            for half in range(2):
                                v_out = V_ps[half * SEQ:(half + 1) * SEQ, :].rearrange("p (m b f) -> p b m f", b=PAIR, m=GROUPS)
                                ins = mm(v_out[:, b, :, :],
                                         src[u][:, b * SEQ:(b + 1) * SEQ], sq(wv), start=True, stop=True)
                        ins.then_inc(sem("v_done"), 1)

                    def scores(g):
                        def stage(t, u):
                            if g == 0:
                                pe.wait_ge(sem("QT_ready"), base + t + 1)
                                pe.wait_ge(sem("Kb_ready"), base + t + 1)
                                after(pe, sem("sub_done"), base + t)
                            if name == "x1":
                                mm(S_att[:, g, :], pairsel[:, :],
                                   maskrow[:, bass.ds(t, 1), :].to_broadcast([PAIR, HPG, SEQ]), start=True, stop=True,
                                   skip_group_check=True)
                            if name == "a3":
                                mm(S_att[:, g, :], identb[:, :],
                                   causal[:, :].unsqueeze(1).to_broadcast([P, HPG, SEQ]), start=True, stop=True,
                                   skip_group_check=True)
                            rows32 = slice(32 * g, 32 * g + 32)
                            for b in range(PAIR):
                                half = slice(b * SEQ, (b + 1) * SEQ)
                                ins = mm(S_att[half, g, :], QT[u][rows32, half], Kb[u][rows32, :, half],
                                         start=name == "x0", stop=True, skip_group_check=name != "x0")
                            if g == GROUPS - 1:
                                ins.then_inc(sem("s_done"), 1)
                        return stage

                    def transpose_P(g):
                        def stage(t, u):
                            if g == 0:
                                pe.wait_ge(sem("exp_done"), base + t + 1)
                                after(pe, sem("PT_ready"), base + t)
                            for j in (2 * g, 2 * g + 1):
                                ins = nc.tensor.transpose(PT_ps[:, j * P:(j + 1) * P], Pr[u][:, j * P:(j + 1) * P],
                                                          ident[:, :])
                            if g == GROUPS - 1:
                                ins.then_inc(sem("pt_done"), 1)
                        return stage

                    def values(t, u):
                        pe.wait_ge(sem("PT_ready"), base + t + 1)
                        pe.wait_ge(sem("Vb_ready"), 2 * (base + t + 1))
                        after(pe, sem("O_ready"), base + t)
                        for r in range(2):
                            for m in range(GROUPS):
                                f32 = slice(32 * m, 32 * m + 32)
                                mm(sum_ps[f32, :], headsum[:, r, :, :, :].rearrange("p q h d -> p (q h d)"),
                                   PT[u][:, (2 * m + r) * P:(2 * m + r + 1) * P], start=r == 0, stop=r == 1,
                                   skip_group_check=True)
                        for b in range(PAIR):
                            for r in range(2):
                                for m in range(GROUPS):
                                    f32 = slice(32 * m, 32 * m + 32)
                                    col0 = (2 * m + r) * P + b * SEQ
                                    ins = mm(O_ps[f32, b * SEQ:(b + 1) * SEQ],
                                             Vb[u][:, 2 * m + b, 2 * r:2 * r + 2, :, :].rearrange("p q h d -> p (q h d)"),
                                             PT[u][:, col0:col0 + SEQ], start=r == 0, stop=r == 1, skip_group_check=True)
                        ins.then_inc(sem("pv_done"), 1)

                    def project(t, u):
                        pe.wait_ge(sem("O_ready"), base + t + 1)
                        if name == "x0":
                            nc.tensor.transpose(OY_ps, OT[u][:, :], ident[:, :]).then_inc(sem("y_done"), 1)
                            return
                        i = {"x1": 1, "a3": 3}[name]
                        mm(OY_ps, OT[u][:, :], sq(f"wo{i}"), start=True, stop=False)
                        mm(OY_ps, ones[0:1, :], row(f"bo{i}"), start=False, stop=True).then_inc(sem("y_done"), 1)

                    att.run(pe, [(qkv, 1), (values, 3), (scores(0), 1), (scores(1), 1), (transpose_P(0), 2),
                                 (t1(name, TO_ps), 0), (scores(2), 1), (transpose_P(1), 2), (transpose_P(2), 2),
                                 (scores(3), 1), (project, 3), (transpose_P(3), 2)])
                if name == "x2":
                    pe.wait_ge(sem("w_in2"), 16 * 4)

                    def both(rows, n):
                        after(pe, sem(rows + "_first"), n)
                        after(pe, sem(rows + "_second"), n)

                    def proj_Q(t, u):
                        pe.wait_ge(sem("hT_ready"), TB[name] + t + 1)
                        after(pe, sem("Vs_ready"), t - 2)
                        for k in range(2):
                            ins = mm(A2[:, k, :], hT[u][:, :], wq2[:, k * 384:(k + 1) * 384], start=True, stop=True)
                        ins.then_inc(sem("q2_done"), 1)

                    def proj_K(t, u):
                        pe.wait_ge(sem("cT_ready"), 2 * NT + t + 1)
                        after(pe, sem("OT2_ready"), t - 3)
                        for k in range(2):
                            ins = mm(B2[:, k, :], cT[u][:, :], wk2[:, k * 384:(k + 1) * 384], start=True, stop=True)
                        ins.then_inc(sem("k2_done"), 1)

                    def proj_V(t, u):
                        pe.wait_ge(sem("cV2_ready"), t + 1)
                        pe.wait_ge(sem("qn_ready"), upto(t + 3, NT))
                        for b in range(PAIR):
                            for hf in range(2):
                                ins = mm(A2[hf * SEQ:(hf + 1) * SEQ, b, :], cV2[u][:, b * SEQ:(b + 1) * SEQ],
                                         wv2[:, :].rearrange("c (m f n) -> c m f n", f=2, n=P)[:, :, hf, :],
                                         start=True, stop=True)
                        ins.then_inc(sem("v2_done"), 1)

                    def transpose_rows(src, ready, freed, done):
                        def stage(t, u):
                            pe.wait_ge(sem(ready), t + 1)
                            freed(t)
                            for i in range(CH2):
                                ins = nc.tensor.transpose(C2[:, i // 3, (i % 3) * P:(i % 3 + 1) * P],
                                                          src[u][:, i * P:(i + 1) * P], ident[:, :])
                            ins.then_inc(sem(done), 1)
                        return stage

                    def await_scores2(t, u):
                        both("KT2", t + 1)
                        after(pe, sem("sub2"), t)
                        pe.wait_ge(sem("hT_ready"), TB[name] + upto(t + 3, NT))
                        after(pe, sem("x2_upd"), t - 1)

                    def scores2(t, u):
                        for i in range(CH2):
                            for p in range(2):
                                for b in range(PAIR):
                                    half = slice(b * SEQ, (b + 1) * SEQ)
                                    hrow = slice(p * DH2, (p + 1) * DH2)
                                    tok = slice(i * P + b * SEQ, i * P + (b + 1) * SEQ)
                                    ins = mm(D2[half, p, i * SEQ:(i + 1) * SEQ], QT2[u][hrow, tok], KT2[u][hrow, tok],
                                             start=True, stop=True)
                        ins.then_inc(sem("s2_done"), 1)

                    def values2(t, u):
                        pe.wait_ge(sem("pool_ready"), 1)
                        pe.wait_ge(sem("PT2_ready"), t + 1)
                        pe.wait_ge(sem("Vs_ready"), t + 1)
                        pe.wait_ge(sem("kn_ready"), upto(t + 4, NT))
                        for i in range(CH2):
                            for p in range(2):
                                m, hf = i // 2, i % 2
                                for b in range(PAIR):
                                    krow = slice(hf * SEQ, (hf + 1) * SEQ)
                                    vcol = m * P + p * DH2
                                    pcol = (p * 3 + m) * P + b * SEQ
                                    ins = mm(B2[p * DH2:(p + 1) * DH2, i % 2, (i // 2) * P + b * SEQ:(i // 2) * P + (b + 1) * SEQ],
                                             Vs[u][krow, b, vcol:vcol + DH2], PT[u][krow, pcol:pcol + SEQ],
                                             start=True, stop=True)
                        ins.then_inc(sem("ot2_done"), 1)

                    def project2(t, u):
                        pe.wait_ge(sem("OT2_ready"), t + 1)
                        pe.wait_ge(sem("sub2"), upto(t + 2, NT))
                        after(pe, sem("x2_upd"), t)
                        for i in range(CH2):
                            mm(Y2_ps, OT2[u][:, 3 * (i % 2) + i // 2, :], wo2[:, i, :], start=i == 0, stop=False)
                        mm(Y2_ps, ones[0:1, :], row("bo2"), start=False, stop=True).then_inc(sem("y2_done"), 1)

                    def rows_free(t):
                        both("KT2", t)
                        after(pe, sem("PT2_ready"), t - 2)

                    att2.run(pe, [
                        (project2, 5), (proj_Q, 1), (proj_K, 1), (await_scores2, 3),
                        (transpose_rows(kn, "kn_ready", lambda t: both("QT2", t + 1), "ktr2"), 2),
                        (scores2, 3),
                        (transpose_rows(Pr, "pn2", lambda t: both("KT2", upto(t + 3, NT)), "ptr2"), 4),
                        (proj_V, 3), (t1(name, T2_ps), 0), (values2, 4),
                        (transpose_rows(qn, "qn_ready", rows_free, "qtr2"), 1)])
                if name == "f2":
                    pe.wait_ge(sem("wabs"), 1)
                    mm(bank[:, 7, 0:1], ones[:, :], wstat[:, 0:1], start=True, stop=True).then_inc(sem("wsum"), 1)
                    pe.wait_ge(sem("wbit_ready"), 1)

                    def tb(t, u):
                        pe.wait_ge(sem("bitq_ready"), t + 1)
                        after(pe, sem("bT_ready"), t)
                        nc.tensor.transpose(bank[:, 0, 0:64].bitcast(BF16), bitq[u][:, :], identb[:, :]) \
                            .then_inc(sem("bt_done"), 1)

                    def yb_(t, u):
                        pe.wait_ge(sem("bT_ready"), t + 1)
                        after(pe, sem("xb_upd"), t)
                        mm(bank[:, 1, 0:C], bitT[u][:, :], wbit[:, :], start=True, stop=True).then_inc(sem("yb_done"), 1)

                    bit.run(pe, [(tb, 1), (yb_, 2)])
                if name == "x3":
                    def gate_scores(t, u):
                        pe.wait_ge(sem("hT_ready"), TB[name] + t + 1)
                        after(pe, sem("th3"), t)
                        mm(bank[:, 0, 0:P], hT[u][:, :], sq("w_gate"), start=True, stop=False)
                        mm(bank[:, 0, 0:P], ones[0:1, :], row("b_gate"), start=False, stop=True).then_inc(sem("g3_done"), 1)
                        after(pe, sem("exp3"), 2 * t)
                        mm(bank[:, 1, 0:P], hT[u][:, :], toks(ctxT, t), start=True, stop=True).then_inc(sem("s3_done"), 1)

                    def pt3(t, u):
                        pe.wait_ge(sem("pn3"), t + 1)
                        after(pe, sem("PT3_ready"), t)
                        nc.tensor.transpose(bank[:, 2, 0:P], P3[u][:, :], ident[:, :]).then_inc(sem("pt3_done"), 1)

                    def r3(t, u):
                        pe.wait_ge(sem("PT3_ready"), t + 1)
                        pe.wait_ge(sem("cs3_ready"), t + 1)
                        after(pe, sem("rT_ready"), t)
                        mm(bank[:, 3, 0:P], cT[u][:, :], PT[u][:, 0:P], start=True, stop=True).then_inc(sem("r3_done"), 1)

                    def l3(t, u):
                        pe.wait_ge(sem("rT_ready"), t + 1)
                        after(pe, sem("hn3"), t)
                        mm(bank[:, 4, 0:P], OT[u][:, :], sq("w_lin_r"), start=True, stop=False)
                        mm(bank[:, 4, 0:P], hT[u][:, :], sq("w_lin_h"), start=False, stop=False)
                        mm(bank[:, 4, 0:P], ones[0:1, :], row("b_lin"), start=False, stop=True).then_inc(sem("l3_done"), 1)

                    xl3.run(pe, [(l3, 2), (t1(name, TO_ps), 0), (gate_scores, 1), (pt3, 1), (r3, 1)])
                if name in MOE:
                    k = MOE.index(name)

                    def logits(t, u):
                        pe.wait_ge(sem("hT_ready"), TB[name] + t + 1)
                        after(pe, sem("lg_ready"), ROUTE[name] + t)
                        mm(L_ps, hT[u][:, :], rw[:, k, :], start=True, stop=True).then_inc(sem("lg_done"), 1)

                    pre.run(pe, [(t1(name, TO_ps), 0), (logits, 1)])
                    pe.wait_ge(sem("oh_ready"), k + 1)
                    ohf = ohs[:, :, :].rearrange("p t e -> p (t e)")
                    mm(bank[:, 0, 0:P], before[:, :], ohf, start=True, stop=True)
                    mm(bank[:, 1, 0:P], ones[:, :], ohf, start=True, stop=True).then_inc(sem("count_done"), 1)
                    if name == "f0":
                        pre.run(pe, [(t1("ctx", TO_ps), 0)])
                        pe.wait_ge(sem("hT_ready"), TB["ctx"] + NT)
                    pe.wait_ge(sem("slots_ready"), k + 1)
                    pe.wait_ge(sem("moe_w"), 16 * (18 if k < 2 else 28))
                    base, nb = BB[name], NBLK[name]
                    nj = (HJ if k < 2 else HID3 // P)

                    def expert(b, u):
                        if name == "f1":
                            return (b - u) * (nj * C // 2)
                        e = nc.tensor.value_load(blke[0:1, bass.ds(b, 1)], min_val=0, max_val=NE - 1)
                        return e * (nj * C)

                    def tblk(b, u):
                        pe.wait_ge(sem(f"xb_in{u}"), 8 * (base + b - u) + 16)
                        after(pe, sem("xbT_ready"), base + b)
                        nc.tensor.transpose(TO_ps, xb[u], ident[:, :]).then_inc(sem("xbT1"), 1)

                    def hid(b, u):
                        pe.wait_ge(sem("xbT_ready"), base + b + 1)
                        after(pe, sem("g_act"), base + b - 1)
                        if name == "m3":
                            after(pe, sem("g3_prod"), b - 1)
                        off = expert(b, u) * (HID // (nj * C))
                        mm(bank[:, u, :], xbT[u], w1[k][:, bass.ds(off, HID)], start=True, stop=True) \
                            .then_inc(sem("h_done"), 1)

                    def tg(b, u):
                        src = G3 if name == "m3" else G
                        pe.wait_ge(sem("g3_prod" if name == "m3" else "g_act"), (0 if name == "m3" else base) + b + 1)
                        after(pe, sem("GT_ready"), base + b - 1)
                        for j in range(nj):
                            ins = nc.tensor.transpose(bank[:, 2 + u, j * P:(j + 1) * P], src[u][:, j * P:(j + 1) * P],
                                                      ident[:, :])
                        ins.then_inc(sem("gtr_done"), 1)

                    def down(b, u):
                        pe.wait_ge(sem("GT_ready"), base + b + 1)
                        after(pe, sem("yb_ready"), base + b - 1)
                        off = expert(b, u)
                        for j in range(nj):
                            ins = mm(bank[:, 4 + u, 0:C], GT[u][:, j * P:(j + 1) * P], w2[k][:, bass.ds(off + j * C, C)],
                                     start=j == 0, stop=j == nj - 1)
                        ins.then_inc(sem("yps_done"), 1)

                    Ring(nb, 3).run(pe, [(tblk, 0), (tg, 2), (hid, 1), (down, 3)])

        @block.vector
        def _(dve):
            v = nc.vector
            chain = [0]

            def link(ins):
                chain[0] += 1
                ins.then_inc(sem("dve_chain"), 1)
                dve.wait_ge(sem("dve_chain"), chain[0])

            def tile_stats(src, t):
                v.bn_stats(tile(st, t), tile(src, t)).then_inc(sem("bn_done"), 1)

            def next_stats(src, updated, base=0):
                def stage(t, u):
                    dve.wait_ge(sem(updated), base + t + 1)
                    tile_stats(src, t)
                return stage

            def stats(name, src):
                i, twice = LNI[name], dict(LNS)[name]
                mn = meanc if name == "ctx" else mean
                if name in ("x0", "ctx"):
                    with dve.Fori(0, NT // 4) as t4:
                        for k in range(4):
                            tile_stats(src, t4 * 4 + k)
                dve.wait_ge(sem("bn_done"), (i + 1) * NT)
                v.tensor_tensor(st_a[:, :], st[:, :, 1], st[:, :, 4], ALU.add).then_inc(sem("st_parts"), 1)
                v.tensor_tensor(st_b[:, :], st[:, :, 1], st[:, :, 4], ALU.subtract).then_inc(sem("st_parts"), 1)
                v.tensor_tensor(st_c[:, :], st[:, :, 2], st[:, :, 5], ALU.add).then_inc(sem("st_parts"), 1)
                dve.wait_ge(sem("st_parts"), 3 * (i + 1))
                link(v.tensor_scalar(mn[:, :], st_a[:, :], 0.5, None, ALU.mult))
                link(v.scalar_tensor_tensor(st_b[:, :], st_b[:, :], 0.25, st_b[:, :], ALU.mult, ALU.mult))
                link(v.scalar_tensor_tensor(var[:, :], st_c[:, :], 1.0 / C, st_b[:, :], ALU.mult, ALU.add))
                v.tensor_scalar(veps[:, :], var[:, :], LN_EPS, None, ALU.add).then_inc(sem("var_ready"), 1)
                dve.wait_ge(sem("rstd_ready"), POW[name] + 1)
                if twice:
                    link(v.tensor_copy(rs1[:, :], rs[:, :]))
                    link(v.tensor_tensor(st_a[:, :], var[:, :], rs1[:, :], ALU.mult))
                    link(v.tensor_tensor(st_b[:, :], st_a[:, :], rs1[:, :], ALU.mult))
                    v.tensor_scalar(veps[:, :], st_b[:, :], LN_EPS, None, ALU.add).then_inc(sem("var_ready"), 1)
                    dve.wait_ge(sem("rstd_ready"), POW[name] + 2)
                    link(v.tensor_tensor(rs[:, :], rs[:, :], rs1[:, :], ALU.mult))

            def norm(name, src, also=None):
                def stage(t, u):
                    after(dve, sem("t1_done"), TB[name] + t - 1)
                    if also:
                        after(dve, sem(also[0]), also[1] + t - 1)
                    m, r = (meanc, rsc) if name == "ctx" else (mean, rs)
                    v.tensor_scalar(hs[u][:, :], tile(src, t), at(m, t), at(r, t), ALU.subtract, ALU.mult) \
                        .then_inc(sem("hs_ready"), 1)
                return stage

            def gx(layer):
                return gates[:, layer:layer + 1]

            def gf(layer):
                return gates[:, 4 + layer:5 + layer]

            dve.wait_ge(sem("pool_ready"), 1)
            dve.wait_ge(sem("x_in"), 16)
            dve.wait_ge(sem("vec_in"), 16 * VEC_LOADS)
            link(v.tensor_copy(maskf[:, :, :].rearrange("b t s -> b (t s)"),
                               maskraw[:, :, :].rearrange("b t s -> b (t s)").bitcast(U8)))
            link(v.tensor_reduce(maskall[:, :], maskf[:, :, :], AX.X, ALU.min))
            link(v.tensor_tensor(maskf[:, :, 0], maskf[:, :, 0], maskall[:, :], ALU.subtract))
            link(v.tensor_scalar(maskrow[:, :, :], maskf[:, :, :], NEG, None, ALU.mult))
            dve.wait_ge(sem("gates_ready"), 1)

            for name in phases():
                phase_start(dve, name)
                src = y3 if name == "m3" else x
                stats(name, src)
                if name == "x0":
                    dve.wait_ge(sem("ctx_in"), 16)
                    stats("ctx", ctxn)
                if name in ATT:
                    base = ATT[name]
                    bias_k = {"x0": "bk0", "x1": "bk1", "a3": None}[name]
                    bias_v = {"x0": 0, "x1": 1, "a3": None}[name]

                    def keys(t, u):
                        dve.wait_ge(sem("QT_ready"), base + t + 1)
                        after(dve, sem("s_done"), base + t - 1)
                        src_k = K_ps.unsqueeze(1).to_broadcast([P, HPG, P])
                        sel = headmask[:, :].unsqueeze(2).to_broadcast([P, HPG, P])
                        v.scalar_tensor_tensor(Kb[u][:, :, :], src_k, col(bias_k) if bias_k else 0.0, sel,
                                               ALU.add, ALU.mult).then_inc(sem("Kb_ready"), 1)

                    def vals(t, u):
                        dve.wait_ge(sem("QT_ready"), base + t + 1)
                        after(dve, sem("pv_done"), base + t - 1)
                        for half in range(2):
                            r = slice(half * SEQ, (half + 1) * SEQ)
                            src_v = V_ps[r, :].rearrange("p (mb q h d) -> p mb q h d", q=2, h=2, d=HD)[:, :, :, half, :]
                            dst = Vb[u][r, :, 0:4:3, half, :]
                            if bias_v is None:
                                ins = v.tensor_copy(dst, src_v)
                            else:
                                bb = bvB[r, bias_v, :, :, :].rearrange("p m b (q h d) -> p (m b) q h d", q=2, h=2)
                                ins = v.tensor_tensor(dst, src_v, bb[:, :, :, half, :], ALU.add)
                            ins.then_inc(sem("Vb_ready"), 1)

                    def s4(u):
                        return S_att.rearrange("p g (h k) -> p g h k", h=HPG)

                    def row_max(t, u):
                        dve.wait_ge(sem("s_done"), base + t + 1)
                        v.tensor_reduce(mx[u][:, :].rearrange("p (g h) -> p g h", g=GROUPS), s4(u), AX.X, ALU.max) \
                            .then_inc(sem("mx_ready"), 1)

                    def subtract(t, u):
                        dve.wait_ge(sem("mx_ready"), base + t + 1)
                        after(dve, sem("pt_done"), base + t - 1)
                        mb = mx[u][:, :].rearrange("p (g h) -> p g h", g=GROUPS).unsqueeze(3) \
                            .to_broadcast([P, GROUPS, HPG, SEQ])
                        v.tensor_tensor(Pr[u][:, :].rearrange("p (g h k) -> p g h k", g=GROUPS, h=HPG), s4(u), mb,
                                        ALU.subtract).then_inc(sem("sub_done"), 1)

                    def normalise(t, u):
                        dve.wait_ge(sem("pv_done"), base + t + 1)
                        after(dve, sem("y_done"), base + t - 1)
                        v.reciprocal(rsum[u], sum_ps).then_inc(sem("rinv_ready"), 1)
                        dve.wait_ge(sem("rinv_ready"), base + t + 1)
                        v.tensor_tensor(OT[u][:, :], O_ps, rsum[u], ALU.mult).then_inc(sem("O_ready"), 1)

                    def update(t, u):
                        dve.wait_ge(sem("y_done"), base + t + 1)
                        dve.wait_ge(sem("pv_done"), base + upto(t + 2, NT))
                        if name == "a3":
                            ins = v.tensor_tensor(tile(y3, t), OY_ps, tile(y3, t), ALU.add)
                        else:
                            ins = v.scalar_tensor_tensor(tile(x, t), OY_ps, gx({"x0": 0, "x1": 1}[name]), tile(x, t),
                                                         ALU.mult, ALU.add)
                        ins.then_inc(sem("x_upd"), 1)

                    def keep_rows(t, u):
                        v.tensor_scalar(tile(y3, t), tile(x, t), at(mean, t), at(rs1, t), ALU.subtract, ALU.mult) \
                            .then_inc(sem("y3_kept"), 1)

                    def update3(t, u):
                        dve.wait_ge(sem("y3_kept"), t + 1)
                        update(t, u)

                    a3 = name == "a3"
                    att.run(dve, [(row_max, 2), (norm(name, src), 0), (subtract, 2), (keys, 1), (vals, 1)]
                            + [(keep_rows, 0)] * a3 + [(update3 if a3 else update, 4), (normalise, 3),
                                                       (next_stats(y3 if a3 else x, "x_upd", base), 4)])
                    dve.wait_ge(sem("x_upd"), base + NT)
                    v.engine_nop().then_inc(sem("phase_done"), 1)
                if name == "x2":
                    def bn_rows(ps, stt, mv, done, ready, var_sem):
                        def stage(t, u):
                            dve.wait_ge(sem(done), t + 1)
                            after(dve, sem(ready), t - 1)
                            for k in range(2):
                                v.bn_stats(stt[u][:, k, :], ps[:, k, :]).then_inc(sem(var_sem + "_c"), 1)
                            dve.wait_ge(sem(var_sem + "_c"), 4 * t + 2)
                            v.memset(aggr_gap[:, :], 0.0)
                            v.bn_aggr(mv[u][:, :], stt[u][:, :, :].rearrange("p k s -> p (k s)")) \
                                .then_inc(sem(var_sem + "_c"), 1)
                            dve.wait_ge(sem(var_sem + "_c"), 4 * t + 3)
                            v.tensor_scalar(mv[u][:, 0:1], mv[u][:, 0:1], -1.0, None, ALU.mult) \
                                .then_inc(sem(var_sem + "_c"), 1)
                            v.tensor_scalar(mv[u][:, 1:2], mv[u][:, 1:2], LN_EPS, None, ALU.add).then_inc(sem(var_sem), 1)
                            dve.wait_ge(sem(var_sem + "_c"), 4 * t + 4)
                        return stage

                    def scaled_rows(dst, done, gain, shift, ready):
                        def stage(t, u):
                            dve.wait_ge(sem(done), t + 1)
                            after(dve, sem("s2_done"), t - 1)
                            for i in range(CH2 // 2, CH2):
                                ins = v.tensor_scalar(dst[u][:, i * P:(i + 1) * P], C2[:, 1, (i - 3) * P:(i - 2) * P],
                                                      col(f"{gain}{i}"), col(f"{shift}{i}"), ALU.mult, ALU.add)
                            ins.then_inc(sem(ready), 1)
                        return stage

                    def s4b():
                        return D2.rearrange("p a (i k) -> p a i k", k=SEQ)

                    def row_max2(t, u):
                        dve.wait_ge(sem("s2_done"), t + 1)
                        v.tensor_reduce(mx[u][:, 0:H2].rearrange("p (a i) -> p a i", a=2), s4b(), AX.X, ALU.max) \
                            .then_inc(sem("mx2"), 1)
                        dve.wait_ge(sem("mx2"), t + 1)
                        after(dve, sem("ptr2"), t - 1)
                        mb = mx[u][:, 0:H2].rearrange("p (a i) -> p a i", a=2).unsqueeze(3).to_broadcast([P, 2, CH2, SEQ])
                        v.tensor_tensor(Pr[u][:, 0:INNER].rearrange("p (a i k) -> p a i k", a=2, i=CH2), s4b(), mb,
                                        ALU.subtract).then_inc(sem("sub2"), 1)

                    def sums2(t, u):
                        dve.wait_ge(sem("exp2"), t + 1)
                        v.tensor_reduce(mx[u][:, 0:H2], Pr[u][:, 0:INNER].rearrange("p (h k) -> p h k", h=H2), AX.X,
                                        ALU.add).then_inc(sem("sum2"), 1)
                        dve.wait_ge(sem("sum2"), t + 1)
                        after(dve, sem("pn2"), t - 1)
                        v.reciprocal(rinv[u][:, 0:H2], mx[u][:, 0:H2]).then_inc(sem("rinv2"), 1)

                    def update2(t, u):
                        dve.wait_ge(sem("y2_done"), t + 1)
                        v.scalar_tensor_tensor(tile(x, t), Y2_ps, gx(2), tile(x, t), ALU.mult, ALU.add) \
                            .then_inc(sem("x2_upd"), 1)

                    att2.run(dve, [(update2, 5), (bn_rows(A2, qst, qmv, "q2_done", "qn_ready", "qvar"), 1),
                                   (bn_rows(B2, kst, kmv, "k2_done", "kn_ready", "kvar"), 1),
                                   (scaled_rows(KT2, "ktr2", "kg", "kb", "KT2_second"), 2), (row_max2, 3),
                                   (norm(name, src), 0), (next_stats(x, "x2_upd"), 5), (sums2, 3),
                                   (scaled_rows(QT2, "qtr2", "qg", "qb", "QT2_second"), 1)])
                    dve.wait_ge(sem("x2_upd"), NT)
                    v.engine_nop().then_inc(sem("phase_done"), 1)
                if name == "f2":
                    link(v.tensor_reduce(wstat[:, 0:1], sq("w_bitT"), AX.X, ALU.add, apply_absolute_value=True))
                    v.engine_nop().then_inc(sem("wabs"), 1)
                    dve.wait_ge(sem("wsum"), 1)
                    link(v.tensor_scalar(wstat[:, 1:2], bank[:, 7, 0:1], 1.0 / (C * C), BIT_EPS, ALU.mult, ALU.add))
                    link(v.reciprocal(wstat[:, 2:3], wstat[:, 1:2]))
                    link(v.tensor_scalar(wbtmp[:, :], sq("w_bitT"), wstat[:, 2:3], ROUND, ALU.mult, ALU.add))
                    link(v.tensor_scalar(wbtmp[:, :], wbtmp[:, :], ROUND, -1.0, ALU.subtract, ALU.max))
                    v.tensor_scalar(wbit[:, :], wbtmp[:, :], 1.0, None, ALU.min).then_inc(sem("wbit_ready"), 1)
                    link(v.scalar_tensor_tensor(wstat[:, 3:4], wstat[:, 1:2], 1.0 / 127.0, gf(2), ALU.mult, ALU.mult))

                    def normb(t, u):
                        v.tensor_scalar(hs[u][:, :], tile(x, t), at(mean, t), at(rs, t), ALU.subtract, ALU.mult) \
                            .then_inc(sem("bit_rows"), 1)

                    def quant(t, u):
                        c = sem("bit_chain")
                        dve.wait_ge(sem("bit_rows"), t + 1)
                        v.tensor_reduce(bits[u][:, 0:1], hs[u][:, :], AX.X, ALU.max, apply_absolute_value=True).then_inc(c, 1)
                        dve.wait_ge(c, 6 * t + 1)
                        v.tensor_scalar(bits[u][:, 1:2], bits[u][:, 0:1], BIT_EPS, None, ALU.add).then_inc(c, 1)
                        dve.wait_ge(c, 6 * t + 2)
                        v.reciprocal(bits[u][:, 2:3], bits[u][:, 1:2]).then_inc(c, 1)
                        v.tensor_tensor(bits[u][:, 3:4], bits[u][:, 1:2], wstat[:, 3:4], ALU.mult).then_inc(c, 1)
                        dve.wait_ge(c, 6 * t + 4)
                        v.tensor_scalar(hs[u][:, :], hs[u][:, :], bits[u][:, 2:3], 127.0, ALU.mult, ALU.mult).then_inc(c, 1)
                        dve.wait_ge(c, 6 * t + 5)
                        v.tensor_scalar(hs[u][:, :], hs[u][:, :], 127.0, ROUND, ALU.min, ALU.add).then_inc(c, 1)
                        dve.wait_ge(c, 6 * t + 6)
                        after(dve, sem("bt_done"), t - 1)
                        v.tensor_scalar(bitq[u][:, :], hs[u][:, :], ROUND, -128.0, ALU.subtract, ALU.max) \
                            .then_inc(sem("bitq_ready"), 1)
                        dve.wait_ge(sem("bitq_ready"), t + 1)

                    def updateb(t, u):
                        dve.wait_ge(sem("yb_done"), t + 1)
                        v.scalar_tensor_tensor(tile(x, t), bank[:, 1, 0:C], bits[u][:, 3:4], tile(x, t), ALU.mult,
                                               ALU.add).then_inc(sem("xb_upd"), 1)

                    bit.run(dve, [(normb, 0), (updateb, 3), (quant, 1), (next_stats(x, "xb_upd"), 3)])
                    dve.wait_ge(sem("xb_upd"), NT)
                    v.engine_nop().then_inc(sem("phase_done"), 1)
                if name == "x3":
                    def max3(t, u):
                        dve.wait_ge(sem("s3_done"), t + 1)
                        after(dve, sem("exp3"), 2 * (t - 1))
                        for b in range(PAIR):
                            half = slice(b * SEQ, (b + 1) * SEQ)
                            v.tensor_reduce(sm3[u][half, 0:1], bank[half, 1, half], AX.X, ALU.max, negate=True) \
                                .then_inc(sem("m3_ready"), 1)

                    def norm3(t, u):
                        dve.wait_ge(sem("exp3"), 2 * (t + 1))
                        v.reciprocal(sm3[u][:, 2:3], sm3[u][:, 1:2]).then_inc(sem("r3inv"), 1)
                        dve.wait_ge(sem("r3inv"), t + 1)
                        v.tensor_scalar(P3[u][:, :], P3[u][:, :], sm3[u][:, 2:3], None, ALU.mult).then_inc(sem("pn3"), 1)

                    def update3x(t, u):
                        c = sem("x3_chain")
                        dve.wait_ge(sem("hn3"), t + 1)
                        dve.wait_ge(sem("hs_kept"), t + 1)
                        v.scalar_tensor_tensor(hn3[u], hn3[u], at(pw, t), tile(y3, t), ALU.mult, ALU.subtract) \
                            .then_inc(c, 1)
                        dve.wait_ge(sem("th3"), t + 1)
                        v.tensor_scalar(th3[u], th3[u], 0.5, 0.5, ALU.mult, ALU.add).then_inc(c, 1)
                        dve.wait_ge(c, 4 * t + 2)
                        v.tensor_tensor(tmp3[u], th3[u], hn3[u], ALU.mult).then_inc(c, 1)
                        dve.wait_ge(c, 4 * t + 3)
                        v.tensor_tensor(tmp3[u], tmp3[u], tile(y3, t), ALU.add).then_inc(c, 1)
                        dve.wait_ge(c, 4 * t + 4)
                        v.scalar_tensor_tensor(tile(x, t), tmp3[u], gx(3), tile(x, t), ALU.mult, ALU.add) \
                            .then_inc(sem("x3_upd"), 1)

                    xl3.run(dve, [(norm(name, src, ("hs_kept", 0)), 0), (update3x, 3), (max3, 1), (norm3, 1), (next_stats(x, "x3_upd"), 3)])
                    dve.wait_ge(sem("x3_upd"), NT)
                    v.engine_nop().then_inc(sem("phase_done"), 1)
                if name in MOE:
                    k = MOE.index(name)

                    def take_logits(t, u):
                        dve.wait_ge(sem("lg_done"), ROUTE[name] + t + 1)
                        v.tensor_copy(tile(lg, t), L_ps).then_inc(sem("lg_ready"), 1)

                    pre.run(dve, [(norm(name, src, ("hn_kept", ROUTE[name])), 0), (take_logits, 2)])
                    dve.wait_ge(sem("lg_ready"), ROUTE[name] + NT)

                    def over_e(m):
                        return m.unsqueeze(2).to_broadcast([P, NT, NE])

                    def over_t(m):
                        return m.unsqueeze(1).to_broadcast([P, NT, NE])

                    def first_max(scores, best, onehot):
                        link(v.tensor_reduce(best[:, :], scores[:, :, :], AX.X, ALU.max))
                        link(v.tensor_tensor(rt[:, :, :], scores[:, :, :], over_e(best[:, :]), ALU.is_equal))
                        link(v.tensor_tensor(rt[:, :, :], rt[:, :, :], over_t(blk[:, 3, :]), ALU.mult))
                        link(v.tensor_reduce(rk[:, :], rt[:, :, :], AX.X, ALU.max))
                        link(v.tensor_tensor(onehot[:, :, :], over_t(blk[:, 3, :]), over_e(rk[:, :]), ALU.is_equal))

                    link(v.tensor_scalar(blk[:, 3, :], iota8[:, :], -1.0, float(NE), ALU.mult, ALU.add))
                    first_max(lg, rm[0], oh[0])
                    if KTOP[name] == 2:
                        link(v.scalar_tensor_tensor(lg2[:, :, :], oh[0][:, :, :], NEG, lg[:, :, :], ALU.mult, ALU.add))
                        first_max(lg2, rm[1], oh[1])
                        link(v.tensor_tensor(ohs[:, :, :], oh[0][:, :, :], oh[1][:, :, :], ALU.add))
                        v.engine_nop().then_inc(sem("oh_ready"), 1)
                        v.tensor_tensor(wt[1][:, :], rm[1][:, :], rm[0][:, :], ALU.subtract).then_inc(sem("gate_in"), 1)
                    else:
                        link(v.tensor_copy(ohs[:, :, :], oh[0][:, :, :]))
                        v.engine_nop().then_inc(sem("oh_ready"), 1)
                        v.tensor_tensor(rt[:, :, :], lg[:, :, :], over_e(rm[0][:, :]), ALU.subtract) \
                            .then_inc(sem("gate_in"), 1)
                    gate = gf({"f0": 0, "f1": 1, "m3": 3}[name])
                    dve.wait_ge(sem("gate_exp"), k + 1)
                    if KTOP[name] == 2:
                        link(v.tensor_scalar(rk[:, :], wt[1][:, :], 1.0, None, ALU.add))
                        link(v.reciprocal(rk[:, :], rk[:, :]))
                        link(v.tensor_scalar(wt[0][:, :], rk[:, :], gate, None, ALU.mult))
                        link(v.tensor_tensor(wt[1][:, :], wt[1][:, :], wt[0][:, :], ALU.mult))
                    else:
                        link(v.tensor_reduce(rk[:, :], rt[:, :, :], AX.X, ALU.add))
                        link(v.reciprocal(rk[:, :], rk[:, :]))
                        link(v.tensor_scalar(wt[0][:, :], rk[:, :], gate, None, ALU.mult))
                    dve.wait_ge(sem("count_done"), k + 1)
                    cnt = bank[:, 0, 0:P].rearrange("p (t e) -> p t e", e=NE)
                    link(v.tensor_copy(rn[:, :, :], bank[:, 1, 0:P].rearrange("p (t e) -> p e t", e=NE)))
                    link(v.tensor_tensor_scan(rscan[:, :, :].rearrange("p e t -> p (e t)"),
                                              runmask[:, :, :].rearrange("p e t -> p (e t)"),
                                              rn[:, :, :].rearrange("p e t -> p (e t)"), 0.0, ALU.mult, ALU.add))
                    link(v.tensor_tensor(rn[:, :, :], rscan[:, :, :], rn[:, :, :], ALU.subtract))
                    link(v.tensor_tensor(rt[:, :, :], cnt, rn[:, :, :].rearrange("p e t -> p t e"), ALU.add))
                    if KTOP[name] == 2:
                        link(v.tensor_scalar(blki[:, :], rscan[:, :, NT - 1], float(P - 1), None, ALU.add))
                        link(v.tensor_scalar(blki[:, :], blki[:, :], 7, None, ALU.arith_shift_right))
                        link(v.tensor_copy(blk[:, 0, :], blki[:, :]))
                        link(v.tensor_tensor_scan(blk[:, 1, :], ones[:, 0:NE], blk[:, 0, :], 0.0, ALU.mult, ALU.add))
                        link(v.tensor_tensor(blk[:, 2, :], blk[:, 1, :], blk[:, 0, :], ALU.subtract))
                        link(v.tensor_scalar(blk[:, 2, :], blk[:, 2, :], float(P), None, ALU.mult))
                        link(v.tensor_tensor(rt[:, :, :], rt[:, :, :], over_t(blk[:, 2, :]), ALU.add))
                        link(v.tensor_tensor(cmpb[:, :, :],
                                             iotab[:, :].unsqueeze(2).to_broadcast([1, TOP2_BLOCKS, NE]),
                                             blk[0:1, 1, :].unsqueeze(1).to_broadcast([1, TOP2_BLOCKS, NE]), ALU.is_ge))
                        link(v.tensor_reduce(blkef[:, :], cmpb[:, :, :], AX.X, ALU.add))
                        link(v.tensor_scalar(blke[:, :], blkef[:, :], float(NE - 1), None, ALU.min))
                    for j in range(KTOP[name]):
                        link(v.tensor_tensor(lg2[:, :, :], rt[:, :, :], oh[j][:, :, :], ALU.mult))
                        link(v.tensor_reduce(slotf[:, :], lg2[:, :, :], AX.X, ALU.add))
                        if KTOP[name] == 1:
                            link(v.tensor_scalar(keep[:, :], slotf[:, :], float(CAP), None, ALU.is_lt))
                            link(v.tensor_tensor(wt[0][:, :], wt[0][:, :], keep[:, :], ALU.mult))
                            link(v.tensor_tensor(lg2[:, :, :], over_t(iota8[:, :]), oh[0][:, :, :], ALU.mult))
                            link(v.tensor_reduce(rk[:, :], lg2[:, :, :], AX.X, ALU.add))
                            link(v.scalar_tensor_tensor(slotf[:, :], rk[:, :], float(CAP), slotf[:, :], ALU.mult, ALU.add))
                            link(v.tensor_scalar(rk[:, :], tokid[:, :], float(NE * CAP), None, ALU.add))
                            link(v.tensor_tensor(slotf[:, :], slotf[:, :], rk[:, :], ALU.subtract))
                            link(v.tensor_tensor(slotf[:, :], slotf[:, :], keep[:, :], ALU.mult))
                            link(v.tensor_tensor(slotf[:, :], slotf[:, :], rk[:, :], ALU.add))
                        link(v.tensor_copy(slot[j][:, :], slotf[:, :]))
                    v.engine_nop().then_inc(sem("slots_ready"), 1)
                    if name == "f0":
                        dve.wait_ge(sem("hn_kept"), ROUTE[name] + NT)
                        pre.run(dve, [(norm("ctx", ctxn), 0)])
                    base, nb = BB[name], NBLK[name]

                    def product3(b, u):
                        dve.wait_ge(sem("g_act"), base + b + 1)
                        after(dve, sem("gtr_done"), base + b - 1)
                        v.tensor_tensor(G3[u][:, :], G[u][:, 0:HID3], bank[:, u, HID3:HID], ALU.mult) \
                            .then_inc(sem("g3_prod"), 1)

                    def evac_GT(b, u):
                        dve.wait_ge(sem("gtr_done"), base + b + 1)
                        after(dve, sem("yps_done"), base + b - 1)
                        w = HID if k < 2 else HID3
                        v.tensor_copy(GT[u][:, 0:w], bank[:, 2 + u, 0:w]).then_inc(sem("GT_ready"), 1)

                    Ring(nb, 3).run(dve, ([(product3, 1)] if name == "m3" else []) + [(evac_GT, 2)])
                    if name == "m3":
                        dve.wait_ge(sem("t1_done"), TB[name] + NT)
                        link(v.scalar_tensor_tensor(x[:, :, :], y3[:, :, :], gate, x[:, :, :], ALU.mult, ALU.add))
                    second = second_rows(name)
                    tiles = 4
                    for q in range(NT // tiles):
                        dve.wait_ge(sem(f"gathered{q}"), 16 * tiles * (SC[name] + KTOP[name]))
                        ts = slice(q * tiles, (q + 1) * tiles)
                        for j in range(KTOP[name]):
                            rowsj = hn if j == 0 else second
                            link(v.tensor_tensor(rowsj[:, ts, :], rowsj[:, ts, :],
                                                 wt[j][:, ts].unsqueeze(2).to_broadcast([P, tiles, C]), ALU.mult))
                            link(v.tensor_tensor(x[:, ts, :], x[:, ts, :], rowsj[:, ts, :], ALU.add))
                        if name != "m3":
                            for t in range(q * tiles, (q + 1) * tiles):
                                tile_stats(x, t)
                    v.engine_nop().then_inc(sem("phase_done"), 1)


def kernel(**inputs):
    import concourse.bacc as bacc
    from concourse.bass_utils import run_bass_kernel_spmd

    a = {k: np.asarray(v) for k, v in inputs.items()}
    xi, ci = a["x"].reshape(TOK, C), a["ctx_1024"].reshape(TOK, C)
    vec = {"bq0": "L0_xattn_Wk_b", "bk0": "L0_xattn_Wv_b", "qn_w1": "L1_xattn_qn_w", "qn_b1": "L1_xattn_qn_b",
           "cn_w1": "L1_xattn_cn_w", "cn_b1": "L1_xattn_cn_b", "bq1": "L1_xattn_bq", "bk1": "L1_xattn_bk",
           "tab_g": "L2_xattn_tab_g", "tab_b": "L2_xattn_tab_b", "vid_g": "L2_xattn_vid_g", "vid_b": "L2_xattn_vid_b",
           "ln1_w": "L3_ffn_ln1_scale", "ln1_b": "L3_ffn_ln1_shift", "ln2_w": "L3_ffn_ln2_scale",
           "ln2_b": "L3_ffn_ln2_shift"}
    columns = [a[vec[n]] for n in COLS[:16]]
    for name in ("q_g", "q_b", "k_g", "k_b"):
        columns += list(a[f"L2_xattn_{name}"].reshape(CH2, P))
    rowv = [a[n] for n in ("L0_xattn_Wv_b", "L1_xattn_bv", "L1_xattn_bo", "L2_xattn_bo", "L3_xattn_b_gate",
                           "L3_xattn_b_lin", "L3_ffn_bo")]
    square = [a["L0_xattn_Wk_w"].T, a["L0_xattn_Wv_w"].T] + [a[f"L1_xattn_{n}"].T for n in ("Wq", "Wk", "Wv", "Wo")] + [
        a["L3_xattn_W_gate"], a["L3_xattn_W_lin"][:C], a["L3_xattn_W_lin"][C:]] + [
            a[f"L3_ffn_{n}"] for n in ("wq", "wk", "wv", "wo")] + [a["L2_ffn_weight"].T]
    arrays = {
        "x": xi, "ctx": ci, "ctxT": ci.T, "cols": np.stack(columns, 1), "rows": np.stack(rowv), "wsq": np.stack(square),
        "g": np.concatenate([a["g_xattn"], a["g_ffn"]]).reshape(1, 8), "pw": a["fside_BxS_0"].reshape(NT, P).T,
        "mask": a["mask_BxS2_bk0"].view(np.int32),
        "rw": np.stack([a["L0_ffn_router_w"].T, a["L1_ffn_wg"], a["L3_ffn_gate_w"]]),
        "wq2": a["L2_xattn_Wq"], "wk2": a["L2_xattn_Wk"], "wv2": a["L2_xattn_Wv"], "wo2": a["L2_xattn_Wo"],
        "w1_0": a["L0_ffn_w1"], "w1_1": a["L1_ffn_w1"], "w1_2": a["L3_ffn_w1"], "w1_3": a["L3_ffn_w2"],
        "w2_0": a["L0_ffn_w2"], "w2_1": a["L1_ffn_w2"], "w2_2": a["L3_ffn_w3"],
    }
    nc = bacc.Bacc("TRN2", target_bir_lowering=False, num_devices=1)
    feed, io = {}, {}
    for name, arr in arrays.items():
        arr = np.ascontiguousarray(arr)
        feed[f"in_{name}"] = arr
        io[name] = nc.dram_tensor(f"in_{name}", arr.shape, mybir.dt.from_np(arr.dtype), kind="ExternalInput").ap()
    io["out"] = nc.dram_tensor("out_dram", (TOK, C), F32, kind="ExternalOutput").ap()
    build(nc, io)
    r = run_bass_kernel_spmd(nc, [feed], core_ids=[0])
    return r.results[0]["out_dram"].reshape(B, SEQ, C)
```

```python
from contextlib import ExitStack

import numpy as np

import concourse.bass as bass
from concourse import mybir

F32 = mybir.dt.float32
BF16 = mybir.dt.bfloat16
I32 = mybir.dt.int32
U32 = mybir.dt.uint32
U8 = mybir.dt.uint8
ALU = mybir.AluOpType
ACT = mybir.ActivationFunctionType
AX = mybir.AxisListType

P = 128
C = 128
B, SEQ = 32, 64
TOK = B * SEQ
NT = TOK // P
PAIR = P // SEQ
HEADS, HD = 16, 8
GROUPS, HPG = 4, 4
H2, DH2 = 12, 64
INNER = H2 * DH2
CH2 = INNER // P
NE, HID = 8, 512
HJ = HID // P
HID3 = 256
CAP = TOK // NE
TOP2_BLOCKS = 2 * TOK // P + NE
TOP1_BLOCKS = TOK // P
ROWS = TOP2_BLOCKS * P
LN_EPS = 1e-5
BIT_EPS = 1e-8
NEG = -1e30
ROUND = 1.5 * 2.0 ** 23

COLS = ["bq0", "bk0", "qn_w1", "qn_b1", "cn_w1", "cn_b1", "bq1", "bk1", "tab_g", "tab_b", "vid_g", "vid_b",
        "ln1_w", "ln1_b", "ln2_w", "ln2_b"] + [f"qg{i}" for i in range(CH2)] + [f"qb{i}" for i in range(CH2)] + [
            f"kg{i}" for i in range(CH2)] + [f"kb{i}" for i in range(CH2)]
COL = {n: i for i, n in enumerate(COLS)}
ROWV = ["bv0", "bv1", "bo1", "bo2", "b_gate", "b_lin", "bo3"]
ROW = {n: i for i, n in enumerate(ROWV)}
PART = (0, 64, 96)
SQ = ["wq0", "wv0", "wq1", "wk1", "wv1", "wo1", "w_gate", "w_lin_r", "w_lin_h", "wq3", "wk3", "wv3", "wo3", "w_bitT"]
SQI = {n: i for i, n in enumerate(SQ)}

FIRST_LOADS, REST_LOADS = 7, 5

N_PHASES = 8


class Ring:

    def __init__(self, n, lag, body=2):
        self.n, self.lag, self.body = n, lag, body

    def run(self, eng, stages):
        body = self.body
        first = -(-(self.lag + 2) // body) * body
        last = self.n - self.n % body

        def step(i, par):
            for stage, lag in stages:
                t = i - lag
                if isinstance(i, int) and not 0 <= t < self.n:
                    continue
                stage(t, (par - lag) % body)

        for i in range(min(first, self.n + self.lag)):
            step(i, i % body)
        if last > first:
            with eng.Fori(first // body, last // body) as several:
                for par in range(body):
                    step(several * body + par, par)
        for i in range(max(first, last), self.n + self.lag):
            step(i, i % body)


def upto(v, most):
    return min(v, most) if isinstance(v, int) else v


def build(nc, io):
    with ExitStack() as ctx:
        def sb(name, shape, dt=F32):
            return ctx.enter_context(nc.sbuf_tensor(name, shape, dt))

        def two(name, shape, dt=F32):
            return [sb(f"{name}{u}", shape, dt) for u in range(2)]

        sems = {}

        def sem(name):
            if name not in sems:
                sems[name] = ctx.enter_context(nc.semaphore(name))
            return sems[name]

        x = sb("x", [P, NT, C])
        y3 = sb("y3", [P, NT, C])
        hn = sb("hn", [P, NT, C])
        ctxn = sb("ctxn", [P, NT, C])
        ctxT = sb("ctxT", [P, TOK])
        zT = sb("zT", [P, TOK])
        wsq = sb("wsq", [P, len(SQ), P])
        cols = sb("cols", [P, len(COLS)])
        rows = sb("rows", [P, len(ROWV) - 2, P])
        row_parts = sb("row_parts", [P, len(ROWV) - 2, P], BF16)
        part_rows = sb("part_rows", [P, P], BF16)
        bvB = sb("bvB", [P, 2, GROUPS, PAIR, HPG * HD])
        wq2 = sb("wq2", [P, INNER])
        wk2 = sb("wk2", [P, INNER])
        wv2 = sb("wv2", [P, INNER])
        wo2 = sb("wo2", [P, CH2, P])
        rw = sb("rw", [P, 3, NE])
        w1 = [sb(f"w1_{n}", [P, NE * HID]) for n in range(2)]
        w2 = [sb(f"w2_{n}", [P, NE * HJ * C]) for n in range(2)]
        w1, w2 = w1 + w1[:1], w2 + w2[:1]
        pw = sb("pw", [P, NT])
        gates_raw = sb("gates_raw", [P, 8])
        gates = sb("gates", [P, 8])
        maskraw = sb("maskraw", [PAIR, NT, SEQ // 4], I32)
        maskf = sb("maskf", [PAIR, NT, SEQ])
        maskall = sb("maskall", [PAIR, NT])
        maskrow = sb("maskrow", [PAIR, NT, SEQ], BF16)

        ident = sb("ident", [P, P])
        identb = sb("identb", [P, P], BF16)
        pairsel = sb("pairsel", [PAIR, P], BF16)
        causal = sb("causal", [P, SEQ], BF16)
        headmask = sb("headmask", [P, HPG])
        ones = sb("ones", [P, P])
        before = sb("before", [P, P])
        powm = sb("powm", [P, NT])
        iota8 = sb("iota8", [P, NE])
        iotab = sb("iotab", [P, TOP2_BLOCKS])
        iotap = sb("iotap", [P, P], BF16)
        rowid1 = sb("rowid1", [P, 1])
        tileid = sb("tileid", [P, 2, NT])
        spare = sb("spare", [P, TOP2_BLOCKS])
        runmask = sb("runmask", [P, NE, NT])
        tokid = sb("tokid", [P, NT])

        st = sb("st", [P, NT, 6])
        st_a = sb("st_a", [P, NT])
        st_b = sb("st_b", [P, NT])
        st_c = sb("st_c", [P, NT])
        mean = sb("mean", [P, NT])
        var = sb("var", [P, NT])
        veps = sb("veps", [P, NT])
        rs = sb("rs", [P, NT])
        veps1 = sb("veps1", [P, NT])
        rs1 = sb("rs1", [P, NT])
        st_ctx = sb("st_ctx", [P, NT, 6])
        meanc = sb("meanc", [P, NT])
        rsc = sb("rsc", [P, NT])

        hs = two("hs", [P, C])
        hT = two("hT", [P, P])
        cT = two("cT", [P, P])
        QT = two("QT", [P, P])
        Kb = two("Kb", [P, HPG, P])
        Vb = two("Vb", [P, GROUPS * PAIR, 4, 2, HD])
        headsum = sb("headsum", [P, 2, 2, 2, HD])
        Pr = two("Pr", [P, HEADS * SEQ])
        PT = two("PT", [P, HEADS * SEQ])
        mx = two("mx", [P, HEADS])
        rinv = two("rinv", [P, HEADS])
        OT = two("OT", [P, P])
        qn = [hn[:, :, :].rearrange("p t c -> p (t c)")[:, u * INNER:(u + 1) * INNER] for u in range(2)]
        kn = [y3[:, :, :].rearrange("p t c -> p (t c)")[:, u * INNER:(u + 1) * INNER] for u in range(2)]
        QT2 = two("QT2", [P, INNER])
        rsum = [QT2[u][:, 0:P] for u in range(2)]
        KT2 = two("KT2", [P, INNER])
        Vs = two("Vs", [P, PAIR, INNER // 2])
        OT2 = two("OT2", [P, CH2, P])
        qst = two("qst", [P, 2, 6])
        kst = two("kst", [P, 2, 6])
        qmv = two("qmv", [P, 2])
        kmv = two("kmv", [P, 2])
        qr = two("qr", [P, 1])
        kr = two("kr", [P, 1])
        cV2 = [Kb[u][:, 0, :] for u in range(2)]
        P3 = two("P3", [P, P])
        sm3 = two("sm3", [P, 4])
        hn3, tmp3 = [[QT2[u][:, i * P:(i + 1) * P] for u in range(2)] for i in range(2)]
        hT4 = [m[:, :] for m in hT] + [KT2[u][:, 0:P] for u in range(2)]
        bitq = two("bitq", [P, P], BF16)
        bitT = two("bitT", [P, P], BF16)
        aggr_gap = sb("aggr_gap", [P, 1])
        wbit = sb("wbit", [P, P], BF16)
        wbtmp = sb("wbtmp", [P, P])
        wstat = sb("wstat", [P, 4])

        route_parts = [Kb[u][:, i, :] for u in range(2) for i in range(HPG)]
        lg, lg2, rt, ohs, *oh = [m.rearrange("p (t e) -> p t e", e=NE) for m in route_parts[:6]]
        own = Kb[0][:, 0:2, :].rearrange("p j (t e) -> p j t e", e=NE)
        rn, rscan = [m.rearrange("p (e t) -> p e t", e=NE) for m in route_parts[6:]]
        rm = [sb(f"rm{k}", [P, NT]) for k in range(2)]
        rk = sb("rk", [P, NT])
        blk = sb("blk", [P, 4, NE])
        blki = sb("blki", [P, NE], I32)
        slotf = sb("slotf", [P, 2, NT])
        keep = sb("keep", [P, NT])
        slot = sb("slot", [P, 2, NT], I32)
        slot_src = sb("slot_src", [P, TOP2_BLOCKS], U32)
        slot_dst = sb("slot_dst", [P, TOP2_BLOCKS], U32)
        row_max_, row_scale, row_inv, out_scale = rm[0], rm[1], rk, slotf[:, 0, :]
        wt = [sb(f"wt{k}", [P, NT]) for k in range(2)]
        cmpb = Vs[0][0:1, 0, 0:TOP2_BLOCKS * NE].rearrange("p (b e) -> p b e", e=NE)
        tab0, tab1, tab2 = [KT2[0][:, i * P:i * P + TOP2_BLOCKS] for i in range(3)]
        slot_blk, slot_row = [KT2[0][:, i * P:i * P + 2 * NT].rearrange("p (j t) -> p j t", t=NT) for i in (3, 4)]
        slot_bi, slot_ri = [OT2[0][:, i, 0:2 * NT].rearrange("p (j t) -> p j t", t=NT).bitcast(I32) for i in range(2)]
        hot_row = [Pr[k][:, :].bitcast(BF16).rearrange("p (t r) -> p t r", r=P) for k in range(2)]

        def hot_blk(k, nb):
            return PT[k][:, :].bitcast(BF16)[:, 0:NT * 3 * nb].rearrange("p (t v b) -> p t v b", t=NT, v=3)

        blkef = sb("blkef", [1, TOP2_BLOCKS])
        blke = sb("blke", [1, TOP2_BLOCKS], I32)
        xb = [QT2[u % 2][:, (0, 3 * C)[u // 2]:(C, 4 * C)[u // 2]] for u in range(4)]
        xbT = [QT2[u][:, C:2 * C] for u in range(2)]
        G = [Pr[u][:, 0:HID] for u in range(2)]
        G3 = [Pr[u][:, HID:HID + HID3] for u in range(2)]
        GT = [PT[u][:, 0:HID] for u in range(2)]
        yb = [QT2[u % 2][:, (2 * C, 4 * C)[u // 2]:(3 * C, 5 * C)[u // 2]] for u in range(4)]
        hc = OT

        rows_h = nc.dram_tensor("rows_h", (TOK, C), F32).ap()
        rows_tok = nc.dram_tensor("rows_tok", (2 * TOK + ROWS, C), F32).ap()

        bank = ctx.enter_context(nc.psum_tensor("bank", [P, 8, 512], F32))
        flat = bank[:, :, :].rearrange("p b n -> p (b n)")
        block = ctx.enter_context(nc.Block())

        def sq(name):
            return wsq[:, SQI[name], :]

        def col(name):
            return cols[:, COL[name]:COL[name] + 1]

        def row(name):
            return row_parts[:, ROW[name] - 2, :]

        def tile(buf, t):
            return buf[:, bass.ds(t, 1), :].rearrange("p a c -> p (a c)")

        def at(buf, t):
            return buf[:, bass.ds(t, 1)]

        def toks(buf, t):
            return buf[:, bass.ds(t * P, P)]

        def after(eng, s, n):
            if not isinstance(n, int) or n > 0:
                eng.wait_ge(s, n)

        TWICE = ("x1", "x2", "a3")
        EARLY = 3 * NT // 4
        STATS = ["x0", "f0", "x1", "f1", "x2", "f2", "x3", "a3", "m3"]
        TILES_OF = {"all": slice(0, NT), "early": slice(0, EARLY), "late": slice(EARLY, NT)}
        VARS, POWS = {}, {}
        n = 0
        for name in STATS:
            for part in ["all"] if name == "x0" else ["early", "late"]:
                n += 2 if name == "a3" else 1
                VARS[name, part], POWS[name, part] = len(VARS) + 1, n
            if name == "f0":
                n += 1
                VARS["ctx", "all"], POWS["ctx", "all"] = len(VARS) + 1, n
        LOOPS = ["x0", "f0", "x1", "f1", "x2", "x3", "a3", "m3"]
        TB = {name: NT * i for i, name in enumerate(LOOPS)}
        ATT = {"x0": 0, "x1": NT, "a3": 2 * NT}
        MOE = ["f0", "f1", "m3"]
        ROUTE = {"f0": 0, "f1": NT, "m3": 2 * NT}
        NBLK = {"f0": TOP2_BLOCKS, "f1": TOP1_BLOCKS, "m3": TOP2_BLOCKS}
        BB = {"f0": 0, "f1": TOP2_BLOCKS, "m3": TOP2_BLOCKS + TOP1_BLOCKS}
        KTOP = {"f0": 2, "f1": 1, "m3": 2}
        SC = {"f0": 0, "f1": 2, "m3": 3}

        HT_READER = {"x2": ("q2_done", 0), }
        HT_READER.update({n: ("v_done", c) for n, c in ATT.items()})
        HT_READER.update({n: ("lg_done", c) for n, c in ROUTE.items()})

        PH = ["x0", "f0", "x1", "f1", "x2", "f2", "x3", "a3", "m3"]
        PHI = {n: i for i, n in enumerate(PH)}

        def phases():
            return PH[:N_PHASES + 1] if N_PHASES >= 8 else PH[:N_PHASES]

        def phase_start(eng, name):
            if PHI[name]:
                eng.wait_ge(sem("phase_done"), PHI[name])
            if name == "f0":
                eng.wait_ge(sem("pool_ready"), 2)
                eng.wait_ge(sem("rest_in"), 16 * REST_LOADS)

        def second_rows(name):
            return ctxn if name == "m3" else y3

        def blocks_lag(name):
            return 4

        att = Ring(NT, 4)
        att2 = Ring(NT, 5)
        pre = Ring(NT, 3, 4)
        xl3 = Ring(NT, 5, 4)
        bit = Ring(NT, 4)

        S_att = bank[:, 0:GROUPS, 0:256]
        PT_ps = flat[:, 4 * 512:6 * 512]
        TO_ps = bank[:, 6, 0:128]
        TO2_ps = bank[:, 4, 0:128]
        Q_ps = bank[:, 6, 0:128]
        K_ps = bank[:, 6, 128:256]
        V_ps = bank[:, 6, 256:512]
        O_ps = bank[:, 7, 0:128]
        sum_ps = bank[:, 7, 128:256]
        OY_ps = bank[:, 7, 256:384]
        L_ps = bank[:, 7, 0:NE]
        Z_ps = bank[:, 5, 0:128]
        tab_ps = bank[:, 2, :]
        A2 = bank[:, 0:2, 0:384]
        B2 = bank[:, 2:4, 0:384]
        C2 = bank[:, 4:6, 0:384]
        D2 = bank[:, 6:8, 0:384]
        T2_ps = bank[:, 6, 384:512]
        Y2_ps = bank[:, 7, 384:512]

        @block.sync
        def _(sp):
            xv = io["x"].rearrange("(t p) c -> p t c", p=P)
            for q in range(4):
                ts = slice(q * NT // 4, (q + 1) * NT // 4)
                sp.dma_start(x[:, ts, :], xv[:, ts, :]).then_inc(sem(f"x_in{q}"), 16)
            sp.dma_start(cols[:, :], io["cols"]).then_inc(sem("first_in"), 16)
            sp.dma_start(gates_raw[:, :], io["g"].to_broadcast([P, 8])).then_inc(sem("first_in"), 16)
            sp.dma_start(wsq[:, 0:2, :], io["wsq"][0:2].rearrange("n p c -> p n c")).then_inc(sem("first_in"), 16)
            for layer in range(2):
                for b in range(PAIR):
                    sp.dma_start(bvB[:, layer, :, b, :], io["rows"][layer:layer + 1, :].rearrange("a (m f) -> a m f", m=GROUPS)
                                 .to_broadcast([P, GROUPS, HPG * HD])).then_inc(sem("first_in"), 16)
            sp.dma_start(ctxT[:, :], io["ctxT"]).then_inc(sem("ctxT_in"), 16)
            sp.dma_start(ctxn[:, :, :], io["ctx"].rearrange("(t p) c -> p t c", p=P)).then_inc(sem("ctx_in"), 16)
            sp.dma_start(wsq[:, 2:, :], io["wsq"][2:].rearrange("n p c -> p n c")).then_inc(sem("rest_in"), 16)
            sp.dma_start(rows[:, :, :], io["rows"][2:].rearrange("(a n) c -> a n c", a=1)
                         .to_broadcast([P, len(ROWV) - 2, P])).then_inc(sem("rest_in"), 16)
            sp.dma_start(pw[:, :], io["pw"]).then_inc(sem("rest_in"), 16)
            sp.dma_start(maskraw[:, :, :], io["mask"].rearrange("(t b) s -> b t s", b=PAIR)).then_inc(sem("rest_in"), 16)
            sp.dma_start(rw[:, :, :], io["rw"].rearrange("n p e -> p n e")).then_inc(sem("rest_in"), 16)
            for name, buf in (("wq2", wq2), ("wk2", wk2), ("wv2", wv2)):
                sp.dma_start(buf[:, :], io[name]).then_inc(sem("w_in2"), 16)
            sp.dma_start(wo2[:, :, :], io["wo2"].rearrange("(i p) c -> p i c", p=P)).then_inc(sem("w_in2"), 16)

            def expert_weights(k):
                w1v = w1[k][:, :].rearrange("p (e h) -> p e h", e=NE)
                if k < 2:
                    sp.dma_start(w1v, io[f"w1_{k}"].rearrange("e c h -> c e h")).then_inc(sem("moe_w"), 16)
                else:
                    sp.dma_start(w1v[:, :, 0:HID3], io["w1_2"].rearrange("e c h -> c e h")).then_inc(sem("moe_w"), 16)
                    sp.dma_start(w1v[:, :, HID3:HID], io["w1_3"].rearrange("e c h -> c e h")).then_inc(sem("moe_w"), 16)
                n = io[f"w2_{k}"].shape[1] // P
                for e in range(NE):
                    sp.dma_start(w2[k][:, e * n * C:(e + 1) * n * C].rearrange("p (j c) -> p j c", c=C),
                                 io[f"w2_{k}"][e].rearrange("(j p) c -> p j c", p=P)).then_inc(sem("moe_w"), 16)

            expert_weights(0)
            expert_weights(1)
            for name in phases():
                if name not in MOE:
                    continue
                base, nb = BB[name], NBLK[name]
                sp.wait_ge(sem("hn_kept"), ROUTE[name] + NT)
                sp.dma_start(rows_h.rearrange("(t p) c -> p t c", p=P), hn[:, :, :]).then_inc(sem("rows_stored"), 16)
                for u in range(4):
                    sp.wait_ge(sem(f"yb_out{u}"), 4 * (base + nb))
                tiles = 4
                for q in range(NT // tiles):
                    for j in range(KTOP[name]):
                        r = slice(j * TOK + q * tiles * P, j * TOK + (q + 1) * tiles * P)
                        into = hn if j == 0 else second_rows(name)
                        sp.dma_start(into[:, q * tiles:(q + 1) * tiles, :],
                                     rows_tok[r, :].rearrange("(t p) c -> p t c", p=P)).then_inc(sem(f"gathered{q}"), 16)
                if name == "f0":
                    sp.wait_ge(sem("phase_done"), PHI[name] + 1)
                    expert_weights(2)

            quarters = 4 if phases()[-1] in MOE else 1
            for q in range(quarters):
                if quarters > 1:
                    sp.wait_ge(sem("x_final"), q + 1)
                else:
                    sp.wait_ge(sem("phase_done"), len(phases()))
                n = NT // quarters
                sp.dma_start(io["out"][q * n * P:(q + 1) * n * P, :].rearrange("(t p) c -> p t c", p=P),
                             x[:, q * n:(q + 1) * n, :]).then_inc(sem("out_done"), 16)
            sp.wait_ge(sem("out_done"), 16 * quarters)

        @block.gpsimd
        def _(pool):
            g = nc.gpsimd
            chain = [0]

            def link(ins):
                chain[0] += 1
                ins.then_inc(sem("pool_chain"), 1)
                pool.wait_ge(sem("pool_chain"), chain[0])

            def select(out, fill, base, pattern, mult, op=ALU.not_equal):
                link(g.affine_select(out=out, in_=out, compare_op=op, fill=fill, base=base, pattern=pattern,
                                     channel_multiplier=mult))

            link(g.memset(ident[:, :], 0.0))
            select(ident[:, :], 1.0, 0, [[-1, P]], 1)
            link(g.tensor_copy(identb[:, :], ident[:, :]))
            link(g.memset(powm[:, :], -0.5))
            link(g.memset(ones[:, :], 1.0))
            link(g.memset(headmask[:, :], 0.0))
            for grp in range(GROUPS):
                link(g.memset(before[:, 0:HPG], 1.0))
                select(before[:, 0:HPG], 0.0, -32 * grp, [[-8, HPG]], 1, ALU.is_ge)
                select(before[:, 0:HPG], 0.0, 32 * grp + 7, [[8, HPG]], -1, ALU.is_ge)
                link(g.tensor_tensor(headmask[:, :], headmask[:, :], before[:, 0:HPG], ALU.add))
            for u in range(2):
                link(g.memset(Vb[u][:, :, :, :, :], 0.0))
            link(g.memset(headsum[:, :, :, :, :], 0.0))
            for half in range(2):
                for r in range(2):
                    link(g.memset(headsum[half * SEQ:(half + 1) * SEQ, r, r, half, :], 1.0))
            g.engine_nop().then_inc(sem("pool_ready"), 1)

            def later_constants():
                link(g.memset(pairsel[:, :], 1.0))
                select(pairsel[:, :].rearrange("b (c q) -> b c q", c=PAIR), 0.0, 0, [[-1, PAIR], [0, SEQ]], 1, ALU.is_equal)
                link(g.memset(causal[:, :], 0.0))
                select(causal[0:SEQ, :], NEG, 0, [[-1, SEQ]], 1, ALU.is_ge)
                select(causal[SEQ:P, :], NEG, 0, [[-1, SEQ]], 1, ALU.is_ge)
                link(g.memset(part_rows[:, :], 0.0))
                for p in PART:
                    link(g.memset(part_rows[p:p + 1, :], 1.0))
                link(g.memset(before[:, :], 1.0))
                select(before[:, :], 0.0, 0, [[1, P]], -1, ALU.is_gt)
                def count_up(out, temp, pattern, base, mult):
                    link(g.iota(temp, pattern=pattern, base=base, channel_multiplier=mult))
                    link(g.tensor_copy(out, temp))

                count_up(iota8[:, :], slot[:, 0, 0:NE], [[1, NE]], 0, 0)
                count_up(tokid[:, :], slot[:, 0, :], [[P, NT]], 0, 1)
                count_up(rowid1[:, :], slot[:, 0, 0:1], [[0, 1]], 1, 1)
                count_up(tileid[:, 0, :], slot[:, 0, :], [[1, NT]], 0, 0)
                count_up(tileid[:, 1, :], slot[:, 0, :], [[1, NT]], NT, 0)
                count_up(iotab[:, :], slot_src[:, :].bitcast(I32), [[1, TOP2_BLOCKS]], 0, 0)
                count_up(spare[:, :], slot_src[:, :].bitcast(I32), [[P, TOP2_BLOCKS]], 2 * TOK, 1)
                count_up(iotap[:, :], KT2[0][:, 0:P].bitcast(I32), [[1, P]], 0, 0)
                link(g.memset(runmask[:, :, :], 1.0))
                link(g.memset(runmask[:, :, 0:1], 0.0))
                for u in range(2):
                    link(g.memset(P3[u][:, :], 0.0))
                g.engine_nop().then_inc(sem("pool_ready"), 1)

            def powers(name, part):
                ts = TILES_OF[part]
                pool.wait_ge(sem("var_ready"), VARS[name, part])
                g.tensor_tensor((rsc if name == "ctx" else rs)[:, ts], veps[:, ts], powm[:, ts], ALU.pow) \
                    .then_inc(sem("rstd_ready"), 1)
                if name == "a3":
                    g.tensor_tensor(rs1[:, ts], veps1[:, ts], powm[:, ts], ALU.pow).then_inc(sem("rstd_ready"), 1)

            for name in phases():
                phase_start(pool, name)
                powers(name, "all" if name == "x0" else "late")
                if name == "f0":
                    powers("ctx", "all")
                if name == "x0":
                    pool.wait_ge(sem("ctxT_in"), 16)

                    def stage(t, u):
                        after(pool, sem("v_done"), ATT[name] + t - 1)
                        g.tensor_copy(cT[u][:, :], toks(ctxT, t)).then_inc(sem("cT_ready"), 1)

                    att.run(pool, [(stage, 0)])
                    later_constants()
                if name == "x2":
                    def pow_rows(mv, rr, var, ready):
                        def stage(t, u):
                            pool.wait_ge(sem(var), t + 1)
                            g.tensor_tensor(rr[u][:, :], mv[u][:, 1:2], powm[:, 0:1], ALU.pow).then_inc(sem(ready + "_c"), 1)
                            pool.wait_ge(sem(ready + "_c"), t + 1)
                            g.tensor_tensor(mv[u][:, 0:1], mv[u][:, 0:1], rr[u][:, :], ALU.mult).then_inc(sem(ready), 1)
                        return stage

                    def stage_keys(t, u):
                        after(pool, sem("k2_done"), t - 1)
                        g.tensor_copy(cT[u][:, :], toks(zT, t)).then_inc(sem("cT_ready"), 1)

                    def stage_values(t, u):
                        after(pool, sem("v2_done"), t - 1)
                        g.tensor_copy(cV2[u], toks(zT, t)).then_inc(sem("cV2_ready"), 1)

                    def pnorm(t, u):
                        pool.wait_ge(sem("rinv2"), t + 1)
                        pv = Pr[u][:, 0:INNER].rearrange("p (h k) -> p h k", h=H2)
                        g.tensor_tensor(pv, pv, rinv[u][:, 0:H2].unsqueeze(2).to_broadcast([P, H2, SEQ]),
                                        ALU.mult).then_inc(sem("pn2"), 1)

                    pool.wait_ge(sem("z_scaled"), 1)
                    att2.run(pool, [(pow_rows(qmv, qr, "qvar", "qr_ready"), 1), (pow_rows(kmv, kr, "kvar", "kr_ready"), 1),
                                    (stage_keys, 0), (stage_values, 2), (pnorm, 3)])
                if name == "x3":
                    def keep_ctx(t, u):
                        after(pool, sem("r3_done"), t - 1)
                        g.tensor_copy(cT[u % 2][:, :], tile(ctxn, t)).then_inc(sem("cs3_ready"), 1)

                    def keep_h(t, u):
                        pool.wait_ge(sem("hs_ready"), TB[name] + t + 1)
                        g.tensor_copy(tile(y3, t), hs[u % 2][:, :]).then_inc(sem("hs_kept"), 1)

                    xl3.run(pool, [(keep_h, 0), (keep_ctx, 2)])
                if name in MOE:
                    def keep_h(t, u):
                        pool.wait_ge(sem("hs_ready"), TB[name] + t + 1)
                        g.tensor_copy(tile(hn, t), hs[u % 2][:, :]).then_inc(sem("hn_kept"), 1)

                    pre.run(pool, [(keep_h, 0)])
                    pool.wait_ge(sem("slots_ready"), MOE.index(name) + 1)
                    pool.wait_ge(sem("rows_stored"), 16 * (MOE.index(name) + 1))
                    nb, base = NBLK[name], BB[name]
                    ahead = 6
                    for i in range(nb + ahead):
                        if i < nb:
                            after(pool, sem("xbT1"), base + i - 3)
                            g.indirect_dma_start(xb[i % 4], None, rows_h[:, :],
                                                 bass.IndirectOffsetOnAxis(ap=slot_src[:, i:i + 1], axis=0)) \
                                .then_inc(sem(f"xb_in{i % 4}"), 16)
                        if i >= ahead:
                            b = i - ahead
                            pool.wait_ge(sem("yb_ready"), base + b + 1)
                            g.indirect_dma_start(rows_tok[:, :], bass.IndirectOffsetOnAxis(ap=slot_dst[:, b:b + 1], axis=0),
                                                 yb[b % 4], None).then_inc(sem(f"yb_out{b % 4}"), 16)
                if name != phases()[-1]:
                    powers(PH[PHI[name] + 1], "early")

        @block.scalar
        def _(act):
            a = nc.scalar
            act.wait_ge(sem("first_in"), 16 * FIRST_LOADS)
            a.activation(gates[:, :], gates_raw[:, :], ACT.Tanh).then_inc(sem("gates_ready"), 1)

            def evac_hT(name, regions, w=None, b=None):
                def stage(t, u):
                    act.wait_ge(sem("t1_done"), TB[name] + t + 1)
                    after(act, sem(HT_READER[name][0]), HT_READER[name][1] + t - 1)
                    if w:
                        ins = a.activation(hT[u % 2][:, :], regions[u % len(regions)], ACT.Identity, bias=col(b), scale=col(w))
                    else:
                        ins = a.activation(hT[u % 2][:, :], regions[u % len(regions)], ACT.Copy)
                    ins.then_inc(sem("hT_ready"), 1)
                return stage

            def stage_ctx(scale, shift, used, used_before):
                def stage(t, u):
                    after(act, sem(used), used_before + t - 1)
                    a.activation(cT[u][:, :], toks(zT, t), ACT.Identity, bias=col(shift), scale=col(scale)) \
                        .then_inc(sem("cT_ready"), 1)
                return stage

            for name in phases():
                phase_start(act, name)
                if name in ATT:
                    base = ATT[name]
                    affine = {"x0": (None, None), "x1": ("qn_w1", "qn_b1"), "a3": ("ln1_w", "ln1_b")}[name]
                    bias_q = {"x0": "bq0", "x1": "bq1", "a3": None}[name]

                    def evac_Q(t, u):
                        act.wait_ge(sem("v_done"), base + t + 1)
                        after(act, sem("s_done"), base + t - 1)
                        if bias_q:
                            ins = a.activation(QT[u][:, :], Q_ps, ACT.Identity, bias=col(bias_q))
                        else:
                            ins = a.activation(QT[u][:, :], Q_ps, ACT.Copy)
                        ins.then_inc(sem("QT_ready"), 1)

                    def expo(h):
                        def stage(t, u):
                            act.wait_ge(sem("sub_done" if h else "sub_first"), base + t + 1)
                            half = Pr[u][:, h * 4 * P:(h + 1) * 4 * P]
                            a.activation(half, half, ACT.Exp, scale=float(HD) ** -0.5) \
                                .then_inc(sem("exp_done" if h else "exp_first"), 1)
                        return stage

                    def evac_PT(h):
                        def stage(t, u):
                            act.wait_ge(sem("pt_done" if h else "pt_first"), base + t + 1)
                            if h == 0:
                                after(act, sem("pv_done"), base + t - 1)
                            cs = slice(h * 4 * P, (h + 1) * 4 * P)
                            a.activation(PT[u][:, cs], PT_ps[:, cs], ACT.Copy).then_inc(sem("PT_ready"), 1)
                        return stage

                    own_ctx = [(stage_ctx("cn_w1", "cn_b1", "v_done", base), 0)] if name == "x1" else []
                    att.run(act, [(evac_Q, 1)] + own_ctx + [(expo(1), 2), (evac_hT(name, (TO_ps,), *affine), 0),
                                                            (evac_PT(0), 2), (evac_PT(1), 2), (expo(0), 1)])
                if name == "x2":
                    a.activation(zT[:, :], zT[:, :], ACT.Identity, bias=col("tab_b"), scale=col("tab_g")) \
                        .then_inc(sem("z_scaled"), 1)

                    def expo(t, u):
                        act.wait_ge(sem("sub2"), t + 1)
                        a.activation(Pr[u][:, 0:INNER], Pr[u][:, 0:INNER], ACT.Exp, scale=float(DH2) ** -0.5) \
                            .then_inc(sem("exp2"), 1)

                    def scaled_rows(dst, done, gain, shift, ready):
                        def stage(t, u):
                            act.wait_ge(sem(done), t + 1)
                            after(act, sem("s2_done"), t - 1)
                            for i in range(CH2 // 2):
                                ins = a.activation(dst[u][:, i * P:(i + 1) * P], C2[:, 0, i * P:(i + 1) * P],
                                                   ACT.Identity, bias=col(f"{shift}{i}"), scale=col(f"{gain}{i}"))
                            ins.then_inc(sem(ready), 1)
                        return stage

                    def norm_rows(dst, src, rr, mv, ready, done, used):
                        def stage(t, u):
                            act.wait_ge(sem(ready), t + 1)
                            after(act, sem(used), t - 1)
                            a.activation(dst[u].rearrange("p (k n) -> p k n", k=2), src, ACT.Identity,
                                         bias=mv[u][:, 0:1], scale=rr[u][:, 0:1]).then_inc(sem(done), 1)
                        return stage

                    def evac_PT2(t, u):
                        act.wait_ge(sem("ptr2"), t + 1)
                        after(act, sem("ot2_done"), t - 1)
                        a.activation(PT[u][:, 0:INNER].rearrange("p (k n) -> p k n", k=2), C2, ACT.Copy) \
                            .then_inc(sem("PT2_ready"), 1)

                    def evac_V2(t, u):
                        act.wait_ge(sem("v2_done"), t + 1)
                        after(act, sem("ot2_done"), t - 1)
                        a.activation(Vs[u][:, :, :], A2, ACT.Copy).then_inc(sem("Vs_ready"), 1)

                    def evac_OT2(t, u):
                        act.wait_ge(sem("ot2_done"), t + 1)
                        after(act, sem("y2_done"), t - 1)
                        a.activation(OT2[u][:, :, :].rearrange("p (k i) n -> p k (i n)", k=2), B2, ACT.Copy).then_inc(sem("OT2_ready"), 1)

                    att2.run(act, [(scaled_rows(KT2, "ktr2", "kg", "kb", "KT2_first"), 2),
                                   (norm_rows(qn, A2, qr, qmv, "qr_ready", "qn_ready", "qtr2"), 1),
                                   (norm_rows(kn, B2, kr, kmv, "kr_ready", "kn_ready", "ktr2"), 1),
                                   (evac_PT2, 4), (expo, 3), (evac_V2, 3), (evac_hT(name, (T2_ps,), "vid_g", "vid_b"), 0),
                                   (evac_OT2, 4), (scaled_rows(QT2, "qtr2", "qg", "qb", "QT2_first"), 1)])
                if name == "f2":
                    def evac_bT(t, u):
                        act.wait_ge(sem("bt_done"), t + 1)
                        after(act, sem("yb_done"), t - 1)
                        a.activation(bitT[u][:, :], bank[:, 0, 0:64].bitcast(BF16), ACT.Copy).then_inc(sem("bT_ready"), 1)

                    bit.run(act, [(evac_bT, 2)])
                if name == "x3":
                    def expo(t, u):
                        act.wait_ge(sem("m3_ready"), 2 * (t + 1))
                        after(act, sem("pt3_done"), t - 1)
                        for b in range(PAIR):
                            half = slice(b * SEQ, (b + 1) * SEQ)
                            ins = a.activation(P3[u % 2][half, half], bank[half, 1, half], ACT.Exp,
                                               bias=sm3[u % 2][half, 0:1], accum_out=sm3[u % 2][half, 1:2])
                            ins.then_inc(sem("exp3"), 1)

                    def sig(t, u):
                        act.wait_ge(sem("g3_done"), t + 1)
                        a.activation(tile(hn, t), bank[:, 0, 0:P], ACT.Tanh, scale=0.5).then_inc(sem("th3"), 1)

                    def evac_PT3(t, u):
                        act.wait_ge(sem("pt3_done"), t + 1)
                        after(act, sem("r3_done"), t - 1)
                        a.activation(PT[u % 2][:, 0:P], bank[:, 2, 0:P], ACT.Copy).then_inc(sem("PT3_ready"), 1)

                    def evac_rT(t, u):
                        act.wait_ge(sem("r3_done"), t + 1)
                        after(act, sem("l3_done"), t - 1)
                        a.activation(OT[u % 2][:, :], bank[:, 3, 0:P], ACT.Copy).then_inc(sem("rT_ready"), 1)

                    def tanh_l(t, u):
                        act.wait_ge(sem("l3_done"), t + 1)
                        after(act, sem("x3_upd"), t - 1)
                        a.activation(hn3[u % 2], bank[:, 4, 0:P], ACT.Tanh).then_inc(sem("hn3"), 1)

                    def evac_h(t, u):
                        act.wait_ge(sem("t1_done"), TB[name] + t + 1)
                        after(act, sem("l3_done"), t - 3)
                        a.activation(hT4[u], TO_ps, ACT.Copy).then_inc(sem("hT_ready"), 1)

                    xl3.run(act, [(evac_PT3, 2), (expo, 1), (evac_rT, 3), (sig, 1), (evac_h, 0), (tanh_l, 4)])
                if name in MOE:
                    affine = ("ln2_w", "ln2_b") if name == "m3" else (None, None)
                    n = MOE.index(name)

                    def evac_z(t, u):
                        act.wait_ge(sem("tc_done"), t + 1)
                        a.activation(toks(zT, t), Z_ps, ACT.Copy).then_inc(sem("z_ready"), 1)

                    pre.run(act, [(evac_hT(name, (TO_ps, TO2_ps), *affine), 0)] + [(evac_z, 3)] * (name == "f0"))
                    act.wait_ge(sem("gate_in"), n + 1)
                    if name == "f1":
                        a.activation(rt[:, :, :], rt[:, :, :], ACT.Exp).then_inc(sem("gate_exp"), 1)
                    else:
                        a.activation(wt[1][:, :], wt[1][:, :], ACT.Exp).then_inc(sem("gate_exp"), 1)
                    for j in range(KTOP[name]):
                        act.wait_ge(sem("hot_ready"), SC[name] + j + 1)
                        hb = hot_blk(j, NBLK[name])
                        a.activation(hb[:, :, 0, :], hb[:, :, 2, :], ACT.Copy, scale=rowid1[:, :]) \
                            .then_inc(sem("row_ids"), 1)
                    base, nb = BB[name], NBLK[name]

                    def evac_xbT(b, u):
                        act.wait_ge(sem("xbT1"), base + b + 1)
                        after(act, sem("h_done"), base + b - 1)
                        if name == "m3":
                            ins = a.activation(xbT[u % 2], TO_ps, ACT.Identity, bias=col("ln2_b"), scale=col("ln2_w"))
                        else:
                            ins = a.activation(xbT[u % 2], TO_ps, ACT.Copy)
                        ins.then_inc(sem("xbT_ready"), 1)

                    def hidden(b, u):
                        act.wait_ge(sem("h_done"), base + b + 1)
                        if name == "m3":
                            after(act, sem("g3_prod"), b - 1)
                            a.activation(G[u % 2][:, 0:HID3], bank[:, u % 2, 0:HID3], ACT.Silu).then_inc(sem("g_act"), 1)
                        else:
                            after(act, sem("gtr_done"), base + b - 1)
                            fn = ACT.Gelu if name == "f0" else ACT.Relu
                            a.activation(G[u % 2][:, :], bank[:, u % 2, :], fn).then_inc(sem("g_act"), 1)

                    def evac_y(b, u):
                        act.wait_ge(sem("yps_done"), base + b + 1)
                        after(act, sem(f"yb_out{u}"), 4 * (base + b - u))
                        a.activation(yb[u], bank[:, 4 + u % 2, 0:C], ACT.Copy).then_inc(sem("yb_ready"), 1)

                    late = blocks_lag(name)
                    Ring(nb, late, 4).run(act, [(evac_xbT, 0), (hidden, 1), (evac_y, late)])

        @block.tensor
        def _(pe):
            mm = nc.tensor.matmul
            pe.wait_ge(sem("pool_ready"), 1)
            pe.wait_ge(sem("first_in"), 16 * FIRST_LOADS)

            def t1(name, *regions):
                def stage(t, u):
                    pe.wait_ge(sem("hs_ready"), TB[name] + t + 1)
                    after(pe, sem("hT_ready"), TB[name] + t - (len(regions) - 1))
                    if name in ATT:
                        after(pe, sem("Vb_ready"), 2 * (ATT[name] + t))
                    if name == "x2":
                        after(pe, sem("sub2"), t - 2)
                    nc.tensor.transpose(regions[u % len(regions)], hs[u % 2][:, :], ident[:, :]).then_inc(sem("t1_done"), 1)
                return stage

            for name in phases():
                phase_start(pe, name)
                if name in ATT:
                    base = ATT[name]
                    wq, wk, wv = {"x0": ("wq0", "wv0", "wv0"), "x1": ("wq1", "wk1", "wv1"), "a3": ("wq3", "wk3", "wv3")}[name]

                    def qkv(t, u):
                        src = hT if name == "a3" else cT
                        pe.wait_ge(sem("hT_ready"), TB[name] + t + 1)
                        mm(Q_ps, sq(wq), hT[u][:, :], start=True, stop=True)
                        if name != "a3":
                            pe.wait_ge(sem("cT_ready"), base + t + 1)
                        mm(K_ps, sq(wk), src[u][:, :], start=True, stop=True)
                        for b in range(PAIR):
                            for half in range(2):
                                v_out = V_ps[half * SEQ:(half + 1) * SEQ, :].rearrange("p (m b f) -> p b m f", b=PAIR, m=GROUPS)
                                ins = mm(v_out[:, b, :, :],
                                         src[u][:, b * SEQ:(b + 1) * SEQ], sq(wv), start=True, stop=True)
                        ins.then_inc(sem("v_done"), 1)

                    def scores(g):
                        def stage(t, u):
                            if g == 0:
                                pe.wait_ge(sem("QT_ready"), base + t + 1)
                                pe.wait_ge(sem("Kb_ready"), base + t + 1)
                                after(pe, sem("sub_first"), base + t)
                            if name == "x1":
                                mm(S_att[:, g, :], pairsel[:, :],
                                   maskrow[:, bass.ds(t, 1), :].to_broadcast([PAIR, HPG, SEQ]), start=True, stop=True,
                                   skip_group_check=True)
                            if name == "a3":
                                mm(S_att[:, g, :], identb[:, :],
                                   causal[:, :].unsqueeze(1).to_broadcast([P, HPG, SEQ]), start=True, stop=True,
                                   skip_group_check=True)
                            rows32 = slice(32 * g, 32 * g + 32)
                            for b in range(PAIR):
                                half = slice(b * SEQ, (b + 1) * SEQ)
                                ins = mm(S_att[half, g, :], QT[u][rows32, half], Kb[u][rows32, :, half],
                                         start=name == "x0", stop=True, skip_group_check=name != "x0")
                            if g == GROUPS // 2 - 1:
                                ins.then_inc(sem("s_first"), 1)
                            if g == GROUPS - 1:
                                ins.then_inc(sem("s_done"), 1)
                        return stage

                    def await_second_half(t, u):
                        after(pe, sem("sub_done"), base + t)

                    def transpose_P(g):
                        def stage(t, u):
                            if g == 0:
                                pe.wait_ge(sem("exp_first"), base + t + 1)
                                after(pe, sem("PT_ready"), 2 * (base + t))
                            if g == GROUPS // 2:
                                pe.wait_ge(sem("exp_done"), base + t + 1)
                            for j in (2 * g, 2 * g + 1):
                                ins = nc.tensor.transpose(PT_ps[:, j * P:(j + 1) * P], Pr[u][:, j * P:(j + 1) * P],
                                                          ident[:, :])
                            if g == GROUPS // 2 - 1:
                                ins.then_inc(sem("pt_first"), 1)
                            if g == GROUPS - 1:
                                ins.then_inc(sem("pt_done"), 1)
                        return stage

                    def values(t, u):
                        pe.wait_ge(sem("PT_ready"), 2 * (base + t + 1))
                        pe.wait_ge(sem("Vb_ready"), 2 * (base + t + 1))
                        after(pe, sem("O_ready"), base + t)
                        for r in range(2):
                            for m in range(GROUPS):
                                f32 = slice(32 * m, 32 * m + 32)
                                mm(sum_ps[f32, :], headsum[:, r, :, :, :].rearrange("p q h d -> p (q h d)"),
                                   PT[u][:, (2 * m + r) * P:(2 * m + r + 1) * P], start=r == 0, stop=r == 1,
                                   skip_group_check=True)
                        for b in range(PAIR):
                            for r in range(2):
                                for m in range(GROUPS):
                                    f32 = slice(32 * m, 32 * m + 32)
                                    col0 = (2 * m + r) * P + b * SEQ
                                    ins = mm(O_ps[f32, b * SEQ:(b + 1) * SEQ],
                                             Vb[u][:, 2 * m + b, 2 * r:2 * r + 2, :, :].rearrange("p q h d -> p (q h d)"),
                                             PT[u][:, col0:col0 + SEQ], start=r == 0, stop=r == 1, skip_group_check=True)
                        ins.then_inc(sem("pv_done"), 1)

                    def project(t, u):
                        pe.wait_ge(sem("O_ready"), base + t + 1)
                        if name == "x0":
                            nc.tensor.transpose(OY_ps, OT[u][:, :], ident[:, :]).then_inc(sem("y_done"), 1)
                            return
                        i = {"x1": 1, "a3": 3}[name]
                        mm(OY_ps, OT[u][:, :], sq(f"wo{i}"), start=True, stop=False)
                        mm(OY_ps, part_rows[:, :], row(f"bo{i}"), start=False, stop=True).then_inc(sem("y_done"), 1)

                    att.run(pe, [(values, 3), (scores(0), 1), (scores(1), 1), (transpose_P(0), 2), (await_second_half, 1),
                                 (t1(name, TO_ps), 0), (scores(2), 1), (transpose_P(1), 2), (transpose_P(2), 2),
                                 (scores(3), 1), (transpose_P(3), 2), (qkv, 0), (project, 3)])
                if name == "x2":
                    pe.wait_ge(sem("w_in2"), 16 * 4)

                    def both(rows, n):
                        after(pe, sem(rows + "_first"), n)
                        after(pe, sem(rows + "_second"), n)

                    def proj_Q(t, u):
                        pe.wait_ge(sem("hT_ready"), TB[name] + t + 1)
                        after(pe, sem("Vs_ready"), t - 2)
                        for k in range(2):
                            ins = mm(A2[:, k, :], hT[u][:, :], wq2[:, k * 384:(k + 1) * 384], start=True, stop=True)
                        ins.then_inc(sem("q2_done"), 1)

                    def proj_K(t, u):
                        pe.wait_ge(sem("cT_ready"), 2 * NT + t + 1)
                        after(pe, sem("OT2_ready"), t - 3)
                        for k in range(2):
                            ins = mm(B2[:, k, :], cT[u][:, :], wk2[:, k * 384:(k + 1) * 384], start=True, stop=True)
                        ins.then_inc(sem("k2_done"), 1)

                    def proj_V(t, u):
                        pe.wait_ge(sem("cV2_ready"), t + 1)
                        pe.wait_ge(sem("qn_ready"), upto(t + 3, NT))
                        for b in range(PAIR):
                            for hf in range(2):
                                ins = mm(A2[hf * SEQ:(hf + 1) * SEQ, b, :], cV2[u][:, b * SEQ:(b + 1) * SEQ],
                                         wv2[:, :].rearrange("c (m f n) -> c m f n", f=2, n=P)[:, :, hf, :],
                                         start=True, stop=True)
                        ins.then_inc(sem("v2_done"), 1)

                    def transpose_rows(src, ready, freed, done):
                        def stage(t, u):
                            pe.wait_ge(sem(ready), t + 1)
                            freed(t)
                            for i in range(CH2):
                                ins = nc.tensor.transpose(C2[:, i // 3, (i % 3) * P:(i % 3 + 1) * P],
                                                          src[u][:, i * P:(i + 1) * P], ident[:, :])
                            ins.then_inc(sem(done), 1)
                        return stage

                    def await_scores2(t, u):
                        both("KT2", t + 1)
                        after(pe, sem("sub2"), t)
                        pe.wait_ge(sem("hT_ready"), TB[name] + upto(t + 3, NT))
                        after(pe, sem("x2_upd"), t - 1)

                    def scores2(t, u):
                        for i in range(CH2):
                            for p in range(2):
                                for b in range(PAIR):
                                    half = slice(b * SEQ, (b + 1) * SEQ)
                                    hrow = slice(p * DH2, (p + 1) * DH2)
                                    tok = slice(i * P + b * SEQ, i * P + (b + 1) * SEQ)
                                    ins = mm(D2[half, p, i * SEQ:(i + 1) * SEQ], QT2[u][hrow, tok], KT2[u][hrow, tok],
                                             start=True, stop=True)
                        ins.then_inc(sem("s2_done"), 1)

                    def values2(t, u):
                        pe.wait_ge(sem("pool_ready"), 1)
                        pe.wait_ge(sem("PT2_ready"), t + 1)
                        pe.wait_ge(sem("Vs_ready"), t + 1)
                        pe.wait_ge(sem("kn_ready"), upto(t + 4, NT))
                        for i in range(CH2):
                            for p in range(2):
                                m, hf = i // 2, i % 2
                                for b in range(PAIR):
                                    krow = slice(hf * SEQ, (hf + 1) * SEQ)
                                    vcol = m * P + p * DH2
                                    pcol = (p * 3 + m) * P + b * SEQ
                                    ins = mm(B2[p * DH2:(p + 1) * DH2, i % 2, (i // 2) * P + b * SEQ:(i // 2) * P + (b + 1) * SEQ],
                                             Vs[u][krow, b, vcol:vcol + DH2], PT[u][krow, pcol:pcol + SEQ],
                                             start=True, stop=True)
                        ins.then_inc(sem("ot2_done"), 1)

                    def project2(t, u):
                        pe.wait_ge(sem("OT2_ready"), t + 1)
                        pe.wait_ge(sem("sub2"), upto(t + 2, NT))
                        after(pe, sem("x2_upd"), t)
                        for i in range(CH2):
                            mm(Y2_ps, OT2[u][:, 3 * (i % 2) + i // 2, :], wo2[:, i, :], start=i == 0, stop=False)
                        mm(Y2_ps, part_rows[:, :], row("bo2"), start=False, stop=True).then_inc(sem("y2_done"), 1)

                    def rows_free(t):
                        both("KT2", t)
                        after(pe, sem("PT2_ready"), t - 2)

                    att2.run(pe, [
                        (project2, 5), (proj_Q, 1), (proj_K, 1), (await_scores2, 3),
                        (transpose_rows(kn, "kn_ready", lambda t: both("QT2", t + 1), "ktr2"), 2),
                        (scores2, 3),
                        (transpose_rows(Pr, "pn2", lambda t: both("KT2", upto(t + 3, NT)), "ptr2"), 4),
                        (proj_V, 3), (t1(name, T2_ps), 0), (values2, 4),
                        (transpose_rows(qn, "qn_ready", rows_free, "qtr2"), 1)])
                if name == "f2":
                    pe.wait_ge(sem("wabs"), 1)
                    mm(bank[:, 7, 0:1], ones[:, :], wstat[:, 0:1], start=True, stop=True).then_inc(sem("wsum"), 1)
                    pe.wait_ge(sem("wbit_ready"), 1)

                    def tb(t, u):
                        pe.wait_ge(sem("bitq_ready"), t + 1)
                        after(pe, sem("bT_ready"), t)
                        nc.tensor.transpose(bank[:, 0, 0:64].bitcast(BF16), bitq[u][:, :], identb[:, :]) \
                            .then_inc(sem("bt_done"), 1)

                    def yb_(t, u):
                        pe.wait_ge(sem("bT_ready"), t + 1)
                        after(pe, sem("xb_upd"), t)
                        mm(bank[:, 1, 0:C], bitT[u][:, :], wbit[:, :], start=True, stop=True).then_inc(sem("yb_done"), 1)

                    bit.run(pe, [(tb, 2), (yb_, 3)])
                if name == "x3":
                    def gate_scores(t, u):
                        pe.wait_ge(sem("hT_ready"), TB[name] + t + 1)
                        after(pe, sem("th3"), t)
                        mm(bank[:, 0, 0:P], hT4[u], sq("w_gate"), start=True, stop=False)
                        mm(bank[:, 0, 0:P], part_rows[:, :], row("b_gate"), start=False, stop=True).then_inc(sem("g3_done"), 1)
                        after(pe, sem("exp3"), 2 * t)
                        mm(bank[:, 1, 0:P], hT4[u], toks(ctxT, t), start=True, stop=True).then_inc(sem("s3_done"), 1)

                    def pt3(t, u):
                        pe.wait_ge(sem("pn3"), t + 1)
                        after(pe, sem("PT3_ready"), t)
                        nc.tensor.transpose(bank[:, 2, 0:P], P3[u % 2][:, :], ident[:, :]).then_inc(sem("pt3_done"), 1)

                    def r3(t, u):
                        pe.wait_ge(sem("PT3_ready"), t + 1)
                        pe.wait_ge(sem("cs3_ready"), t + 1)
                        after(pe, sem("rT_ready"), t)
                        mm(bank[:, 3, 0:P], cT[u % 2][:, :], PT[u % 2][:, 0:P], start=True, stop=True).then_inc(sem("r3_done"), 1)

                    def l3(t, u):
                        pe.wait_ge(sem("rT_ready"), t + 1)
                        after(pe, sem("hn3"), t)
                        mm(bank[:, 4, 0:P], OT[u % 2][:, :], sq("w_lin_r"), start=True, stop=False)
                        mm(bank[:, 4, 0:P], hT4[u], sq("w_lin_h"), start=False, stop=False)
                        mm(bank[:, 4, 0:P], part_rows[:, :], row("b_lin"), start=False, stop=True).then_inc(sem("l3_done"), 1)

                    xl3.run(pe, [(pt3, 2), (gate_scores, 1), (r3, 3), (t1(name, TO_ps), 0), (l3, 4)])
                if name in MOE:
                    k = MOE.index(name)

                    def logits(t, u):
                        pe.wait_ge(sem("hT_ready"), TB[name] + t + 1)
                        after(pe, sem("lg_ready"), ROUTE[name] + t)
                        mm(L_ps, hT[u % 2][:, :], rw[:, k, :], start=True, stop=True).then_inc(sem("lg_done"), 1)

                    def t1_ctx(t, u):
                        pe.wait_ge(sem("hc_ready"), t + 1)
                        after(pe, sem("z_ready"), t)
                        nc.tensor.transpose(Z_ps, hc[u % 2][:, :], ident[:, :]).then_inc(sem("tc_done"), 1)

                    pre.run(pe, [(t1(name, TO_ps, TO2_ps), 0)] + [(t1_ctx, 3)] * (name == "f0") + [(logits, 1)])
                    pe.wait_ge(sem("oh_ready"), k + 1)
                    ohf = ohs[:, :, :].rearrange("p t e -> p (t e)")
                    mm(bank[:, 0, 0:P], before[:, :], ohf, start=True, stop=True)
                    mm(bank[:, 1, 0:P], ones[:, :], ohf, start=True, stop=True).then_inc(sem("count_done"), 1)
                    nb = NBLK[name]
                    for j in range(KTOP[name]):
                        pe.wait_ge(sem("tiles_hot"), SC[name] + j + 1)
                        pe.wait_ge(sem("row_ids"), SC[name] + j + 1)
                        for t in range(NT):
                            ins = mm(tab_ps[:, 0:2 * nb].rearrange("p (v b) -> p v b", v=2), hot_row[j][:, t, :],
                                     hot_blk(j, nb)[:, t, 0:2, :], start=j == 0 and t == 0,
                                     stop=j == KTOP[name] - 1 and t == NT - 1)
                    ins.then_inc(sem("table_done"), 1)
                    pe.wait_ge(sem("slots_ready"), k + 1)
                    pe.wait_ge(sem("moe_w"), 16 * (18 if k < 2 else 28))
                    base, nb = BB[name], NBLK[name]
                    nj = (HJ if k < 2 else HID3 // P)

                    def expert(b, u):
                        if name == "f1":
                            return (b - u % 2) * (nj * C // 2)
                        e = nc.tensor.value_load(blke[0:1, bass.ds(b, 1)], min_val=0, max_val=NE - 1)
                        return e * (nj * C)

                    def tblk(b, u):
                        pe.wait_ge(sem(f"xb_in{u}"), 4 * (base + b - u) + 16)
                        after(pe, sem("xbT_ready"), base + b)
                        nc.tensor.transpose(TO_ps, xb[u], ident[:, :]).then_inc(sem("xbT1"), 1)

                    def hid(b, u):
                        off = expert(b, u) * (HID // (nj * C))
                        pe.wait_ge(sem("xbT_ready"), base + b + 1)
                        mm(bank[:, u % 2, :], xbT[u % 2], w1[k][:, bass.ds(off, HID)], start=True, stop=True) \
                            .then_inc(sem("h_done"), 1)

                    def tg(b, u):
                        src_g = G3 if name == "m3" else G
                        pe.wait_ge(sem("g3_prod" if name == "m3" else "g_act"), (0 if name == "m3" else base) + b + 1)
                        for j in range(nj):
                            ins = nc.tensor.transpose(bank[:, 2 + u % 2, j * P:(j + 1) * P], src_g[u % 2][:, j * P:(j + 1) * P],
                                                      ident[:, :])
                        ins.then_inc(sem("gtr_done"), 1)

                    def down(b, u):
                        off = expert(b, u)
                        pe.wait_ge(sem("GT_ready"), base + b + 1)
                        after(pe, sem("yb_ready"), base + b - 1)
                        for j in range(nj):
                            ins = mm(bank[:, 4 + u % 2, 0:C], GT[u % 2][:, j * P:(j + 1) * P], w2[k][:, bass.ds(off + j * C, C)],
                                     start=j == 0, stop=j == nj - 1)
                        ins.then_inc(sem("yps_done"), 1)

                    late = blocks_lag(name)
                    def fourth(stage):
                        return lambda b, u: stage(b, u % 4)

                    Ring(nb, late, 8).run(pe, [(fourth(tblk), 0), (fourth(tg), late - 1), (fourth(hid), 1),
                                               (fourth(down), late)])

        @block.vector
        def _(dve):
            v = nc.vector
            chain = [0]

            def link(ins):
                chain[0] += 1
                ins.then_inc(sem("dve_chain"), 1)
                dve.wait_ge(sem("dve_chain"), chain[0])

            def tile_stats(src, t):
                v.bn_stats(tile(st, t), tile(src, t)).then_inc(sem("bn_done"), 1)

            def next_stats(name, src, updated, base=0):
                done = []

                def stage(t, u):
                    dve.wait_ge(sem(updated), base + t + 1)
                    tile_stats(src, t)
                    if isinstance(t, int) and t >= EARLY and not done and name != phases()[-1]:
                        done.append(t)
                        row_scales(PH[PHI[name] + 1], "early")
                return stage

            parts = [0]

            def row_scales(name, part):
                ts = TILES_OF[part]
                mn, sums = (meanc, st_ctx) if name == "ctx" else (mean, st)
                if name == "ctx":
                    dve.wait_ge(sem("ctx_summed"), NT)
                    dve.wait_ge(sem("rstd_ready"), POWS["f0", "late"])
                else:
                    dve.wait_ge(sem("bn_done"), NT * STATS.index(name) + ts.stop)
                parts[0] += 3
                v.tensor_tensor(st_a[:, ts], sums[:, ts, 1], sums[:, ts, 4], ALU.add).then_inc(sem("st_parts"), 1)
                v.tensor_tensor(st_b[:, ts], sums[:, ts, 1], sums[:, ts, 4], ALU.subtract).then_inc(sem("st_parts"), 1)
                v.tensor_tensor(st_c[:, ts], sums[:, ts, 2], sums[:, ts, 5], ALU.add).then_inc(sem("st_parts"), 1)
                dve.wait_ge(sem("st_parts"), parts[0])
                link(v.tensor_scalar(mn[:, ts], st_a[:, ts], 0.5, None, ALU.mult))
                link(v.scalar_tensor_tensor(st_b[:, ts], st_b[:, ts], 0.25, st_b[:, ts], ALU.mult, ALU.mult))
                link(v.scalar_tensor_tensor(var[:, ts], st_c[:, ts], 1.0 / C, st_b[:, ts], ALU.mult, ALU.add))
                if name in TWICE:
                    link(v.tensor_scalar(veps1[:, ts], var[:, ts], LN_EPS, None, ALU.add))
                    v.scalar_tensor_tensor(veps[:, ts], veps1[:, ts], LN_EPS, var[:, ts], ALU.mult, ALU.add) \
                        .then_inc(sem("var_ready"), 1)
                else:
                    v.tensor_scalar(veps[:, ts], var[:, ts], LN_EPS, None, ALU.add).then_inc(sem("var_ready"), 1)

            def await_scales(name, t):
                part = "all" if name == "x0" else "early" if isinstance(t, int) and t < EARLY else "late"
                dve.wait_ge(sem("rstd_ready"), POWS[name, part])

            def late_scales(name, t):
                if name != "x0" and isinstance(t, int) and t == 0:
                    row_scales(name, "late")
                    if name == "f0":
                        row_scales("ctx", "all")

            def norm(name, xs, also=None):
                def stage(t, u):
                    await_scales(name, t)
                    after(dve, sem("t1_done"), TB[name] + t - 1)
                    if also:
                        after(dve, sem(also[0]), also[1] + t - 1)
                    v.tensor_scalar(hs[u % 2][:, :], tile(xs, t), at(mean, t), at(rs, t), ALU.subtract, ALU.mult) \
                        .then_inc(sem("hs_ready"), 1)
                    late_scales(name, t)
                return stage

            def gx(layer):
                return gates[:, layer:layer + 1]

            def gf(layer):
                return gates[:, 4 + layer:5 + layer]


            def mask_rows():
                link(v.tensor_copy(maskf[:, :, :].rearrange("b t s -> b (t s)"),
                                   maskraw[:, :, :].rearrange("b t s -> b (t s)").bitcast(U8)))
                link(v.tensor_reduce(maskall[:, :], maskf[:, :, :], AX.X, ALU.min))
                link(v.tensor_tensor(maskf[:, :, 0], maskf[:, :, 0], maskall[:, :], ALU.subtract))
                link(v.tensor_scalar(maskrow[:, :, :], maskf[:, :, :], NEG, None, ALU.mult))

            def split_rows():
                link(v.tensor_copy(row_parts[:, :, :], rows[:, :, :]))
                for p in PART[1:]:
                    link(v.tensor_tensor(rows[p:P, :, :], rows[p:P, :, :], row_parts[p:P, :, :], ALU.subtract))
                    link(v.tensor_copy(row_parts[p:P, :, :], rows[p:P, :, :]))

            for name in phases():
                phase_start(dve, name)
                xs = y3 if name == "m3" else x
                if name == "x0":
                    for q in range(4):
                        dve.wait_ge(sem(f"x_in{q}"), 16)
                        for t in range(q * NT // 4, (q + 1) * NT // 4):
                            tile_stats(x, t)
                    row_scales(name, "all")
                if name == "x0":
                    dve.wait_ge(sem("pool_ready"), 1)
                    dve.wait_ge(sem("first_in"), 16 * FIRST_LOADS)
                    dve.wait_ge(sem("gates_ready"), 1)
                if name in ATT:
                    base = ATT[name]
                    bias_k = {"x0": "bk0", "x1": "bk1", "a3": None}[name]
                    bias_v = {"x0": 0, "x1": 1, "a3": None}[name]

                    def keys(t, u):
                        dve.wait_ge(sem("QT_ready"), base + t + 1)
                        after(dve, sem("s_done"), base + t - 1)
                        src_k = K_ps.unsqueeze(1).to_broadcast([P, HPG, P])
                        sel = headmask[:, :].unsqueeze(2).to_broadcast([P, HPG, P])
                        v.scalar_tensor_tensor(Kb[u][:, :, :], src_k, col(bias_k) if bias_k else 0.0, sel,
                                               ALU.add, ALU.mult).then_inc(sem("Kb_ready"), 1)

                    def vals(t, u):
                        dve.wait_ge(sem("QT_ready"), base + t + 1)
                        after(dve, sem("pv_done"), base + t - 1)
                        for half in range(2):
                            r = slice(half * SEQ, (half + 1) * SEQ)
                            src_v = V_ps[r, :].rearrange("p (mb q h d) -> p mb q h d", q=2, h=2, d=HD)[:, :, :, half, :]
                            dst = Vb[u][r, :, 0:4:3, half, :]
                            if bias_v is None:
                                ins = v.tensor_copy(dst, src_v)
                            else:
                                bb = bvB[r, bias_v, :, :, :].rearrange("p m b (q h d) -> p (m b) q h d", q=2, h=2)
                                ins = v.tensor_tensor(dst, src_v, bb[:, :, :, half, :], ALU.add)
                            ins.then_inc(sem("Vb_ready"), 1)

                    def half_scores(h):
                        gs = slice(h * GROUPS // 2, (h + 1) * GROUPS // 2)
                        return gs, S_att[:, gs, :].rearrange("p g (h k) -> p g h k", h=HPG)

                    def row_max(h):
                        def stage(t, u):
                            gs, part = half_scores(h)
                            dve.wait_ge(sem("s_done" if h else "s_first"), base + t + 1)
                            v.tensor_reduce(mx[u][:, :].rearrange("p (g h) -> p g h", g=GROUPS)[:, gs, :], part,
                                            AX.X, ALU.max).then_inc(sem("mx_ready" if h else "mx_first"), 1)
                        return stage

                    def subtract(h):
                        def stage(t, u):
                            gs, part = half_scores(h)
                            dve.wait_ge(sem("mx_ready" if h else "mx_first"), base + t + 1)
                            if h == 0:
                                after(dve, sem("pt_done"), base + t - 1)
                            mb = mx[u][:, :].rearrange("p (g h) -> p g h", g=GROUPS)[:, gs, :].unsqueeze(3) \
                                .to_broadcast([P, GROUPS // 2, HPG, SEQ])
                            v.tensor_tensor(Pr[u][:, :].rearrange("p (g h k) -> p g h k", g=GROUPS, h=HPG)[:, gs, :, :],
                                            part, mb, ALU.subtract).then_inc(sem("sub_done" if h else "sub_first"), 1)
                        return stage

                    def normalise(t, u):
                        dve.wait_ge(sem("pv_done"), base + t + 1)
                        after(dve, sem("y_done"), base + t - 1)
                        v.reciprocal(rsum[u], sum_ps).then_inc(sem("rinv_ready"), 1)
                        dve.wait_ge(sem("rinv_ready"), base + t + 1)
                        v.tensor_tensor(OT[u][:, :], O_ps, rsum[u], ALU.mult).then_inc(sem("O_ready"), 1)

                    def update(t, u):
                        dve.wait_ge(sem("y_done"), base + t + 1)
                        dve.wait_ge(sem("pv_done"), base + upto(t + 2, NT))
                        if name == "a3":
                            ins = v.tensor_tensor(tile(y3, t), OY_ps, tile(y3, t), ALU.add)
                        else:
                            ins = v.scalar_tensor_tensor(tile(x, t), OY_ps, gx({"x0": 0, "x1": 1}[name]), tile(x, t),
                                                         ALU.mult, ALU.add)
                        ins.then_inc(sem("x_upd"), 1)

                    def keep_rows(t, u):
                        v.tensor_scalar(tile(y3, t), tile(x, t), at(mean, t), at(rs1, t), ALU.subtract, ALU.mult) \
                            .then_inc(sem("y3_kept"), 1)

                    def update3(t, u):
                        dve.wait_ge(sem("y3_kept"), t + 1)
                        update(t, u)

                    def ctx_stats(t, u):
                        dve.wait_ge(sem("ctx_in"), 16)
                        v.bn_stats(tile(st_ctx, t), tile(ctxn, t)).then_inc(sem("ctx_summed"), 1)

                    a3 = name == "a3"
                    att.run(dve, [(norm(name, xs), 0), (row_max(1), 2), (keys, 1), (subtract(1), 2), (vals, 1)]
                            + [(keep_rows, 0)] * a3
                            + [(update3 if a3 else update, 4), (normalise, 3), (row_max(0), 1),
                               (next_stats(name, y3 if a3 else x, "x_upd", base), 4), (subtract(0), 1)]
                            + [(ctx_stats, 4)] * (name == "x0"))
                    dve.wait_ge(sem("x_upd"), base + NT)
                    v.engine_nop().then_inc(sem("phase_done"), 1)
                if name == "x2":
                    def bn_rows(ps, stt, mv, done, ready, var_sem):
                        def stage(t, u):
                            dve.wait_ge(sem(done), t + 1)
                            after(dve, sem(ready), t - 1)
                            for k in range(2):
                                v.bn_stats(stt[u][:, k, :], ps[:, k, :]).then_inc(sem(var_sem + "_c"), 1)
                            dve.wait_ge(sem(var_sem + "_c"), 4 * t + 2)
                            v.memset(aggr_gap[:, :], 0.0)
                            v.bn_aggr(mv[u][:, :], stt[u][:, :, :].rearrange("p k s -> p (k s)")) \
                                .then_inc(sem(var_sem + "_c"), 1)
                            dve.wait_ge(sem(var_sem + "_c"), 4 * t + 3)
                            v.tensor_scalar(mv[u][:, 0:1], mv[u][:, 0:1], -1.0, None, ALU.mult) \
                                .then_inc(sem(var_sem + "_c"), 1)
                            v.tensor_scalar(mv[u][:, 1:2], mv[u][:, 1:2], LN_EPS, None, ALU.add).then_inc(sem(var_sem), 1)
                            dve.wait_ge(sem(var_sem + "_c"), 4 * t + 4)
                        return stage

                    def scaled_rows(dst, done, gain, shift, ready):
                        def stage(t, u):
                            dve.wait_ge(sem(done), t + 1)
                            after(dve, sem("s2_done"), t - 1)
                            for i in range(CH2 // 2, CH2):
                                ins = v.tensor_scalar(dst[u][:, i * P:(i + 1) * P], C2[:, 1, (i - 3) * P:(i - 2) * P],
                                                      col(f"{gain}{i}"), col(f"{shift}{i}"), ALU.mult, ALU.add)
                            ins.then_inc(sem(ready), 1)
                        return stage

                    def s4b():
                        return D2.rearrange("p a (i k) -> p a i k", k=SEQ)

                    def row_max2(t, u):
                        dve.wait_ge(sem("s2_done"), t + 1)
                        v.tensor_reduce(mx[u][:, 0:H2].rearrange("p (a i) -> p a i", a=2), s4b(), AX.X, ALU.max) \
                            .then_inc(sem("mx2"), 1)
                        dve.wait_ge(sem("mx2"), t + 1)
                        after(dve, sem("ptr2"), t - 1)
                        mb = mx[u][:, 0:H2].rearrange("p (a i) -> p a i", a=2).unsqueeze(3).to_broadcast([P, 2, CH2, SEQ])
                        v.tensor_tensor(Pr[u][:, 0:INNER].rearrange("p (a i k) -> p a i k", a=2, i=CH2), s4b(), mb,
                                        ALU.subtract).then_inc(sem("sub2"), 1)

                    def sums2(t, u):
                        dve.wait_ge(sem("exp2"), t + 1)
                        v.tensor_reduce(mx[u][:, 0:H2], Pr[u][:, 0:INNER].rearrange("p (h k) -> p h k", h=H2), AX.X,
                                        ALU.add).then_inc(sem("sum2"), 1)
                        dve.wait_ge(sem("sum2"), t + 1)
                        after(dve, sem("pn2"), t - 1)
                        v.reciprocal(rinv[u][:, 0:H2], mx[u][:, 0:H2]).then_inc(sem("rinv2"), 1)

                    def update2(t, u):
                        dve.wait_ge(sem("y2_done"), t + 1)
                        v.scalar_tensor_tensor(tile(x, t), Y2_ps, gx(2), tile(x, t), ALU.mult, ALU.add) \
                            .then_inc(sem("x2_upd"), 1)

                    att2.run(dve, [(update2, 5), (bn_rows(A2, qst, qmv, "q2_done", "qn_ready", "qvar"), 1),
                                   (bn_rows(B2, kst, kmv, "k2_done", "kn_ready", "kvar"), 1),
                                   (scaled_rows(KT2, "ktr2", "kg", "kb", "KT2_second"), 2), (row_max2, 3),
                                   (norm(name, xs), 0), (next_stats(name, x, "x2_upd"), 5), (sums2, 3),
                                   (scaled_rows(QT2, "qtr2", "qg", "qb", "QT2_second"), 1)])
                    dve.wait_ge(sem("x2_upd"), NT)
                    v.engine_nop().then_inc(sem("phase_done"), 1)
                if name == "f2":
                    link(v.tensor_reduce(wstat[:, 0:1], sq("w_bitT"), AX.X, ALU.add, apply_absolute_value=True))
                    v.engine_nop().then_inc(sem("wabs"), 1)
                    dve.wait_ge(sem("wsum"), 1)
                    link(v.tensor_scalar(wstat[:, 1:2], bank[:, 7, 0:1], 1.0 / (C * C), BIT_EPS, ALU.mult, ALU.add))
                    link(v.reciprocal(wstat[:, 2:3], wstat[:, 1:2]))
                    link(v.tensor_scalar(wbtmp[:, :], sq("w_bitT"), wstat[:, 2:3], ROUND, ALU.mult, ALU.add))
                    link(v.tensor_scalar(wbtmp[:, :], wbtmp[:, :], ROUND, -1.0, ALU.subtract, ALU.max))
                    v.tensor_scalar(wbit[:, :], wbtmp[:, :], 1.0, None, ALU.min).then_inc(sem("wbit_ready"), 1)
                    link(v.scalar_tensor_tensor(wstat[:, 3:4], wstat[:, 1:2], 1.0 / 127.0, gf(2), ALU.mult, ALU.mult))

                    def normb(t, u):
                        await_scales(name, t)
                        after(dve, sem("bitq_ready"), t - 1)
                        v.tensor_scalar(hs[u][:, :], tile(x, t), at(mean, t), at(rs, t), ALU.subtract, ALU.mult) \
                            .then_inc(sem("bit_rows"), 1)
                        late_scales(name, t)

                    def step(waits, freed, done, make):
                        def stage(t, u):
                            dve.wait_ge(sem(waits), t + 1)
                            if freed:
                                after(dve, sem(freed), t - 1)
                            make(t, u).then_inc(sem(done), 1)
                        return stage

                    def whole(u):
                        return hs[u][:, :]

                    largest = step("bit_rows", None, "bit_max", lambda t, u: v.tensor_reduce(
                        at(row_max_, t), whole(u), AX.X, ALU.max, apply_absolute_value=True))
                    scale = step("bit_max", None, "bit_scale", lambda t, u: v.tensor_scalar(
                        at(row_scale, t), at(row_max_, t), BIT_EPS, None, ALU.add))
                    invert = step("bit_scale", None, "bit_inv", lambda t, u: v.reciprocal(at(row_inv, t), at(row_scale, t)))
                    scale_out = step("bit_scale", None, "bit_out", lambda t, u: v.tensor_tensor(
                        at(out_scale, t), at(row_scale, t), wstat[:, 3:4], ALU.mult))
                    stretch = step("bit_inv", None, "bit_z", lambda t, u: v.tensor_scalar(
                        whole(u), whole(u), at(row_inv, t), 127.0, ALU.mult, ALU.mult))
                    round_ = step("bit_z", None, "bit_round", lambda t, u: v.tensor_scalar(
                        whole(u), whole(u), 127.0, ROUND, ALU.min, ALU.add))
                    clip = step("bit_round", "bt_done", "bitq_ready", lambda t, u: v.tensor_scalar(
                        bitq[u][:, :], whole(u), ROUND, -128.0, ALU.subtract, ALU.max))

                    def updateb(t, u):
                        dve.wait_ge(sem("yb_done"), t + 1)
                        dve.wait_ge(sem("bit_out"), t + 1)
                        v.scalar_tensor_tensor(tile(x, t), bank[:, 1, 0:C], at(out_scale, t), tile(x, t), ALU.mult,
                                               ALU.add).then_inc(sem("xb_upd"), 1)

                    bit.run(dve, [(largest, 1), (stretch, 2), (scale, 1), (round_, 2), (invert, 1), (scale_out, 1), (clip, 2),
                                  (updateb, 4), (normb, 0), (next_stats(name, x, "xb_upd"), 4)])
                    dve.wait_ge(sem("xb_upd"), NT)
                    v.engine_nop().then_inc(sem("phase_done"), 1)
                if name == "x3":
                    def max3(t, u):
                        dve.wait_ge(sem("s3_done"), t + 1)
                        after(dve, sem("exp3"), 2 * (t - 1))
                        for b in range(PAIR):
                            half = slice(b * SEQ, (b + 1) * SEQ)
                            v.tensor_reduce(sm3[u % 2][half, 0:1], bank[half, 1, half], AX.X, ALU.max, negate=True) \
                                .then_inc(sem("m3_ready"), 1)

                    def norm3(t, u):
                        dve.wait_ge(sem("exp3"), 2 * (t + 1))
                        v.reciprocal(sm3[u % 2][:, 2:3], sm3[u % 2][:, 1:2]).then_inc(sem("r3inv"), 1)
                        dve.wait_ge(sem("r3inv"), t + 1)
                        v.tensor_scalar(P3[u % 2][:, :], P3[u % 2][:, :], sm3[u % 2][:, 2:3], None, ALU.mult).then_inc(sem("pn3"), 1)

                    def update3x(t, u):
                        c = sem("x3_chain")
                        dve.wait_ge(sem("hn3"), t + 1)
                        dve.wait_ge(sem("hs_kept"), t + 1)
                        v.scalar_tensor_tensor(hn3[u % 2], hn3[u % 2], at(pw, t), tile(y3, t), ALU.mult, ALU.subtract) \
                            .then_inc(c, 1)
                        dve.wait_ge(sem("th3"), t + 1)
                        v.tensor_scalar(tile(hn, t), tile(hn, t), 0.5, 0.5, ALU.mult, ALU.add).then_inc(c, 1)
                        dve.wait_ge(c, 4 * t + 2)
                        v.tensor_tensor(tmp3[u % 2], tile(hn, t), hn3[u % 2], ALU.mult).then_inc(c, 1)
                        dve.wait_ge(c, 4 * t + 3)
                        v.tensor_tensor(tmp3[u % 2], tmp3[u % 2], tile(y3, t), ALU.add).then_inc(c, 1)
                        dve.wait_ge(c, 4 * t + 4)
                        v.scalar_tensor_tensor(tile(x, t), tmp3[u % 2], gx(3), tile(x, t), ALU.mult, ALU.add) \
                            .then_inc(sem("x3_upd"), 1)

                    xl3.run(dve, [(norm(name, xs, ("hs_kept", 0)), 0), (max3, 1), (update3x, 5), (norm3, 1), (next_stats(name, x, "x3_upd"), 5)])
                    dve.wait_ge(sem("x3_upd"), NT)
                    v.engine_nop().then_inc(sem("phase_done"), 1)
                if name in MOE:
                    k = MOE.index(name)

                    def take_logits(t, u):
                        dve.wait_ge(sem("lg_done"), ROUTE[name] + t + 1)
                        v.tensor_copy(tile(lg, t), L_ps).then_inc(sem("lg_ready"), 1)

                    def norm_ctx(t, u):
                        dve.wait_ge(sem("rstd_ready"), POWS["ctx", "all"])
                        after(dve, sem("tc_done"), t - 1)
                        v.tensor_scalar(hc[u % 2][:, :], tile(ctxn, t), at(meanc, t), at(rsc, t), ALU.subtract, ALU.mult) \
                            .then_inc(sem("hc_ready"), 1)

                    pre.run(dve, [(norm(name, xs, ("hn_kept", ROUTE[name])), 0)] + [(norm_ctx, 3)] * (name == "f0")
                            + [(take_logits, 2)])
                    dve.wait_ge(sem("lg_ready"), ROUTE[name] + NT)

                    def over_e(m):
                        return m.unsqueeze(2).to_broadcast([P, NT, NE])

                    def over_t(m):
                        return m.unsqueeze(1).to_broadcast([P, NT, NE])

                    def first_max(scores, best, onehot):
                        link(v.tensor_reduce(best[:, :], scores[:, :, :], AX.X, ALU.max))
                        link(v.tensor_tensor(rt[:, :, :], scores[:, :, :], over_e(best[:, :]), ALU.is_equal))
                        link(v.tensor_tensor(rt[:, :, :], rt[:, :, :], over_t(blk[:, 3, :]), ALU.mult))
                        link(v.tensor_reduce(rk[:, :], rt[:, :, :], AX.X, ALU.max))
                        link(v.tensor_tensor(onehot[:, :, :], over_t(blk[:, 3, :]), over_e(rk[:, :]), ALU.is_equal))

                    link(v.tensor_scalar(blk[:, 3, :], iota8[:, :], -1.0, float(NE), ALU.mult, ALU.add))
                    first_max(lg, rm[0], oh[0])
                    if KTOP[name] == 2:
                        link(v.scalar_tensor_tensor(lg2[:, :, :], oh[0][:, :, :], NEG, lg[:, :, :], ALU.mult, ALU.add))
                        first_max(lg2, rm[1], oh[1])
                        link(v.tensor_tensor(ohs[:, :, :], oh[0][:, :, :], oh[1][:, :, :], ALU.add))
                        v.engine_nop().then_inc(sem("oh_ready"), 1)
                        v.tensor_tensor(wt[1][:, :], rm[1][:, :], rm[0][:, :], ALU.subtract).then_inc(sem("gate_in"), 1)
                    else:
                        link(v.tensor_copy(ohs[:, :, :], oh[0][:, :, :]))
                        v.engine_nop().then_inc(sem("oh_ready"), 1)
                        v.tensor_tensor(rt[:, :, :], lg[:, :, :], over_e(rm[0][:, :]), ALU.subtract) \
                            .then_inc(sem("gate_in"), 1)
                    gate = gf({"f0": 0, "f1": 1, "m3": 3}[name])
                    dve.wait_ge(sem("gate_exp"), k + 1)
                    if KTOP[name] == 2:
                        link(v.tensor_scalar(rk[:, :], wt[1][:, :], 1.0, None, ALU.add))
                        link(v.reciprocal(rk[:, :], rk[:, :]))
                        link(v.tensor_scalar(wt[0][:, :], rk[:, :], gate, None, ALU.mult))
                        link(v.tensor_tensor(wt[1][:, :], wt[1][:, :], wt[0][:, :], ALU.mult))
                    else:
                        link(v.tensor_reduce(rk[:, :], rt[:, :, :], AX.X, ALU.add))
                        link(v.reciprocal(rk[:, :], rk[:, :]))
                        link(v.tensor_scalar(wt[0][:, :], rk[:, :], gate, None, ALU.mult))
                    dve.wait_ge(sem("count_done"), k + 1)
                    cnt = bank[:, 0, 0:P].rearrange("p (t e) -> p t e", e=NE)
                    link(v.tensor_copy(rn[:, :, :], bank[:, 1, 0:P].rearrange("p (t e) -> p e t", e=NE)))
                    link(v.tensor_tensor_scan(rscan[:, :, :].rearrange("p e t -> p (e t)"),
                                              runmask[:, :, :].rearrange("p e t -> p (e t)"),
                                              rn[:, :, :].rearrange("p e t -> p (e t)"), 0.0, ALU.mult, ALU.add))
                    link(v.tensor_tensor(rn[:, :, :], rscan[:, :, :], rn[:, :, :], ALU.subtract))
                    link(v.tensor_tensor(rt[:, :, :], cnt, rn[:, :, :].rearrange("p e t -> p t e"), ALU.add))
                    if KTOP[name] == 2:
                        link(v.tensor_scalar(blki[:, :], rscan[:, :, NT - 1], float(P - 1), None, ALU.add))
                        link(v.tensor_scalar(blki[:, :], blki[:, :], 7, None, ALU.arith_shift_right))
                        link(v.tensor_copy(blk[:, 0, :], blki[:, :]))
                        link(v.tensor_tensor_scan(blk[:, 1, :], ones[:, 0:NE], blk[:, 0, :], 0.0, ALU.mult, ALU.add))
                        link(v.tensor_tensor(blk[:, 2, :], blk[:, 1, :], blk[:, 0, :], ALU.subtract))
                        link(v.tensor_scalar(blk[:, 2, :], blk[:, 2, :], float(P), None, ALU.mult))
                        link(v.tensor_tensor(rt[:, :, :], rt[:, :, :], over_t(blk[:, 2, :]), ALU.add))
                        link(v.tensor_tensor(cmpb[:, :, :],
                                             iotab[0:1, :].unsqueeze(2).to_broadcast([1, TOP2_BLOCKS, NE]),
                                             blk[0:1, 1, :].unsqueeze(1).to_broadcast([1, TOP2_BLOCKS, NE]), ALU.is_ge))
                        link(v.tensor_reduce(blkef[:, :], cmpb[:, :, :], AX.X, ALU.add))
                        link(v.tensor_scalar(blke[:, :], blkef[:, :], float(NE - 1), None, ALU.min))
                    top = KTOP[name]
                    slots, slots_i = slotf[:, 0:top, :], slot[:, 0:top, :]
                    for j in range(top):
                        ins = v.tensor_tensor(own[:, j, :, :], rt[:, :, :], oh[j][:, :, :], ALU.mult)
                    link(ins)
                    link(v.tensor_reduce(slots, own[:, 0:top, :, :], AX.X, ALU.add))
                    if top == 1:
                        place = slotf[:, 0, :]
                        link(v.tensor_scalar(keep[:, :], place, float(CAP), None, ALU.is_lt))
                        link(v.tensor_tensor(wt[0][:, :], wt[0][:, :], keep[:, :], ALU.mult))
                        link(v.tensor_tensor(lg2[:, :, :], over_t(iota8[:, :]), oh[0][:, :, :], ALU.mult))
                        link(v.tensor_reduce(rk[:, :], lg2[:, :, :], AX.X, ALU.add))
                        link(v.scalar_tensor_tensor(place, rk[:, :], float(CAP), place, ALU.mult, ALU.add))
                        link(v.tensor_scalar(rk[:, :], tokid[:, :], float(NE * CAP), None, ALU.add))
                        link(v.tensor_tensor(place, place, rk[:, :], ALU.subtract))
                        link(v.tensor_tensor(place, place, keep[:, :], ALU.mult))
                        link(v.tensor_tensor(place, place, rk[:, :], ALU.add))
                    nb = NBLK[name]
                    link(v.tensor_copy(slots_i, slots))
                    v.tensor_scalar(slot_bi[:, 0:top, :], slots_i, 7, None, ALU.arith_shift_right)
                    link(v.tensor_scalar(slot_ri[:, 0:top, :], slots_i, P - 1, None, ALU.bitwise_and))
                    v.tensor_copy(slot_blk[:, 0:top, :], slot_bi[:, 0:top, :])
                    link(v.tensor_copy(slot_row[:, 0:top, :], slot_ri[:, 0:top, :]))
                    for j in range(top):
                        hb = hot_blk(j, nb)
                        link(v.tensor_tensor(hb[:, :, 2, :], iotab[:, 0:nb].unsqueeze(1).to_broadcast([P, NT, nb]),
                                             slot_blk[:, j, :].unsqueeze(2).to_broadcast([P, NT, nb]), ALU.is_equal))
                        v.engine_nop().then_inc(sem("hot_ready"), 1)
                        v.tensor_tensor(hb[:, :, 1, :], hb[:, :, 2, :],
                                        tileid[:, j, :].unsqueeze(2).to_broadcast([P, NT, nb]), ALU.mult)
                        link(v.tensor_tensor(hot_row[j], iotap[:, :].unsqueeze(1).to_broadcast([P, NT, P]),
                                             slot_row[:, j, :].unsqueeze(2).to_broadcast([P, NT, P]), ALU.is_equal))
                        v.engine_nop().then_inc(sem("tiles_hot"), 1)
                    dve.wait_ge(sem("table_done"), k + 1)
                    rows1, tiles_ = tab_ps[:, 0:nb], tab_ps[:, nb:2 * nb]
                    g0, g1, g2 = tab0[:, 0:nb], tab1[:, 0:nb], tab2[:, 0:nb]
                    link(v.tensor_copy(g1, rows1))
                    link(v.scalar_tensor_tensor(g0, tiles_, float(P), g1, ALU.mult, ALU.add))
                    link(v.tensor_scalar(g1, g1, 1.0, None, ALU.min))
                    link(v.tensor_scalar(g0, g0, 1.0, 0.0, ALU.subtract, ALU.max))
                    link(v.tensor_scalar(g2, g0, float(TOK), -float(TOK), ALU.is_ge, ALU.mult))
                    link(v.tensor_tensor(slot_src[:, 0:nb], g0, g2, ALU.add))
                    link(v.tensor_tensor(g0, g0, spare[:, 0:nb], ALU.subtract))
                    link(v.tensor_tensor(g0, g0, g1, ALU.mult))
                    link(v.tensor_tensor(slot_dst[:, 0:nb], g0, spare[:, 0:nb], ALU.add))
                    v.engine_nop().then_inc(sem("slots_ready"), 1)
                    base, nb = BB[name], NBLK[name]

                    def product3(b, u):
                        dve.wait_ge(sem("g_act"), base + b + 1)
                        after(dve, sem("gtr_done"), base + b - 1)
                        v.tensor_tensor(G3[u][:, :], G[u][:, 0:HID3], bank[:, u, HID3:HID], ALU.mult) \
                            .then_inc(sem("g3_prod"), 1)

                    def evac_GT(b, u):
                        dve.wait_ge(sem("gtr_done"), base + b + 1)
                        after(dve, sem("yps_done"), base + b - 1)
                        w = HID if k < 2 else HID3
                        v.tensor_copy(GT[u][:, 0:w], bank[:, 2 + u, 0:w]).then_inc(sem("GT_ready"), 1)

                    late = blocks_lag(name)
                    Ring(nb, late).run(dve, [(evac_GT, late - 1)] + [(product3, 1)] * (name == "m3"))
                    if name == "m3":
                        dve.wait_ge(sem("t1_done"), TB[name] + NT)
                        link(v.scalar_tensor_tensor(x[:, :, :], y3[:, :, :], gate, x[:, :, :], ALU.mult, ALU.add))
                    if name == "f0":
                        mask_rows()
                        split_rows()
                    second = second_rows(name)
                    tiles = 4
                    for q in range(NT // tiles):
                        dve.wait_ge(sem(f"gathered{q}"), 16 * (SC[name] + KTOP[name]))
                        ts = slice(q * tiles, (q + 1) * tiles)
                        for j in range(KTOP[name]):
                            for t in range(q * tiles, (q + 1) * tiles):
                                ins = v.scalar_tensor_tensor(tile(x, t), tile(hn if j == 0 else second, t), at(wt[j], t),
                                                             tile(x, t), ALU.mult, ALU.add)
                            link(ins)
                        if name == phases()[-1]:
                            v.engine_nop().then_inc(sem("x_final"), 1)
                        if name != "m3":
                            for t in range(q * tiles, (q + 1) * tiles):
                                tile_stats(x, t)
                            if (q + 1) * tiles == EARLY and name != phases()[-1]:
                                row_scales(PH[PHI[name] + 1], "early")
                    v.engine_nop().then_inc(sem("phase_done"), 1)


def kernel(**inputs):
    import concourse.bacc as bacc
    from concourse.bass_utils import run_bass_kernel_spmd

    a = {k: np.asarray(v) for k, v in inputs.items()}
    xi, ci = a["x"].reshape(TOK, C), a["ctx_1024"].reshape(TOK, C)
    vec = {"bq0": "L0_xattn_Wk_b", "bk0": "L0_xattn_Wv_b", "qn_w1": "L1_xattn_qn_w", "qn_b1": "L1_xattn_qn_b",
           "cn_w1": "L1_xattn_cn_w", "cn_b1": "L1_xattn_cn_b", "bq1": "L1_xattn_bq", "bk1": "L1_xattn_bk",
           "tab_g": "L2_xattn_tab_g", "tab_b": "L2_xattn_tab_b", "vid_g": "L2_xattn_vid_g", "vid_b": "L2_xattn_vid_b",
           "ln1_w": "L3_ffn_ln1_scale", "ln1_b": "L3_ffn_ln1_shift", "ln2_w": "L3_ffn_ln2_scale",
           "ln2_b": "L3_ffn_ln2_shift"}
    columns = [a[vec[n]] for n in COLS[:16]]
    for name in ("q_g", "q_b", "k_g", "k_b"):
        columns += list(a[f"L2_xattn_{name}"].reshape(CH2, P))
    rowv = [a[n] for n in ("L0_xattn_Wv_b", "L1_xattn_bv", "L1_xattn_bo", "L2_xattn_bo", "L3_xattn_b_gate",
                           "L3_xattn_b_lin", "L3_ffn_bo")]
    square = [a["L0_xattn_Wk_w"].T, a["L0_xattn_Wv_w"].T] + [a[f"L1_xattn_{n}"].T for n in ("Wq", "Wk", "Wv", "Wo")] + [
        a["L3_xattn_W_gate"], a["L3_xattn_W_lin"][:C], a["L3_xattn_W_lin"][C:]] + [
            a[f"L3_ffn_{n}"] for n in ("wq", "wk", "wv", "wo")] + [a["L2_ffn_weight"].T]
    arrays = {
        "x": xi, "ctx": ci, "ctxT": ci.T, "cols": np.stack(columns, 1), "rows": np.stack(rowv), "wsq": np.stack(square),
        "g": np.concatenate([a["g_xattn"], a["g_ffn"]]).reshape(1, 8), "pw": a["fside_BxS_0"].reshape(NT, P).T,
        "mask": a["mask_BxS2_bk0"].view(np.int32),
        "rw": np.stack([a["L0_ffn_router_w"].T, a["L1_ffn_wg"], a["L3_ffn_gate_w"]]),
        "wq2": a["L2_xattn_Wq"], "wk2": a["L2_xattn_Wk"], "wv2": a["L2_xattn_Wv"], "wo2": a["L2_xattn_Wo"],
        "w1_0": a["L0_ffn_w1"], "w1_1": a["L1_ffn_w1"], "w1_2": a["L3_ffn_w1"], "w1_3": a["L3_ffn_w2"],
        "w2_0": a["L0_ffn_w2"], "w2_1": a["L1_ffn_w2"], "w2_2": a["L3_ffn_w3"],
    }
    nc = bacc.Bacc("TRN2", target_bir_lowering=False, num_devices=1)
    feed, io = {}, {}
    for name, arr in arrays.items():
        arr = np.ascontiguousarray(arr)
        feed[f"in_{name}"] = arr
        io[name] = nc.dram_tensor(f"in_{name}", arr.shape, mybir.dt.from_np(arr.dtype), kind="ExternalInput").ap()
    io["out"] = nc.dram_tensor("out_dram", (TOK, C), F32, kind="ExternalOutput").ap()
    build(nc, io)
    r = run_bass_kernel_spmd(nc, [feed], core_ids=[0])
    return r.results[0]["out_dram"].reshape(B, SEQ, C)
```
